# Optimizing a Trainium2 kernel written in Bass

```python
import numpy as np
import jax
import jax.numpy as jnp

def _softmax(x, axis=-1):
    return jax.nn.softmax(x, axis=axis)

def _gelu(x):
    return jax.nn.gelu(x, approximate=True)

def _silu(x):
    return jax.nn.silu(x)

def _sigmoid(x):
    return jax.nn.sigmoid(x)

def _layernorm(x, axis=-1, eps=1e-05):
    m = jnp.mean(x, axis=axis, keepdims=True)
    v = jnp.var(x, axis=axis, keepdims=True)
    return (x - m) / jnp.sqrt(v + eps)

def _scatter_add(tgt, idx, src, axis=0):
    return tgt.at[idx].add(src)

def _segment_sum(src, seg, n):
    return jax.ops.segment_sum(src, seg, n)
kernel_name = 'mk_cond_seq_d4_seqx_r4_0eaaec'

def setup_inputs(seed: int=0):
    np.random.seed(seed)
    _w = jnp.asarray

    def _rec_inputs():
        import jax
        import jax.numpy as jnp
        _rk = jax.random.key(seed)
        x = -0.0003929 + 0.9999 * jax.random.normal(jax.random.fold_in(_rk, 1), (2, 1024, 256), jnp.float32)
        _lenS = 1024 - jax.random.randint(jax.random.fold_in(_rk, 7), (2,), 0, max(1, 1024 // 4) + 1, jnp.int32)
        _lenS2 = 1024 - jax.random.randint(jax.random.fold_in(_rk, 8), (2,), 0, max(1, 1024 // 4) + 1, jnp.int32)
        cond_1024 = 0.0061147 + 1.02565 * jax.random.normal(jax.random.fold_in(_rk, 11), (2, 256), jnp.float32)
        _validS = jnp.arange(1024)[None, :] < _lenS[:, None]
        _validS2 = jnp.arange(1024)[None, :] < _lenS2[:, None]
        _causal = jnp.tril(jnp.ones((1024, 1024), dtype=bool))
        mask_BxS_bf1 = jnp.ones((2, 1024), dtype=bool)
        return (x, cond_1024, mask_BxS_bf1)
    x, cond_1024, mask_BxS_bf1 = _rec_inputs()

    def _L0_cond_setup():
        import jax, jax.numpy as jnp
        import numpy as np
        H = 16
        EPS = 1e-05

        def layer_norm(x, g, b):
            mu = jnp.mean(x, axis=-1, keepdims=True)
            var = jnp.var(x, axis=-1, keepdims=True)
            return (x - mu) * jax.lax.rsqrt(var + EPS) * g + b
        key = jax.random.key(seed)
        ks = jax.random.split(key, 8)
        B, T, D, TE = (4, 1024, 256, 256)
        s = 0.02
        return {'x': jax.random.normal(ks[0], (B, T, D), jnp.float32), 'emb': jax.random.normal(ks[1], (B, 1, TE), jnp.float32), 'gate_msa': jax.random.normal(ks[2], (B, 1, D), jnp.float32), 'norm_g': jnp.ones((D,), jnp.float32), 'norm_b': jnp.zeros((D,), jnp.float32), 'Wq': jax.random.normal(ks[3], (D, D), jnp.float32) * s, 'bq': jnp.zeros((D,), jnp.float32), 'Wk': jax.random.normal(ks[4], (D, D), jnp.float32) * s, 'bk': jnp.zeros((D,), jnp.float32), 'Wv': jax.random.normal(ks[5], (D, D), jnp.float32) * s, 'bv': jnp.zeros((D,), jnp.float32), 'emb_W': jax.random.normal(ks[6], (TE, 2 * D), jnp.float32) * s, 'emb_b': jnp.zeros((2 * D,), jnp.float32), 'sn_g': jnp.ones((D,), jnp.float32), 'sn_b': jnp.zeros((D,), jnp.float32), 'out_W': jax.random.normal(ks[7], (D, D), jnp.float32) * s, 'out_b': jnp.zeros((D,), jnp.float32)}
    _L0_cond_all = _L0_cond_setup()
    _L0_cond_in = {k: v for k, v in _L0_cond_all.items() if k in ('norm_g', 'norm_b', 'Wq', 'bq', 'Wk', 'bk', 'Wv', 'bv', 'emb_W', 'emb_b', 'sn_g', 'sn_b', 'out_W', 'out_b')}
    del _L0_cond_all

    def _L1_cond_setup():
        import jax, jax.numpy as jnp
        import numpy as np
        EPS = 1e-05

        def _sln(h, w, ln_g, ln_b, Wg, bg, Wb, bb):
            mu = jnp.mean(h, axis=-1, keepdims=True)
            var = jnp.mean((h - mu) ** 2, axis=-1, keepdims=True)
            ln = (h - mu) / jnp.sqrt(var + EPS) * ln_g + ln_b
            gamma = (w @ Wg.T + bg)[:, None, :]
            beta = (w @ Wb.T + bb)[:, None, :]
            return gamma * ln + beta
        key = jax.random.key(seed)
        ks = jax.random.split(key, 20)
        B, N, D = (4, 256, 256)
        F = 4 * D
        s = lambda fan: 1.0 / np.sqrt(fan)
        inp = {'hidden': jax.random.normal(ks[0], (B, N, D), jnp.float32), 'w': jax.random.normal(ks[1], (B, D), jnp.float32), 'ln_g': jnp.ones((D,), jnp.float32), 'ln_b': jnp.zeros((D,), jnp.float32), 'Wg': jax.random.normal(ks[2], (D, D), jnp.float32) * s(D), 'bg': jnp.zeros((D,), jnp.float32), 'Wb': jax.random.normal(ks[3], (D, D), jnp.float32) * s(D), 'bb': jnp.zeros((D,), jnp.float32), 'Wqkv': jax.random.normal(ks[4], (3 * D, D), jnp.float32) * s(D), 'bqkv': jnp.zeros((3 * D,), jnp.float32), 'Wp': jax.random.normal(ks[5], (D, D), jnp.float32) * s(D), 'bp': jnp.zeros((D,), jnp.float32), 'W1': jax.random.normal(ks[6], (F, D), jnp.float32) * s(D), 'b1': jnp.zeros((F,), jnp.float32), 'W2': jax.random.normal(ks[7], (D, F), jnp.float32) * s(F), 'b2': jnp.zeros((D,), jnp.float32), 'num_heads': 16}
        return inp
    _L1_cond_all = _L1_cond_setup()
    _L1_cond_in = {k: v for k, v in _L1_cond_all.items() if k in ('ln_g', 'ln_b', 'Wg', 'bg', 'Wb', 'bb', 'Wqkv', 'bqkv', 'Wp', 'bp', 'W1', 'b1', 'W2', 'b2')}
    del _L1_cond_all

    def _L2_cond_setup():
        import jax, jax.numpy as jnp
        import numpy as np
        DIM = 256
        MLP_RATIO = 4
        EPS = 1e-06

        def rmsnorm(x, w):
            return x * jax.lax.rsqrt(jnp.mean(x * x, axis=-1, keepdims=True) + EPS) * w

        def film(x, cond, w, b):
            ss = cond @ w + b
            scale, shift = jnp.split(ss, 2, axis=-1)
            return x * (1.0 + scale[:, None, :]) + shift[:, None, :]
        key = jax.random.key(seed)
        ks = jax.random.split(key, 16)
        B, N, D = (4, 512, DIM)
        H = D * MLP_RATIO
        s = lambda fan_in: 1.0 / np.sqrt(fan_in)
        return {'x': jax.random.normal(ks[0], (B, N, D), jnp.float32), 'cond': jax.random.normal(ks[1], (B, D), jnp.float32), 'norm1_w': jnp.ones((D,), jnp.float32), 'film1_w': jax.random.normal(ks[2], (D, 2 * D), jnp.float32) * s(D), 'film1_b': jnp.zeros((2 * D,), jnp.float32), 'q_w': jax.random.normal(ks[3], (D, D), jnp.float32) * s(D), 'q_b': jnp.zeros((D,), jnp.float32), 'k_w': jax.random.normal(ks[4], (D, D), jnp.float32) * s(D), 'k_b': jnp.zeros((D,), jnp.float32), 'v_w': jax.random.normal(ks[5], (D, D), jnp.float32) * s(D), 'v_b': jnp.zeros((D,), jnp.float32), 'proj_w': jax.random.normal(ks[6], (D, D), jnp.float32) * s(D), 'proj_b': jnp.zeros((D,), jnp.float32), 'norm2_w': jnp.ones((D,), jnp.float32), 'film2_w': jax.random.normal(ks[7], (D, 2 * D), jnp.float32) * s(D), 'film2_b': jnp.zeros((2 * D,), jnp.float32), 'mlp_w1': jax.random.normal(ks[8], (D, H), jnp.float32) * s(D), 'mlp_b1': jnp.zeros((H,), jnp.float32), 'mlp_w2': jax.random.normal(ks[9], (H, D), jnp.float32) * s(H), 'mlp_b2': jnp.zeros((D,), jnp.float32)}
    _L2_cond_all = _L2_cond_setup()
    _L2_cond_in = {k: v for k, v in _L2_cond_all.items() if k in ('norm1_w', 'film1_w', 'film1_b', 'q_w', 'q_b', 'k_w', 'k_b', 'v_w', 'v_b', 'proj_w', 'proj_b', 'norm2_w', 'film2_w', 'film2_b', 'mlp_w1', 'mlp_b1', 'mlp_w2', 'mlp_b2')}
    del _L2_cond_all

    def _L3_cond_setup():
        import jax, jax.numpy as jnp
        import numpy as np
        B, S, H, NH = (2, 512, 256, 16)
        HD = H // NH
        ROT = HD // 2
        COND, FF = (256, 4 * H)
        BASE = 10000.0
        EPS = 1e-05

        def _layer_norm(x, g, b):
            mu = jnp.mean(x, axis=-1, keepdims=True)
            var = jnp.mean(jnp.square(x - mu), axis=-1, keepdims=True)
            return (x - mu) * jax.lax.rsqrt(var + EPS) * g + b

        def _ada_norm(x, cond, g, b, w, bw):
            shift, scale = jnp.split(cond @ w + bw, 2, axis=-1)
            return _layer_norm(x, g, b) * (1.0 + scale[:, None, :]) + shift[:, None, :]

        def _rotary_sin_cos(seq_len):
            inv_freq = 1.0 / BASE ** (jnp.arange(ROT, dtype=jnp.float32) / ROT)
            freqs = jnp.arange(seq_len, dtype=jnp.float32)[:, None] * inv_freq[None, :]
            return (jnp.sin(freqs), jnp.cos(freqs))

        def _apply_rotary(x, sin, cos):
            xe, xo = (x[..., ::2], x[..., 1::2])
            re = xe * cos - xo * sin
            ro = xo * cos + xe * sin
            return jnp.stack((re, ro), axis=-1).reshape(x.shape)

        def _split_heads(x):
            b, s, _ = x.shape
            return x.reshape(b, s, NH, HD).transpose(0, 2, 1, 3)
        key = jax.random.key(seed)
        ks = jax.random.split(key, 16)
        w = lambda k, shape: jax.random.normal(k, shape, dtype=jnp.float32) * 0.02
        z = lambda shape: jnp.zeros(shape, dtype=jnp.float32)
        o = lambda shape: jnp.ones(shape, dtype=jnp.float32)
        return {'x': jax.random.normal(ks[0], (B, S, H), dtype=jnp.float32), 'cond': jax.random.normal(ks[1], (B, COND), dtype=jnp.float32), 'attn_mask': jnp.ones((B, S), dtype=bool), 'wq': w(ks[2], (H, H)), 'bq': z((H,)), 'wk': w(ks[3], (H, H)), 'bk': z((H,)), 'wv': w(ks[4], (H, H)), 'bv': z((H,)), 'wo': w(ks[5], (H, H)), 'bo': z((H,)), 'ln1_g': o((H,)), 'ln1_b': z((H,)), 'ada1_w': w(ks[6], (COND, 2 * H)), 'ada1_b': z((2 * H,)), 'ln2_g': o((H,)), 'ln2_b': z((H,)), 'ada2_w': w(ks[7], (COND, 2 * H)), 'ada2_b': z((2 * H,)), 'ff_w1': w(ks[8], (H, FF)), 'ff_b1': z((FF,)), 'ff_w2': w(ks[9], (FF, H)), 'ff_b2': z((H,))}
    _L3_cond_all = _L3_cond_setup()
    _L3_cond_in = {k: v for k, v in _L3_cond_all.items() if k in ('wq', 'bq', 'wk', 'bk', 'wv', 'bv', 'wo', 'bo', 'ln1_g', 'ln1_b', 'ada1_w', 'ada1_b', 'ln2_g', 'ln2_b', 'ada2_w', 'ada2_b', 'ff_w1', 'ff_b1', 'ff_w2', 'ff_b2')}
    del _L3_cond_all
    return {'x': x, 'cond_1024': cond_1024, 'mask_BxS_bf1': mask_BxS_bf1, 'L0_cond_norm_g': _L0_cond_in['norm_g'], 'L0_cond_norm_b': _L0_cond_in['norm_b'], 'L0_cond_Wq': _L0_cond_in['Wq'], 'L0_cond_bq': _L0_cond_in['bq'], 'L0_cond_Wk': _L0_cond_in['Wk'], 'L0_cond_bk': _L0_cond_in['bk'], 'L0_cond_Wv': _L0_cond_in['Wv'], 'L0_cond_bv': _L0_cond_in['bv'], 'L0_cond_emb_W': _L0_cond_in['emb_W'], 'L0_cond_emb_b': _L0_cond_in['emb_b'], 'L0_cond_sn_g': _L0_cond_in['sn_g'], 'L0_cond_sn_b': _L0_cond_in['sn_b'], 'L0_cond_out_W': _L0_cond_in['out_W'], 'L0_cond_out_b': _L0_cond_in['out_b'], 'L1_cond_ln_g': _L1_cond_in['ln_g'], 'L1_cond_ln_b': _L1_cond_in['ln_b'], 'L1_cond_Wg': _L1_cond_in['Wg'], 'L1_cond_bg': _L1_cond_in['bg'], 'L1_cond_Wb': _L1_cond_in['Wb'], 'L1_cond_bb': _L1_cond_in['bb'], 'L1_cond_Wqkv': _L1_cond_in['Wqkv'], 'L1_cond_bqkv': _L1_cond_in['bqkv'], 'L1_cond_Wp': _L1_cond_in['Wp'], 'L1_cond_bp': _L1_cond_in['bp'], 'L1_cond_W1': _L1_cond_in['W1'], 'L1_cond_b1': _L1_cond_in['b1'], 'L1_cond_W2': _L1_cond_in['W2'], 'L1_cond_b2': _L1_cond_in['b2'], 'L2_cond_norm1_w': _L2_cond_in['norm1_w'], 'L2_cond_film1_w': _L2_cond_in['film1_w'], 'L2_cond_film1_b': _L2_cond_in['film1_b'], 'L2_cond_q_w': _L2_cond_in['q_w'], 'L2_cond_q_b': _L2_cond_in['q_b'], 'L2_cond_k_w': _L2_cond_in['k_w'], 'L2_cond_k_b': _L2_cond_in['k_b'], 'L2_cond_v_w': _L2_cond_in['v_w'], 'L2_cond_v_b': _L2_cond_in['v_b'], 'L2_cond_proj_w': _L2_cond_in['proj_w'], 'L2_cond_proj_b': _L2_cond_in['proj_b'], 'L2_cond_norm2_w': _L2_cond_in['norm2_w'], 'L2_cond_film2_w': _L2_cond_in['film2_w'], 'L2_cond_film2_b': _L2_cond_in['film2_b'], 'L2_cond_mlp_w1': _L2_cond_in['mlp_w1'], 'L2_cond_mlp_b1': _L2_cond_in['mlp_b1'], 'L2_cond_mlp_w2': _L2_cond_in['mlp_w2'], 'L2_cond_mlp_b2': _L2_cond_in['mlp_b2'], 'L3_cond_wq': _L3_cond_in['wq'], 'L3_cond_bq': _L3_cond_in['bq'], 'L3_cond_wk': _L3_cond_in['wk'], 'L3_cond_bk': _L3_cond_in['bk'], 'L3_cond_wv': _L3_cond_in['wv'], 'L3_cond_bv': _L3_cond_in['bv'], 'L3_cond_wo': _L3_cond_in['wo'], 'L3_cond_bo': _L3_cond_in['bo'], 'L3_cond_ln1_g': _L3_cond_in['ln1_g'], 'L3_cond_ln1_b': _L3_cond_in['ln1_b'], 'L3_cond_ada1_w': _L3_cond_in['ada1_w'], 'L3_cond_ada1_b': _L3_cond_in['ada1_b'], 'L3_cond_ln2_g': _L3_cond_in['ln2_g'], 'L3_cond_ln2_b': _L3_cond_in['ln2_b'], 'L3_cond_ada2_w': _L3_cond_in['ada2_w'], 'L3_cond_ada2_b': _L3_cond_in['ada2_b'], 'L3_cond_ff_w1': _L3_cond_in['ff_w1'], 'L3_cond_ff_b1': _L3_cond_in['ff_b1'], 'L3_cond_ff_w2': _L3_cond_in['ff_w2'], 'L3_cond_ff_b2': _L3_cond_in['ff_b2']}

def reference(x, cond_1024, mask_BxS_bf1, L0_cond_norm_g, L0_cond_norm_b, L0_cond_Wq, L0_cond_bq, L0_cond_Wk, L0_cond_bk, L0_cond_Wv, L0_cond_bv, L0_cond_emb_W, L0_cond_emb_b, L0_cond_sn_g, L0_cond_sn_b, L0_cond_out_W, L0_cond_out_b, L1_cond_ln_g, L1_cond_ln_b, L1_cond_Wg, L1_cond_bg, L1_cond_Wb, L1_cond_bb, L1_cond_Wqkv, L1_cond_bqkv, L1_cond_Wp, L1_cond_bp, L1_cond_W1, L1_cond_b1, L1_cond_W2, L1_cond_b2, L2_cond_norm1_w, L2_cond_film1_w, L2_cond_film1_b, L2_cond_q_w, L2_cond_q_b, L2_cond_k_w, L2_cond_k_b, L2_cond_v_w, L2_cond_v_b, L2_cond_proj_w, L2_cond_proj_b, L2_cond_norm2_w, L2_cond_film2_w, L2_cond_film2_b, L2_cond_mlp_w1, L2_cond_mlp_b1, L2_cond_mlp_w2, L2_cond_mlp_b2, L3_cond_wq, L3_cond_bq, L3_cond_wk, L3_cond_bk, L3_cond_wv, L3_cond_bv, L3_cond_wo, L3_cond_bo, L3_cond_ln1_g, L3_cond_ln1_b, L3_cond_ada1_w, L3_cond_ada1_b, L3_cond_ln2_g, L3_cond_ln2_b, L3_cond_ada2_w, L3_cond_ada2_b, L3_cond_ff_w1, L3_cond_ff_b1, L3_cond_ff_w2, L3_cond_ff_b2):
    import jax
    import jax.numpy as jnp

    def _L0_cond_ref(x, emb, gate_msa, norm_g, norm_b, Wq, bq, Wk, bk, Wv, bv, emb_W, emb_b, sn_g, sn_b, out_W, out_b):
        import jax, jax.numpy as jnp
        import numpy as np
        H = 16
        EPS = 1e-05

        def layer_norm(x, g, b):
            mu = jnp.mean(x, axis=-1, keepdims=True)
            var = jnp.var(x, axis=-1, keepdims=True)
            return (x - mu) * jax.lax.rsqrt(var + EPS) * g + b
        B, T, D = x.shape
        dh = D // H
        xn = layer_norm(x, norm_g, norm_b)
        q = (xn @ Wq + bq).reshape(B, T, H, dh)
        k = (xn @ Wk + bk).reshape(B, T, H, dh)
        v = (xn @ Wv + bv).reshape(B, T, H, dh)
        q = jax.nn.softmax(q, axis=-1)
        k = jax.nn.softmax(k, axis=1)
        ctx = jnp.einsum('bnhd,bnhl->bhdl', k, v)
        y = jnp.einsum('bnhd,bhdl->bnhl', q, ctx).reshape(B, T, D)
        emb_out = jax.nn.silu(emb) @ emb_W + emb_b
        scale, shift = jnp.split(emb_out, 2, axis=-1)
        h = layer_norm(y, sn_g, sn_b) * (1.0 + scale) + shift
        h = jax.nn.silu(h) @ out_W + out_b
        return x + gate_msa * h

    def _L1_cond_ref(hidden, w, ln_g, ln_b, Wg, bg, Wb, bb, Wqkv, bqkv, Wp, bp, W1, b1, W2, b2, num_heads):
        import jax, jax.numpy as jnp
        import numpy as np
        EPS = 1e-05

        def _sln(h, w, ln_g, ln_b, Wg, bg, Wb, bb):
            mu = jnp.mean(h, axis=-1, keepdims=True)
            var = jnp.mean((h - mu) ** 2, axis=-1, keepdims=True)
            ln = (h - mu) / jnp.sqrt(var + EPS) * ln_g + ln_b
            gamma = (w @ Wg.T + bg)[:, None, :]
            beta = (w @ Wb.T + bb)[:, None, :]
            return gamma * ln + beta
        B, N, D = hidden.shape
        hd = D // num_heads
        h = _sln(hidden, w, ln_g, ln_b, Wg, bg, Wb, bb)
        qkv = (h @ Wqkv.T + bqkv).reshape(B, N, num_heads, hd, 3)
        q = jnp.moveaxis(qkv[..., 0], 2, 1)
        k = jnp.moveaxis(qkv[..., 1], 2, 1)
        v = jnp.moveaxis(qkv[..., 2], 2, 1)
        energy = jnp.einsum('bhqd,bhkd->bhqk', q, k)
        att = jax.nn.softmax(energy, axis=-1) / D ** 0.5
        out = jnp.einsum('bhqk,bhkd->bhqd', att, v)
        out = jnp.moveaxis(out, 1, 2).reshape(B, N, D)
        out = out @ Wp.T + bp
        h1 = out + hidden
        h2 = _sln(h1, w, ln_g, ln_b, Wg, bg, Wb, bb)
        return h2 + h1

    def _L2_cond_ref(x, cond, norm1_w, film1_w, film1_b, q_w, q_b, k_w, k_b, v_w, v_b, proj_w, proj_b, norm2_w, film2_w, film2_b, mlp_w1, mlp_b1, mlp_w2, mlp_b2):
        import jax, jax.numpy as jnp
        import numpy as np
        DIM = 256
        MLP_RATIO = 4
        EPS = 1e-06

        def rmsnorm(x, w):
            return x * jax.lax.rsqrt(jnp.mean(x * x, axis=-1, keepdims=True) + EPS) * w

        def film(x, cond, w, b):
            ss = cond @ w + b
            scale, shift = jnp.split(ss, 2, axis=-1)
            return x * (1.0 + scale[:, None, :]) + shift[:, None, :]
        B, N, D = x.shape
        x_in = x
        h = film(rmsnorm(x, norm1_w), cond, film1_w, film1_b)
        Q = h @ q_w + q_b
        K = h @ k_w + k_b
        V = h @ v_w + v_b
        scores = jnp.einsum('bnd,bmd->bnm', Q, K) * D ** (-0.5)
        attn = jax.nn.softmax(scores, axis=-1)
        out = jnp.einsum('bnm,bmd->bnd', attn, V)
        x = x_in + (out @ proj_w + proj_b)
        x_in = x
        h = film(rmsnorm(x, norm2_w), cond, film2_w, film2_b)
        h = jax.nn.gelu(h @ mlp_w1 + mlp_b1, approximate=False) @ mlp_w2 + mlp_b2
        return x_in + h

    def _L3_cond_ref(x, cond, attn_mask, wq, bq, wk, bk, wv, bv, wo, bo, ln1_g, ln1_b, ada1_w, ada1_b, ln2_g, ln2_b, ada2_w, ada2_b, ff_w1, ff_b1, ff_w2, ff_b2):
        import jax, jax.numpy as jnp
        import numpy as np
        B, S, H, NH = (2, 512, 256, 16)
        HD = H // NH
        ROT = HD // 2
        COND, FF = (256, 4 * H)
        BASE = 10000.0
        EPS = 1e-05

        def _layer_norm(x, g, b):
            mu = jnp.mean(x, axis=-1, keepdims=True)
            var = jnp.mean(jnp.square(x - mu), axis=-1, keepdims=True)
            return (x - mu) * jax.lax.rsqrt(var + EPS) * g + b

        def _ada_norm(x, cond, g, b, w, bw):
            shift, scale = jnp.split(cond @ w + bw, 2, axis=-1)
            return _layer_norm(x, g, b) * (1.0 + scale[:, None, :]) + shift[:, None, :]

        def _rotary_sin_cos(seq_len):
            inv_freq = 1.0 / BASE ** (jnp.arange(ROT, dtype=jnp.float32) / ROT)
            freqs = jnp.arange(seq_len, dtype=jnp.float32)[:, None] * inv_freq[None, :]
            return (jnp.sin(freqs), jnp.cos(freqs))

        def _apply_rotary(x, sin, cos):
            xe, xo = (x[..., ::2], x[..., 1::2])
            re = xe * cos - xo * sin
            ro = xo * cos + xe * sin
            return jnp.stack((re, ro), axis=-1).reshape(x.shape)

        def _split_heads(x):
            b, s, _ = x.shape
            return x.reshape(b, s, NH, HD).transpose(0, 2, 1, 3)
        residual = x
        h = _ada_norm(x, cond, ln1_g, ln1_b, ada1_w, ada1_b)
        q = _split_heads(h @ wq + bq)
        k = _split_heads(h @ wk + bk)
        v = _split_heads(h @ wv + bv)
        sin, cos = _rotary_sin_cos(x.shape[1])
        q = _apply_rotary(q, sin, cos)
        k = _apply_rotary(k, sin, cos)
        scores = jnp.einsum('bhqd,bhkd->bhqk', q, k) / np.sqrt(HD).astype(np.float32)
        scores = jnp.where(attn_mask[:, None, None, :], scores, -jnp.inf)
        attn = jax.nn.softmax(scores, axis=-1)
        out = jnp.einsum('bhqk,bhkd->bhqd', attn, v)
        out = out.transpose(0, 2, 1, 3).reshape(x.shape[0], x.shape[1], H)
        x = residual + out @ wo + bo
        residual = x
        h = _ada_norm(x, cond, ln2_g, ln2_b, ada2_w, ada2_b)
        ff = jax.nn.gelu(h @ ff_w1 + ff_b1, approximate=False) @ ff_w2 + ff_b2
        return residual + ff
    x = _L0_cond_ref(x, cond_1024[:, None, :], cond_1024[:, None, :], L0_cond_norm_g, L0_cond_norm_b, L0_cond_Wq, L0_cond_bq, L0_cond_Wk, L0_cond_bk, L0_cond_Wv, L0_cond_bv, L0_cond_emb_W, L0_cond_emb_b, L0_cond_sn_g, L0_cond_sn_b, L0_cond_out_W, L0_cond_out_b)
    x = _L1_cond_ref(x, cond_1024, L1_cond_ln_g, L1_cond_ln_b, L1_cond_Wg, L1_cond_bg, L1_cond_Wb, L1_cond_bb, L1_cond_Wqkv, L1_cond_bqkv, L1_cond_Wp, L1_cond_bp, L1_cond_W1, L1_cond_b1, L1_cond_W2, L1_cond_b2, 16)
    x = _L2_cond_ref(x, cond_1024, L2_cond_norm1_w, L2_cond_film1_w, L2_cond_film1_b, L2_cond_q_w, L2_cond_q_b, L2_cond_k_w, L2_cond_k_b, L2_cond_v_w, L2_cond_v_b, L2_cond_proj_w, L2_cond_proj_b, L2_cond_norm2_w, L2_cond_film2_w, L2_cond_film2_b, L2_cond_mlp_w1, L2_cond_mlp_b1, L2_cond_mlp_w2, L2_cond_mlp_b2)
    x = _L3_cond_ref(x, cond_1024, mask_BxS_bf1, L3_cond_wq, L3_cond_bq, L3_cond_wk, L3_cond_bk, L3_cond_wv, L3_cond_bv, L3_cond_wo, L3_cond_bo, L3_cond_ln1_g, L3_cond_ln1_b, L3_cond_ada1_w, L3_cond_ada1_b, L3_cond_ln2_g, L3_cond_ln2_b, L3_cond_ada2_w, L3_cond_ada2_b, L3_cond_ff_w1, L3_cond_ff_b1, L3_cond_ff_w2, L3_cond_ff_b2)
    return x

_drawn_inputs = setup_inputs


def setup_inputs(seed=0):
    import zlib

    import numpy as np

    out = dict(_drawn_inputs(seed))
    spreads = {'L0_cond_norm_g': (1.0, 0.6),
     'L0_cond_norm_b': (0.0, 0.379),
     'L0_cond_bq': (0.0, 0.8),
     'L0_cond_bk': (0.0, 2.0),
     'L0_cond_bv': (0.0, 0.1),
     'L0_cond_emb_b': (0.0, 0.299),
     'L0_cond_sn_g': (1.0, 0.2),
     'L0_cond_sn_b': (0.0, 0.487),
     'L0_cond_out_b': (0.0, 0.1),
     'L1_cond_ln_g': (1.0, 0.2),
     'L1_cond_ln_b': (0.0, 0.1),
     'L1_cond_bg': (0.0, 0.1),
     'L1_cond_bb': (0.0, 0.1),
     'L1_cond_bqkv': (0.0, 0.8),
     'L1_cond_bp': (0.0, 0.1),
     'L1_cond_b1': (0.0, 0.1),
     'L1_cond_b2': (0.0, 0.1),
     'L2_cond_norm1_w': (1.0, 0.2),
     'L2_cond_film1_b': (0.0, 0.1),
     'L2_cond_q_b': (0.0, 0.543),
     'L2_cond_k_b': (0.0, 2.0),
     'L2_cond_v_b': (0.0, 0.1),
     'L2_cond_proj_b': (0.0, 0.1),
     'L2_cond_norm2_w': (1.0, 0.2),
     'L2_cond_film2_b': (0.0, 0.1),
     'L2_cond_mlp_b1': (0.0, 0.305),
     'L2_cond_mlp_b2': (0.0, 0.1),
     'L3_cond_bq': (0.0, 2.0),
     'L3_cond_bk': (0.0, 2.0),
     'L3_cond_bv': (0.0, 0.657),
     'L3_cond_bo': (0.0, 0.1),
     'L3_cond_ln1_g': (1.0, 0.6),
     'L3_cond_ln1_b': (0.0, 0.8),
     'L3_cond_ada1_b': (0.0, 0.8),
     'L3_cond_ln2_g': (1.0, 0.6),
     'L3_cond_ln2_b': (0.0, 0.8),
     'L3_cond_ada2_b': (0.0, 0.8),
     'L3_cond_ff_b1': (0.0, 0.564),
     'L3_cond_ff_b2': (0.0, 0.1)}
    factors = {'L0_cond_Wq': 8.0,
     'L0_cond_Wk': 8.0,
     'L3_cond_wq': 8.0,
     'L3_cond_wk': 8.0,
     'L3_cond_ada1_w': 3.668,
     'L3_cond_ada2_w': 2.824}
    for name, (base, spread) in spreads.items():
        noise = np.random.default_rng([zlib.crc32(name.encode()), seed]).standard_normal(out[name].shape)
        drawn = base * np.exp(spread * noise) if base else spread * noise
        out[name] = jnp.asarray(drawn.astype(out[name].dtype))
    for name, factor in factors.items():
        out[name] = (out[name] * factor).astype(out[name].dtype)
    return out
```

```python
from contextlib import ExitStack

import numpy as np

import concourse.bass as bass
from concourse import mybir

F32 = mybir.dt.float32
BF16 = mybir.dt.bfloat16
U8 = mybir.dt.uint8
ACT = mybir.ActivationFunctionType
ALU = mybir.AluOpType
AX = mybir.AxisListType

P = 128
B = 2
T = 1024
D = 256
H = 16
HD = D // H
NH = B * H
CC = D // P
NT = B * T // P
TT = T // P
CW = 512
NC = B * T // CW
CT = CW // P
CPB = T // CW
FF = 4 * D
FC = FF // P
PARTS = 3
Q_PARTS = (0, 0, 0, 1, 1, 2)
K_PARTS = (0, 1, 2, 0, 1, 0)
ROW_MASK = HD * len(Q_PARTS)
ROW_MAX = ROW_MASK + 1
MAX_ROWS = ROW_MASK + 1
EXP_ROWS = ROW_MASK + 3
LDS = 4

SITES = ("l0_out", "l1", "l3_attn", "l3_mlp", "l2_attn", "l2_mlp")
AB = {n: i for i, n in enumerate(SITES)}
AB["l0_in"] = len(SITES)
NS = len(SITES)

COLS = ["emb_b", "sln_b", "ada1_b", "ada2_b", "film1_b", "film2_b"]
COL_MOD = 0
COL_G = 4 * NS
COL_B = COL_G + 2 * NS
COL_L0G, COL_L0B, COL_BK0 = (COL_B + 2 * NS + 2 * i for i in range(3))
COL_L1 = COL_BK0 + 2
COL_L2 = COL_L1 + 4
COL_L3 = COL_L2 + 4
COL_L3S = COL_L3 + 4
COL_M2 = COL_L3S + 4
COL_M3 = COL_M2 + FC
NCOL = COL_M3 + FC

ROWS = ["bq0", "bv0", "ob0", "gate0", "gate1", "bv1", "bp1", "bg1", "bb1", "lng1", "lnb1",
        "bv2", "bp2", "b22", "bv3", "bo3", "b23"]
ROW = {n: i for i, n in enumerate(ROWS)}
EARLY_ROWS = 5


def build(nc, ins, out):
    ctx = ExitStack()
    with ctx:
        def sb(name, shape, dt=F32):
            return ctx.enter_context(nc.sbuf_tensor(name, shape, dt))

        class Sems(dict):
            def __missing__(self, name):
                self[name] = ctx.enter_context(nc.semaphore(name))
                return self[name]

        S = Sems()

        MLP = {"l2": "l2m", "l3": "l3m"}
        NORMS = ("l0_in", "l0_out", "l1", "l1_post", "l2_attn", "l2_mlp", "l3_attn", "l3_mlp")
        ADDS = ("l0", "l1a", "l2a", "l2m", "l3a", "l3m")
        HEADED = ("l1", "l3")
        NQK = 2 * CC * NC
        TURNED = tuple(n for n in NORMS if n != "l1_post")
        COUNTS = {
            "xh": (NORMS, NC), "transposed": (TURNED, 2 * NC), "h": (TURNED, 2 * NC),
            "pre": (ADDS, NC), "out": (ADDS, 2 * NC), "x": (ADDS, 2 * NC),
            "hid": (("l2", "l3"), FC * NC), "gelu": (("l2", "l3"), FC * NC),
            "v": (HEADED, 2 * NC), "vp": (HEADED, 2 * NC),
            "max_used": (HEADED, 2 * TT * NH), "max_scores": (HEADED, 2 * TT * NH),
            "exp": (HEADED, TT * NH), "scores": (HEADED, TT * NH), "values": (HEADED, TT * NH),
            "sums": (HEADED, 16), "sums_inv": (HEADED, 1), "sums_back": (HEADED, 16),
            "sums_raw": (HEADED, 1), "on": (HEADED, NC), "ones": (HEADED, 1), "rot": (("l3",), NQK),
        }
        for n in ("qkp", "qk_used", "r1", "part0", "part1", "part2"):
            COUNTS[n] = (HEADED, NQK)
        for n in ("out_used", "max_turned", "max_split", "max_copied", "max_min", "max_hi"):
            COUNTS[n] = (HEADED, NH)
        for i in range(LDS):
            COUNTS[f"pqk_{i}"] = (HEADED, 16 * (NQK // 4))
            COUNTS[f"max_row_{i}"] = (HEADED, 16 * (NH // LDS))
            COUNTS[f"stack_{i}"] = (HEADED, 16 * 6 * (NH // LDS))
        for i in range(2):
            COUNTS[f"head_v_{i}"] = (HEADED, 16 * (NH // 2))
            COUNTS[f"stored_{i}"] = (HEADED, 16 * (NH // 2))
            COUNTS[f"heads_out_{i}"] = (HEADED, 64 * (NC // 2))

        def at(name, stage, value):
            stages, per_stage = COUNTS[name]
            return S[name], value + stages.index(stage) * per_stage

        X = sb("X", [P, NT, D])
        hT = sb("hT", [P, CC, B * T])
        xh = sb("xh", [P, 2, CT, D])
        arena = sb("arena", [P, 4 * NT * D])
        aux = sb("aux", [P, NT * D])
        work = sb("work", [P, 4, CW])
        split = sb("split", [P, 4 * PARTS * CW // 2])
        wA = sb("wA", [P, 4, CC, D])
        wB = sb("wB", [P, 6, CC, D])
        wM = sb("wM", [P, 8, CC * D])
        cols = sb("cols", [P, NCOL])
        rows = sb("rows", [P, len(ROWS), D])
        ident = sb("ident", [P, P])
        identb = sb("identb", [P, P], BF16)
        bdmask = sb("bdmask", [P, P])
        condT = sb("condT", [P, CC, B])
        scond = sb("scond", [P, CC, B])
        mods = sb("mods", [P, 4 * NS, B])
        modg = sb("modg", [P, NS, CC, B])
        ab = sb("ab", [P, NS + 1, 2, CC, B])
        abrow = sb("abrow", [P, B, 2, D])
        stats = sb("stats", [P, NT, 6])
        mv = sb("mv", [P, NT, 2])
        ve = sb("ve", [P, NT])
        rstd = sb("rstd", [P, NT])
        mhalf = sb("mhalf", [P, NT])
        nmx = sb("nmx", [P, 4, 16])
        mx = sb("mx", [P, 4, 8])
        zeros8 = sb("zeros8", [P, 8])
        msplit = sb("msplit", [P, 4, 16], BF16)
        mrow = sb("mrow", [16, 4, P], BF16)
        nm2 = sb("nm2", [P, NT])
        sum2 = sb("sum2", [P, NT])
        rinv2 = sb("rinv2", [P, NT])
        Vc = sb("Vc", [P, 2, 2 * HD, TT])
        OE = sb("OE", [P, 2, 256])
        k_nmax = sb("k_nmax", [P, CC * B])
        k_sum = sb("k_sum", [P, CC * B])

        Q4 = NT * D
        condW = arena[:, 0:CC * NS * 2 * D].rearrange("p (k n) -> p k n", k=CC)
        condBC = arena[:, 3 * Q4:3 * Q4 + CC * B * P].rearrange("p (k b m) -> p k b m", k=CC, b=B)
        maskf = arena[:, 3 * Q4 + 1024:3 * Q4 + 2048]
        masku = arena[:, 3 * Q4 + 2048:3 * Q4 + 2304].bitcast(U8)
        maskb = arena[:, 3 * Q4 + 2304:3 * Q4 + 2816].bitcast(BF16)
        kTs = arena[:, 0:Q4].rearrange("p (m t) -> p m t", m=CC)
        q_sb = arena[:, Q4:2 * Q4].rearrange("p (n d) -> p n d", d=D)
        v_sb = arena[:, 2 * Q4:3 * Q4].rearrange("p (n d) -> p n d", d=D)
        ekt = arena[:, 3 * Q4:].rearrange("p (n d) -> p n d", d=D)
        qTs = aux[:, :].rearrange("p (m t) -> p m t", m=CC)
        ctx_sb = work[:, 0, :].rearrange("p (b m d) -> p b m d", b=B, m=CC)
        wo_g = work[:, 2:4, :].rearrange("p b (k d) -> p b k d", k=CC)
        gbias = split[:, 0:B * D].rearrange("p (b d) -> p b d", b=B)
        q_red = split[:, B * D:B * D + NT * 2 * H].rearrange("p (n s h) -> p n s h", n=NT, s=2)
        parts = split[:, :].bitcast(BF16).rearrange("p (s i t) -> p s i t", s=4, i=PARTS)
        rope = arena[:, 3 * Q4 + 1024:3 * Q4 + 1024 + 2 * T].rearrange("p (a t) -> p a t", a=2)
        QS = arena[:, 0:Q4 // 2].bitcast(BF16).rearrange("p (s t) -> p s t", s=LDS)
        KS = arena[:, Q4 // 2:Q4].bitcast(BF16).rearrange("p (s t) -> p s t", s=LDS)
        PT = arena[:, Q4:2 * Q4].rearrange("p (s t) -> p s t", s=4)
        Vh = arena[:, 2 * Q4:3 * Q4].rearrange("p (i d k) -> p i d k", i=NH, d=HD)
        OTn = aux[:, 0:2 * CC * CW].rearrange("p (s m t) -> p s m t", s=2, m=CC)
        RT = aux[:, 2 * CC * CW:].rearrange("p (s m t) -> p s m t", s=2, m=CC)
        Rs = arena[:, 3 * Q4:3 * Q4 + 256]
        QT2 = arena[:, 0:Q4].rearrange("p (m t) -> p m t", m=CC)
        KT2 = arena[:, Q4:2 * Q4].rearrange("p (m t) -> p m t", m=CC)
        V2 = arena[:, 2 * Q4:3 * Q4].rearrange("p (n d) -> p n d", d=D)
        PT4 = arena[:, 3 * Q4:].rearrange("p (k q) -> p k q", k=TT)
        P2 = work[:, :, :].rearrange("p (s h) t -> p s (h t)", s=2)
        G = arena[:, 0:2 * FC * CW].rearrange("p (s f t) -> p s f t", s=2, f=FC)
        wM1 = wM[:, 0:4, :].rearrange("p a b -> p (a b)").rearrange("p (k n) -> p k n", k=CC)
        wM2 = wM[:, 4:8, :].rearrange("p a b -> p (a b)").rearrange("p (f d) -> p f d", f=FC)

        PQK = nc.dram_tensor("pqk", (2, NH, HD, PARTS, T), BF16, kind="Internal").ap()
        OD = nc.dram_tensor("od", (NH, 2 * HD, T), F32, kind="Internal").ap()
        RD = nc.dram_tensor("rd", (NH, T), F32, kind="Internal").ap()
        MD = nc.dram_tensor("md", (NH, T), BF16, kind="Internal").ap()

        PS = ctx.enter_context(nc.psum_tensor("PS", [P, 8, CW], F32))

        def bank(i):
            return PS[:, i, :]

        def bank2(i):
            return PS[:, i:i + 2, :].rearrange("p a b -> p (a b)")

        def banks2t(i):
            return PS[:, i, :].rearrange("p (t d) -> p t d", t=2)

        ready = {
            "l0_in": lambda e, c: e.wait_ge(S[f"x_{c}"], 16),
            "l0_out": lambda e, c: e.wait_ge(S["l0_y"], 2 * c + 2),
            "l1": lambda e, c: e.wait_ge(*at("x", "l0", 2 * c + 2)),
            "l1_post": lambda e, c: e.wait_ge(*at("x", "l1a", 2 * c + 2)),
            "l2_attn": lambda e, c: e.wait_ge(S["x_l1"], c + 1),
            "l2_mlp": lambda e, c: e.wait_ge(*at("x", "l2a", 2 * c + 2)),
            "l3_attn": lambda e, c: e.wait_ge(*at("x", "l2m", 2 * c + 2)),
            "l3_mlp": lambda e, c: e.wait_ge(*at("x", "l3a", 2 * c + 2)),
        }
        ORDER = ["l0_in", "l0_out", "l1", "l1_post", "l2_attn", "l2_mlp", "l3_attn", "l3_mlp"]
        RMS = {"l2_attn": True, "l2_mlp": True}

        def norm_stats(dve, site, src, c):
            ready[site](dve, c)
            for k in range(CT):
                n = CT * c + k
                nc.vector.bn_stats(stats[:, n, :], src[:, n, :]).then_inc(S["stats"], 1)
            done = NT * ORDER.index(site) + CT * (c + 1)
            dve.wait_ge(S["stats"], done)
            for k in range(CT):
                n = CT * c + k
                last = nc.vector.bn_aggr(mv[:, n, :], stats[:, n, :])
            last.then_inc(S["moments"], 1)
            if site in RMS:
                sl = slice(CT * c, CT * c + CT)
                dve.wait_ge(S["moments"], NC * ORDER.index(site) + c + 1)
                nc.vector.tensor_tensor(ve[:, sl], mv[:, sl, 0], mv[:, sl, 0], ALU.mult).then_inc(S["msq"], 1)
                r = 2 * (NC * (site == "l2_mlp") + c)
                dve.wait_ge(S["msq"], r + 1)
                nc.vector.tensor_tensor(mv[:, sl, 1], mv[:, sl, 1], ve[:, sl], ALU.add).then_inc(S["msq"], 1)

        def norm_rstd(pool, site, c):
            k = NC * ORDER.index(site) + c
            sl = slice(CT * c, CT * c + CT)
            if site in RMS:
                pool.wait_ge(S["msq"], 2 * (NC * (site == "l2_mlp") + c) + 2)
            else:
                pool.wait_ge(S["moments"], k + 1)
            nc.gpsimd.tensor_scalar(ve[:, sl], mv[:, sl, 1], 1e-6 if site in RMS else 1e-5, None,
                                    ALU.add).then_inc(S["var_eps"], 1)
            pool.wait_ge(S["var_eps"], k + 1)
            nc.gpsimd.tensor_tensor(rstd[:, sl], ve[:, sl], mhalf[:, sl], ALU.pow).then_inc(S["rstd"], 1)

        def norm_apply(dve, site, src, c):
            i = NC * ORDER.index(site) + c
            dve.wait_ge(S["rstd"], i + 1)
            if site == "l1_post" and c >= 2:
                dve.wait_ge(S["x_l1"], c - 1)
            elif c >= 2:
                dve.wait_ge(*at("transposed", site, 2 * (c - 1)))
            for k in range(CT):
                n = CT * c + k
                if site in RMS:
                    last = nc.vector.tensor_scalar(xh[:, c % 2, k, :], src[:, n, :], rstd[:, n:n + 1],
                                                   None, ALU.mult)
                else:
                    last = nc.vector.tensor_scalar(xh[:, c % 2, k, :], src[:, n, :], mv[:, n, 0:1],
                                                   rstd[:, n:n + 1], ALU.subtract, ALU.mult)
            last.then_inc(S["xh"], 1)

        def norm_transpose(pe, site, c):
            pe.wait_ge(*at("xh", site, c + 1))
            for m in range(CC):
                if c:
                    pe.wait_ge(*at("h", site, 2 * (c - 1) + m + 1))
                for k in range(CT):
                    last = nc.tensor.transpose(PS[:, m, k * P:(k + 1) * P],
                                               xh[:, c % 2, k, m * P:(m + 1) * P], ident[:, :])
                last.then_inc(S["transposed"], 1)

        def norm_modulate(act, site, c, func=ACT.Identity):
            b = c // CPB
            i = AB[site]
            for m in range(CC):
                act.wait_ge(*at("transposed", site, 2 * c + m + 1))
                nc.scalar.activation(hT[:, m, c * CW:(c + 1) * CW], bank(m), func,
                                     bias=ab[:, i, 1, m, b:b + 1],
                                     scale=ab[:, i, 0, m, b:b + 1]).then_inc(S["h"], 1)

        def h_chunk(m, c):
            return hT[:, m, c * CW:(c + 1) * CW]

        def h_tile(m, n):
            return hT[:, m, n * P:(n + 1) * P]

        def add_rows(pool, site, name, row):
            for c in range(NC):
                pool.wait_ge(*at("xh", site, c + 1))
                bias = row(c // CPB)
                nc.gpsimd.tensor_tensor(X[:, CT * c:CT * c + CT, :], X[:, CT * c:CT * c + CT, :],
                                        bias[:, None, :].to_broadcast([P, CT, D]),
                                        ALU.add).then_inc(S["pre"], 1)

        def add_to_x(dve, name, c, b0):
            dve.wait_ge(*at("pre", name, c + 1))
            for p in range(2):
                n = CT * c + 2 * p
                dve.wait_ge(*at("out", name, 2 * c + p + 1))
                nc.vector.tensor_tensor(X[:, n:n + 2, :], banks2t(b0 + p), X[:, n:n + 2, :],
                                        ALU.add).then_inc(S["x"], 1)

        def project_tiles(pe, name, c, b0, lhs, w, wait_bank=True):
            nk = len(w)
            for p in range(2):
                if c and wait_bank:
                    pe.wait_ge(*at("x", name, 2 * (c - 1) + p + 1))
                for q in range(2):
                    for k in range(nk):
                        last = nc.tensor.matmul(PS[:, b0 + p, q * D:(q + 1) * D], lhs(k, 2 * p + q), w[k],
                                                start=(k == 0), stop=(k == nk - 1))
                last.then_inc(S["out"], 1)

        def sp_loads(sp):
            sp.dma_start(condW, ins["cond_w"].rearrange("(k p) n -> p k n", p=P)).then_inc(S["w_cond"], 16)
            for c in range(NC):
                sp.dma_start(X[:, CT * c:CT * c + CT, :],
                             ins["x"].rearrange("b (n p) d -> p (b n) d", p=P)[:, CT * c:CT * c + CT, :]
                             ).then_inc(S[f"x_{c}"], 16)
            sp.dma_start(wA[:, 0:4], ins["w_l0"].rearrange("w (k p) n -> p w k n", p=P)).then_inc(S["w_l0"], 16)
            sp.dma_start(masku[0:1], ins["mask"][0:1, :]).then_inc(S["mask_u8"], 16)
            sp.dma_start(masku[32:33], ins["mask"][1:2, :]).then_inc(S["mask_u8"], 16)
            sp.dma_start(wB[:, 0:4], ins["w_l1"].rearrange("w (k p) n -> p w k n", p=P)).then_inc(S["w_l1"], 16)
            sp.dma_start(wM1, ins["w_m2a"].rearrange("(k p) n -> p k n", p=P)).then_inc(S["w_m2"], 16)
            sp.dma_start(wM2, ins["w_m2b"].rearrange("(k p) n -> p k n", p=P)).then_inc(S["w_m2"], 16)
            sp.wait_ge(S["mask_bias"], 1)
            for b in range(B):
                sp.dma_start(MD[b * H:(b + 1) * H, :],
                             maskb[32 * b:32 * b + 1, None, :].to_broadcast([1, H, T])).then_inc(S["mask_dram"], 16)

        def act_loads(act):
            act.dma_start(cols[:, :], ins["cols"]).then_inc(S["small"], 16)
            act.dma_start(condT[:, :, :], ins["condT"]).then_inc(S["small"], 16)
            act.dma_start(ident[:, :], ins["ident"]).then_inc(S["small"], 16)
            act.dma_start(bdmask[:, :], ins["bdmask"]).then_inc(S["small"], 16)
            act.dma_start(rows[:, :, :], ins["rows"].partition_broadcast(P)).then_inc(S["rows"], 16)

        def pe_cond(pe):
            pe.wait_ge(S["w_cond"], 16)
            pe.wait_ge(S["small"], 64)
            pe.wait_ge(S["scond"], 1)
            pe.wait_ge(S["cond_bc"], 1)
            for b in range(B):
                for k in range(CC):
                    last = nc.tensor.matmul(bank(6 + b), condBC[:, k, b, :],
                                            condW[:, k, 2 * D:4 * D], start=(k == 0), stop=(k == CC - 1))
            last.then_inc(S["cond_rows"], 1)
            for i in range(4 * NS):
                c = scond if i < 4 else condT
                for k in range(CC):
                    last = nc.tensor.matmul(PS[:, 5, i * B:(i + 1) * B], condW[:, k, i * P:(i + 1) * P],
                                            c[:, k, :], start=(k == 0), stop=(k == CC - 1))
            last.then_inc(S["cond_cols"], 1)

        def dve_cond(dve):
            nc.vector.memset(mhalf[:, :], -0.5)
            nc.vector.memset(zeros8[:, :], 0.0)
            nc.vector.memset(Vc[:, :, :, :], 1.0).then_inc(S["consts"], 1)
            dve.wait_ge(S["small"], 64)
            nc.vector.tensor_copy(identb[:, :], ident[:, :]).then_inc(S["consts"], 1)
            nc.vector.tensor_copy(condBC, condT[:, :, :, None].to_broadcast([P, CC, B, P])).then_inc(S["cond_bc"], 1)
            nc.vector.tensor_copy(ab[:, NS, 0], cols[:, COL_L0G:COL_L0G + 2, None].to_broadcast([P, CC, B]))
            nc.vector.tensor_copy(ab[:, NS, 1], cols[:, COL_L0B:COL_L0B + 2, None].to_broadcast([P, CC, B])
                                  ).then_inc(S["ab_in"], 1)

        def dve_cond2(dve):
            dve.wait_ge(S["mask_u8"], 32)
            for q in (0, 32):
                nc.vector.tensor_scalar(maskf[q:q + 1, :], masku[q:q + 1, :], 1.0, 3e38, ALU.subtract,
                                        ALU.mult).then_inc(S["mask_f32"], 1)
            dve.wait_ge(S["mask_f32"], 2)
            for q in (0, 32):
                last = nc.vector.tensor_scalar(maskb[q:q + 1, :], maskf[q:q + 1, :], 10.0, None, ALU.mult)
            last.then_inc(S["mask_bias"], 1)
            dve.wait_ge(S["cond_cols"], 1)
            nc.vector.tensor_tensor(mods[:, :, :], PS[:, 5, 0:4 * NS * B].rearrange("p (i b) -> p i b", b=B),
                                    cols[:, 0:4 * NS, None].to_broadcast([P, 4 * NS, B]), ALU.add).then_inc(S["mod"], 1)
            dve.wait_ge(S["mod"], 1)
            m4 = mods[:, :, :].rearrange("p (s h c) b -> p s h c b", s=NS, h=2)
            nc.vector.tensor_scalar(modg[:, :], m4[:, :, 0], 1.0, None, ALU.add).then_inc(S["mod"], 1)
            dve.wait_ge(S["mod"], 2)
            nc.vector.tensor_copy(modg[:, 1], m4[:, 1, 0]).then_inc(S["mod"], 1)
            dve.wait_ge(S["mod"], 3)
            g = cols[:, COL_G:COL_G + 2 * NS].rearrange("p (s c) -> p s c", s=NS)
            bb = cols[:, COL_B:COL_B + 2 * NS].rearrange("p (s c) -> p s c", s=NS)
            for b in range(B):
                nc.vector.tensor_tensor(ab[:, 0:NS, 0, :, b], modg[:, :, :, b], g, ALU.mult)
                nc.vector.tensor_tensor(ab[:, 0:4, 1, :, b], modg[:, 0:4, :, b], bb[:, 0:4], ALU.mult).then_inc(S["mod"], 1)
            dve.wait_ge(S["mod"], 5)
            for b in range(B):
                nc.vector.tensor_tensor(ab[:, 0:4, 1, :, b], ab[:, 0:4, 1, :, b], m4[:, 0:4, 1, :, b], ALU.add)
                last = nc.vector.tensor_copy(ab[:, 4:6, 1, :, b], m4[:, 4:6, 1, :, b])
            last.then_inc(S["ab"], 1)
            dve.wait_ge(S["cond_rows"], 1)
            dve.wait_ge(S["rows"], 16)
            for b in range(B):
                r = rows[:, ROW["bg1"]:ROW["bb1"] + 1, :]
                nc.vector.tensor_tensor(abrow[:, b], banks2t(6 + b), r, ALU.add).then_inc(S["abrow"], 1)
                dve.wait_ge(S["abrow"], 3 * b + 1)
                nc.vector.tensor_tensor(xh[:, 1, b, :], abrow[:, b, 0], rows[:, ROW["lnb1"], :], ALU.mult).then_inc(S["abrow"], 1)
                dve.wait_ge(S["abrow"], 3 * b + 2)
                nc.vector.tensor_tensor(abrow[:, b, 0], abrow[:, b, 0], rows[:, ROW["lng1"], :], ALU.mult)
                nc.vector.tensor_tensor(abrow[:, b, 1], abrow[:, b, 1], xh[:, 1, b, :], ALU.add).then_inc(S["abrow"], 1)
            dve.wait_ge(S["w_l0"], 16)
            for b in range(B):
                gate = rows[:, ROW["gate0"] + b, :]
                nc.vector.tensor_tensor(gbias[:, b], rows[:, ROW["ob0"], :], gate, ALU.mult)
                last = nc.vector.tensor_tensor(wo_g[:, b], wA[:, 3], gate[:, None, :].to_broadcast([P, CC, D]), ALU.mult)
            last.then_inc(S["gated"], 1)

        def pe_l0(pe):
            pe.wait_ge(S["consts"], 2)
            for c in range(NC + 1):
                if c < NC:
                    norm_transpose(pe, "l0_in", c)
                if c == 0:
                    continue
                d = c - 1
                if d == 0:
                    pe.wait_ge(S["w_l0"], 16)
                    pe.wait_ge(S["ab"], 1)
                    pe.wait_ge(S["abrow"], 6)
                pe.wait_ge(*at("h", "l0_in", 2 * d + 2))
                for m in range(CC):
                    if d:
                        pe.wait_ge(S["l0_kT"], 2 * (d - 1) + m + 1)
                    for k in range(CC):
                        last = nc.tensor.matmul(bank(4 + m), wA[:, 1, k, m * P:(m + 1) * P], h_chunk(k, d),
                                                start=(k == 0), stop=(k == CC - 1))
                    last.then_inc(S["l0_kp"], 1)
                for p in range(2):
                    for j, w in ((0, 0), (1, 2)):
                        u = 2 * (2 * d + p) + j
                        if u >= 2:
                            pe.wait_ge(S["l0_qv"], u - 1)
                        for q in range(2):
                            for k in range(CC):
                                last = nc.tensor.matmul(PS[:, 6 + j, q * D:(q + 1) * D],
                                                        h_tile(k, CT * d + 2 * p + q), wA[:, w, k, :],
                                                        start=(k == 0), stop=(k == CC - 1))
                        last.then_inc(S["l0_qvp"], 1)
            for c in range(NC):
                pe.wait_ge(S["l0_qn"], 2 * c + 2)
                for m in range(CC):
                    pe.wait_ge(*at("h", "l0_in", 2 * NC)) if c == 0 else pe.wait_ge(S["l0_qT"], 2 * (c - 1) + m + 1)
                    for k in range(CT):
                        last = nc.tensor.transpose(PS[:, m, k * P:(k + 1) * P],
                                                   q_sb[:, CT * c + k, m * P:(m + 1) * P], ident[:, :])
                    last.then_inc(S["l0_qTp"], 1)
            for g in range(NT // 2):
                pe.wait_ge(S["l0_kexp"], 2 * (g // (TT // 2)) + 2)
                if g >= 2:
                    pe.wait_ge(S["l0_ekt"], g - 1)
                for q in range(2):
                    for m in range(CC):
                        n = 2 * g + q
                        last = nc.tensor.transpose(PS[:, 2 + g % 2, q * D + m * P:q * D + (m + 1) * P],
                                                   kTs[:, m, n * P:(n + 1) * P], ident[:, :])
                last.then_inc(S["l0_ektp"], 1)
            pe.wait_ge(S["l0_kT"], 2 * NC)
            pe.wait_ge(S["l0_ekt"], NT // 2)
            for b in range(B):
                for m in range(CC):
                    for k in range(TT):
                        n = TT * b + k
                        last = nc.tensor.matmul(PS[:, 4, (CC * b + m) * P:(CC * b + m + 1) * P],
                                                ekt[:, n, m * P:(m + 1) * P], v_sb[:, n, m * P:(m + 1) * P],
                                                start=(k == 0), stop=(k == TT - 1))
            last.then_inc(S["l0_ctxp"], 1)
            pe.wait_ge(S["l0_ctx"], 4)
            pe.wait_ge(S["l0_qT"], 2 * NC)
            pe.wait_ge(S["l0_qv"], 4 * NC)
            for g in range(NT // 2):
                if g >= 2:
                    pe.wait_ge(S["l0_y"], g - 1)
                for q in range(2):
                    n = 2 * g + q
                    for m in range(CC):
                        last = nc.tensor.matmul(PS[:, 6 + g % 2, q * D + m * P:q * D + (m + 1) * P],
                                                qTs[:, m, n * P:(n + 1) * P], ctx_sb[:, n // TT, m, :],
                                                start=True, stop=True)
                last.then_inc(S["l0_yp"], 1)
            for c in range(NC + 1):
                if c < NC:
                    norm_transpose(pe, "l0_out", c)
                if c:
                    d = c - 1
                    pe.wait_ge(*at("h", "l0_out", 2 * d + 2))
                    if d == 0:
                        pe.wait_ge(S["gated"], 1)
                    project_tiles(pe, "l0", d, 2, lambda k, q: h_tile(k, CT * d + q),
                                  [wo_g[:, d // CPB, k, :] for k in range(CC)])

        def act_l0(act):
            act.wait_ge(S["ab_in"], 1)
            for c in range(NC + 1):
                if c < NC:
                    norm_modulate(act, "l0_in", c)
                if c:
                    d = c - 1
                    for m in range(CC):
                        act.wait_ge(S["l0_kp"], 2 * d + m + 1)
                        nc.scalar.activation(kTs[:, m, d * CW:(d + 1) * CW], bank(4 + m), ACT.Identity,
                                             bias=cols[:, COL_BK0 + m:COL_BK0 + m + 1]).then_inc(S["l0_kT"], 1)
            for g in range(NT // 2):
                act.wait_ge(S["l0_qsub"], g + 1)
                nc.scalar.activation(q_sb[:, 2 * g:2 * g + 2, :], q_sb[:, 2 * g:2 * g + 2, :],
                                     ACT.Exp).then_inc(S["l0_qexp"], 1)
            for b in range(B):
                for m in range(CC):
                    i = CC * b + m
                    act.wait_ge(S["l0_kmax"], i + 1)
                    kk = kTs[:, m, b * T:(b + 1) * T]
                    nc.scalar.activation(kk, kk, ACT.Exp, bias=k_nmax[:, i:i + 1],
                                         accum_out=k_sum[:, i:i + 1]).then_inc(S["l0_kexp"], 1)
            for c in range(NC):
                for m in range(CC):
                    act.wait_ge(S["l0_qTp"], 2 * c + m + 1)
                    nc.scalar.copy(qTs[:, m, c * CW:(c + 1) * CW], bank(m)).then_inc(S["l0_qT"], 1)
            for g in range(NT // 2):
                act.wait_ge(S["l0_yp"], g + 1)
                nc.scalar.copy(q_sb[:, 2 * g:2 * g + 2, :], banks2t(6 + g % 2)).then_inc(S["l0_y"], 1)
            act.wait_ge(S["ab"], 1)
            for c in range(NC):
                norm_modulate(act, "l0_out", c, ACT.Silu)

        def q_heads(g):
            return q_sb[:, 2 * g:2 * g + 2, :].rearrange("p n (h d) -> p n h d", h=H)

        def dve_l0(dve):
            dve_cond(dve)
            for c in range(NC + 2):
                if c < NC:
                    norm_stats(dve, "l0_in", X, c)
                if 1 <= c <= NC:
                    norm_apply(dve, "l0_in", X, c - 1)
                if c == 1:
                    dve_cond2(dve)
                if c < 2:
                    continue
                d = c - 2
                for p in range(2):
                    g = 2 * d + p
                    for j, (dst, r) in enumerate(((q_sb, "bq0"), (v_sb, "bv0"))):
                        dve.wait_ge(S["l0_qvp"], 2 * g + j + 1)
                        nc.vector.tensor_tensor(dst[:, 2 * g:2 * g + 2, :], banks2t(6 + j),
                                                rows[:, ROW[r], None, :].to_broadcast([P, 2, D]),
                                                ALU.add).then_inc(S["l0_qv"], 1)
                    dve.wait_ge(S["l0_qv"], 2 * g + 1)
                    nc.vector.tensor_reduce(q_red[:, 2 * g:2 * g + 2, 0, :], q_heads(g), AX.X,
                                            ALU.max).then_inc(S["l0_qmax"], 1)
            for b in range(B):
                for m in range(CC):
                    i = CC * b + m
                    dve.wait_ge(S["l0_kT"], 2 * (CPB * b + CPB - 1) + m + 1)
                    nc.vector.tensor_reduce(k_nmax[:, i:i + 1], kTs[:, m, b * T:(b + 1) * T], AX.X, ALU.max,
                                            negate=True).then_inc(S["l0_kmax"], 1)
            for g in range(NT // 2):
                sl = q_red[:, 2 * g:2 * g + 2, 1, :]
                dve.wait_ge(S["l0_qexp"], g + 1)
                nc.vector.tensor_reduce(sl, q_heads(g), AX.X, ALU.add).then_inc(S["l0_qsum"], 1)
                dve.wait_ge(S["l0_qsum"], g + 1)
                nc.vector.reciprocal(sl, sl).then_inc(S["l0_qinv"], 1)
            dve.wait_ge(S["mask_dram"], 32)
            for g in range(NT // 2):
                dve.wait_ge(S["l0_ektp"], g + 1)
                nc.vector.tensor_copy(ekt[:, 2 * g:2 * g + 2, :], banks2t(2 + g % 2)).then_inc(S["l0_ekt"], 1)
            dve.wait_ge(S["l0_kexp"], B * CC)
            nc.vector.reciprocal(k_sum[:, :], k_sum[:, :]).then_inc(S["l0_kinv"], 1)
            dve.wait_ge(S["l0_kinv"], 1)
            dve.wait_ge(S["l0_ctxp"], 1)
            for b in range(B):
                for m in range(CC):
                    i = CC * b + m
                    nc.vector.scalar_tensor_tensor(ctx_sb[:, b, m, :], PS[:, 4, i * P:(i + 1) * P],
                                                   k_sum[:, i:i + 1], bdmask[:, :], ALU.mult,
                                                   ALU.mult).then_inc(S["l0_ctx"], 1)
            for c in range(NC + 2):
                if c < NC:
                    norm_stats(dve, "l0_out", q_sb, c)
                if 1 <= c <= NC:
                    norm_apply(dve, "l0_out", q_sb, c - 1)
                if c >= 2:
                    add_to_x(dve, "l0", c - 2, 2)

        def pool_l0(pool):
            pool.wait_ge(S["consts"], 1)
            for c in range(NC):
                norm_rstd(pool, "l0_in", c)
            for g in range(NT // 2):
                pool.wait_ge(S["l0_qmax"], g + 1)
                nc.gpsimd.tensor_tensor(q_heads(g), q_heads(g),
                                        q_red[:, 2 * g:2 * g + 2, 0, :, None].to_broadcast([P, 2, H, HD]),
                                        ALU.subtract).then_inc(S["l0_qsub"], 1)
            for g in range(NT // 2):
                pool.wait_ge(S["l0_qinv"], g + 1)
                nc.gpsimd.tensor_tensor(q_heads(g), q_heads(g),
                                        q_red[:, 2 * g:2 * g + 2, 1, :, None].to_broadcast([P, 2, H, HD]),
                                        ALU.mult).then_inc(S["l0_qn"], 1)
            pool.wait_ge(S["gated"], 1)
            add_rows(pool, "l0_in", "l0", lambda b: gbias[:, b, :])
            for c in range(NC):
                norm_rstd(pool, "l0_out", c)

        HEADS = {
            "l1": dict(w=wB, col=COL_L1, bv="bv1", scale=1.0, rope=False, loads=6, rsum=1.0 / 16.0),
            "l3": dict(w=wB, col=COL_L3, bv="bv3", scale=HD ** -0.5, rope=True, loads=7, rsum=1.0),
        }
        SITE = {"l1": "l1", "l3": "l3_attn"}
        LAYER = {"l1": 0, "l3": 1}

        def pe_qkv(pe, L):
            w, rot = HEADS[L]["w"], HEADS[L]["rope"]
            pe.wait_ge(S["w_" + L], 16)
            for c in range(NC + 1):
                if c < NC:
                    norm_transpose(pe, SITE[L], c)
                if c == 0:
                    continue
                d = c - 1
                pe.wait_ge(*at("h", SITE[L], 2 * d + 2))
                if d == 0 and L == "l1":
                    pe.wait_ge(S["l0_y"], NT // 2)
                    pe.wait_ge(*at("x", "l0", 2 * NC))
                if d == 0 and L == "l3":
                    pe.wait_ge(*at("x", "l2m", 2 * NC))
                    pe.wait_ge(*at("gelu", "l2", FC * NC))
                for j in range(2 * CC):
                    i = 2 * CC * d + j
                    b0 = 4 + 2 * (i % 2)
                    if i >= 2:
                        pe.wait_ge(*at("qk_used", L, i - 1))
                    for k in range(CC):
                        last = nc.tensor.matmul(bank(b0), w[:, j // 2, k, (j % 2) * P:(j % 2 + 1) * P],
                                                h_chunk(k, d), start=(k == 0), stop=(k == CC - 1))
                    if rot:
                        for k in range(CC):
                            last = nc.tensor.matmul(bank(b0 + 1),
                                                    w[:, 4 + j // 2, k, (j % 2) * P:(j % 2 + 1) * P],
                                                    h_chunk(k, d), start=(k == 0), stop=(k == CC - 1))
                    last.then_inc(S["qkp"], 1)
                for p in range(2):
                    if d:
                        pe.wait_ge(*at("v", L, 2 * (d - 1) + p + 1))
                    for q in range(2):
                        for k in range(CC):
                            last = nc.tensor.matmul(PS[:, 2 + p, q * D:(q + 1) * D],
                                                    h_tile(k, CT * d + 2 * p + q), w[:, 2, k, :],
                                                    start=(k == 0), stop=(k == CC - 1))
                    last.then_inc(S["vp"], 1)

        def act_split(act, L, i, stage):
            if stage == 0:
                if not HEADS[L]["rope"]:
                    act.wait_ge(*at("qkp", L, i + 1))
                    if i >= 2:
                        act.wait_ge(*at("r1", L, i - 1))
                    col = HEADS[L]["col"] + i % (2 * CC)
                    nc.scalar.activation(work[:, i % 2, :], bank(4 + 2 * (i % 2)), ACT.Identity,
                                         bias=cols[:, col:col + 1]).then_inc(S["qk_used"], 1)
                    act.wait_ge(*at("qk_used", L, i + 1))
                else:
                    act.wait_ge(*at("rot", L, i + 1))
                if i >= 4:
                    act.wait_ge(*at(f"pqk_{i % 4}", L, 16 * (i // 4)))
                nc.scalar.copy(parts[:, i % 4, 0, :], work[:, i % 2, :]).then_inc(S["part0"], 1)
            else:
                act.wait_ge(*at("r1", L, i + 1))
                nc.scalar.copy(parts[:, i % 4, 1, :], work[:, 2 + i % 2, :]).then_inc(S["part1"], 1)

        def dve_split(dve, L, i, stage):
            if stage == 0:
                if HEADS[L]["rope"]:
                    j, c = i % (2 * CC), i // (2 * CC)
                    t0 = (c % CPB) * CW
                    if i == 0:
                        dve.wait_ge(S["rope"], 16)
                    dve.wait_ge(*at("qkp", L, i + 1))
                    if i >= 2:
                        dve.wait_ge(*at("part2", L, i - 1))
                    nc.vector.scalar_tensor_tensor(work[:, i % 2, :], bank(4 + 2 * (i % 2)),
                                                   cols[:, COL_L3 + j:COL_L3 + j + 1],
                                                   rope[:, 0, t0:t0 + CW], ALU.add, ALU.mult)
                    nc.vector.scalar_tensor_tensor(work[:, 2 + i % 2, :], bank(5 + 2 * (i % 2)),
                                                   cols[:, COL_L3S + j:COL_L3S + j + 1],
                                                   rope[:, 1, t0:t0 + CW], ALU.add,
                                                   ALU.mult).then_inc(S["qk_used"], 1)
                    dve.wait_ge(*at("qk_used", L, i + 1))
                    nc.vector.tensor_tensor(work[:, i % 2, :], work[:, i % 2, :], work[:, 2 + i % 2, :],
                                            ALU.add).then_inc(S["rot"], 1)
            elif stage == 1:
                dve.wait_ge(*at("part0", L, i + 1))
                if i >= 2:
                    dve.wait_ge(*at("part2", L, i - 1))
                nc.vector.tensor_tensor(work[:, 2 + i % 2, :], work[:, i % 2, :], parts[:, i % 4, 0, :],
                                        ALU.subtract).then_inc(S["r1"], 1)
            else:
                dve.wait_ge(*at("part1", L, i + 1))
                nc.vector.tensor_tensor(parts[:, i % 4, 2, :], work[:, 2 + i % 2, :], parts[:, i % 4, 1, :],
                                        ALU.subtract).then_inc(S["part2"], 1)

        def act_qkv(act, L):
            for c in range(NC + 1):
                if c < NC:
                    norm_modulate(act, SITE[L], c)
                if c:
                    for j in range(2 * CC):
                        i = 2 * CC * (c - 1) + j
                        act_split(act, L, i, 0)
                        if i:
                            act_split(act, L, i - 1, 1)
            act_split(act, L, NQK - 1, 1)

        def dve_qkv(dve, L):
            two_ones = float(np.array([0x3F803F80], np.uint32).view(np.float32)[0])
            nc.vector.memset(arena[ROW_MASK:EXP_ROWS, 0:Q4], two_ones).then_inc(S["ones"], 1)
            for c in range(NC + 2):
                if c < NC:
                    norm_stats(dve, SITE[L], X, c)
                if 1 <= c <= NC:
                    norm_apply(dve, SITE[L], X, c - 1)
                if c < 2:
                    continue
                d = c - 2
                for j in range(2 * CC):
                    i = 2 * CC * d + j
                    dve_split(dve, L, i, 0)
                    dve_split(dve, L, i, 1)
                    if i:
                        dve_split(dve, L, i - 1, 2)
                b = d // CPB
                for p in range(2):
                    dve.wait_ge(*at("vp", L, 2 * d + p + 1))
                    for q in range(2):
                        k = (CT * d + 2 * p + q) % TT
                        last = nc.vector.tensor_tensor(
                            Vh[:, b * H:(b + 1) * H, :, k],
                            PS[:, 2 + p, q * D:(q + 1) * D].rearrange("p (h d) -> p h d", h=H),
                            rows[:, ROW[HEADS[L]["bv"]], :].rearrange("p (h d) -> p h d", h=H), ALU.add)
                    last.then_inc(S["v"], 1)
            dve_split(dve, L, NQK - 1, 2)

        def sp_qkv(sp, L):
            for i in range(NQK):
                j, c = i % (2 * CC), i // (2 * CC)
                qk, m = j // 2, j % 2
                h0 = (c // CPB) * H + m * (H // 2)
                t0 = (c % CPB) * CW
                sp.wait_ge(*at("part2", L, i + 1))
                sp.dma_start(PQK[qk, h0:h0 + H // 2, :, :, t0:t0 + CW].rearrange("h d s t -> (h d) s t"),
                             parts[:, i % 4, :, :]).then_inc(S[f"pqk_{i % 4}"], 16)

        def v(it, per_head, e, const=0):
            k = per_head * e + const
            return k if it is None else it * (4 * per_head) + k

        def v4(it, e, n):
            k = n * (e // 4 + 1)
            return k if it is None else it * n + k

        def v2(it, e, n):
            k = n * (e // 2 + 1)
            return k if it is None else it * (2 * n) + k

        def heads_loop(eng, step):
            step(None, 0)
            with eng.Fori(0, NH // 4 - 1) as it:
                for e in range(1, 5):
                    step(it, e)
            for e in range(NH - 3, NH):
                step(None, e)

        def head_at(it, e):
            return e if it is None else it * 4 + e

        def last_of(it, e, ahead):
            return it is None and e + ahead >= NH

        def pe_heads(pe, L):
            def max_tile(it, e, t):
                s = e % LDS
                if t == 0:
                    pe.wait_ge(*at(f"stack_{s}", L, v4(it, e, 16 * HEADS[L]["loads"])))
                for half in range(2):
                    r = 2 * t + half
                    if it is not None or 16 * e + r >= 2:
                        pe.wait_ge(*at("max_used", L, v(it, 16, e, r - 1)))
                    nc.tensor.matmul(bank(4 + half), QS[0:MAX_ROWS, s, t * P:(t + 1) * P],
                                     KS[0:MAX_ROWS, s, half * CW:(half + 1) * CW],
                                     start=True, stop=True).then_inc(S["max_scores"], 1)

            def max_turn(it, e):
                pe.wait_ge(*at("max_split", L, v(it, 1, e, 1)))
                if it is not None or e >= 2:
                    pe.wait_ge(*at("out_used", L, v(it, 1, e, -1)))
                nc.tensor.transpose(PS[:, 6 + e % 2, 256:320].bitcast(BF16)[0:16, 0:P], msplit[:, e % 4, :],
                                    identb[:, :]).then_inc(S["max_turned"], 1)

            def scores(it, e, t):
                s = e % LDS
                if t == 0:
                    pe.wait_ge(*at(f"max_row_{s}", L, v4(it, e, 16)))
                if it is not None or 8 * e + t >= 2:
                    pe.wait_ge(*at("exp", L, v(it, 8, e, t - 1)))
                for half in range(2):
                    last = nc.tensor.matmul(bank(2 * (t % 2) + half), KS[0:EXP_ROWS, s, t * P:(t + 1) * P],
                                            QS[0:EXP_ROWS, s, half * CW:(half + 1) * CW], start=True, stop=True)
                last.then_inc(S["scores"], 1)

            def values(it, e, t):
                pe.wait_ge(*at("exp", L, v(it, 8, e, t + 1)))
                if t == 0:
                    pe.wait_ge(*at(f"head_v_{e % 2}", L, v2(it, e, 16)))
                    if it is not None or e >= 2:
                        pe.wait_ge(*at("out_used", L, v(it, 1, e, -1)))
                for j in range(4):
                    last = nc.tensor.matmul(PS[32 * j:32 * j + 32, 6 + e % 2, 0:256], Vc[:, e % 2, :, t],
                                            PT[:, t % 4, 256 * j:256 * j + 256], start=(t == 0), stop=(t == TT - 1))
                last.then_inc(S["values"], 1)

            def step(it, e):
                for t in range(TT):
                    if not last_of(it, e, 2):
                        max_tile(it, e + 2, t)
                    scores(it, e, t)
                    if t:
                        values(it, e, t - 1)
                    elif it is not None or e:
                        values(it, e - 1, TT - 1)
                    if t == 3 and not last_of(it, e, 1):
                        max_turn(it, e + 1)

            if L == "l1":
                pe.wait_ge(S["consts"], 2)
            pe.wait_ge(*at("ones", L, 1))
            pe.wait_ge(*at("h", SITE[L], 2 * NC))
            pe.wait_ge(*at("qk_used", L, NQK))
            pe.wait_ge(*at("v", L, 2 * NC))
            for e in range(2):
                for t in range(TT):
                    max_tile(None, e, t)
                if e == 0:
                    max_turn(None, 0)
            heads_loop(pe, step)
            values(None, NH - 1, TT - 1)

        def act_heads(act, L):
            def turned(it, e):
                act.wait_ge(*at("max_turned", L, v(it, 1, e, 1)))
                nc.scalar.copy(mrow[:, e % 4, :], PS[:, 6 + e % 2, 256:320].bitcast(BF16)[0:16, 0:P]
                               ).then_inc(S["max_copied"], 1)

            def out_copy(it, e):
                act.wait_ge(*at("values", L, v(it, 8, e, 8)))
                if it is not None or e >= 2:
                    act.wait_ge(*at(f"stored_{e % 2}", L, v2(it, e - 2, 16)))
                nc.scalar.copy(OE[:, e % 2, :], PS[:, 6 + e % 2, 0:256]).then_inc(S["out_used"], 1)

            def step(it, e):
                for t in range(TT):
                    act.wait_ge(*at("scores", L, v(it, 8, e, t + 1)))
                    if it is not None or 8 * e + t >= 4:
                        act.wait_ge(*at("values", L, v(it, 8, e, t - 3)))
                    nc.scalar.activation(PT[:, t % 4, :], bank2(2 * (t % 2)), ACT.Exp,
                                         scale=HEADS[L]["scale"]).then_inc(S["exp"], 1)
                    if t == 1 and (it is not None or e):
                        out_copy(it, e - 1)
                    if t == 4 and not last_of(it, e, 1):
                        turned(it, e + 1)

            turned(None, 0)
            heads_loop(act, step)
            out_copy(None, NH - 1)

        def dve_heads(dve, L):
            def head(it, e):
                for r in range(2 * TT):
                    dve.wait_ge(*at("max_scores", L, v(it, 16, e, r + 1)))
                    nc.vector.tensor_reduce(nmx[:, e, r:r + 1], bank(4 + r % 2), AX.X, ALU.max,
                                            negate=True).then_inc(S["max_used"], 1)
                dve.wait_ge(*at("max_used", L, v(it, 16, e, 16)))
                halves = nmx[:, e, :].rearrange("p (t h) -> p t h", h=2)
                nc.vector.tensor_tensor(mx[:, e, :], halves[:, :, 0], halves[:, :, 1],
                                        ALU.min).then_inc(S["max_min"], 1)
            with dve.Fori(0, NH // 4) as it:
                for e in range(4):
                    head(it, e)

        def pool_heads(pool, L):
            with pool.Fori(0, NH // 4) as it:
                for e in range(4):
                    pool.wait_ge(*at("max_min", L, v(it, 1, e, 1)))
                    nc.gpsimd.tensor_tensor(msplit[:, e, 0:8], mx[:, e, :], zeros8[:, :],
                                            ALU.add).then_inc(S["max_hi"], 1)
                    pool.wait_ge(*at("max_hi", L, v(it, 1, e, 1)))
                    nc.gpsimd.tensor_tensor(msplit[:, e, 8:16], mx[:, e, :], msplit[:, e, 0:8],
                                            ALU.subtract).then_inc(S["max_split"], 1)

        def sp_heads(sp, L):
            def stack(it, e):
                s = e % LDS
                i = head_at(it, e)
                if it is not None or e >= LDS:
                    sp.wait_ge(*at("scores", L, v(it, 8, e, 8 - 8 * LDS)))
                for qk, dst in ((0, QS), (1, KS)):
                    groups = [(0, 3), (3, 5), (5, 6)]
                    for lo, hi in groups:
                        rows_ = dst[HD * lo:HD * hi, s, :]
                        if qk == 0:
                            src = PQK[qk, bass.ds(i, 1), :, Q_PARTS[lo], :].to_broadcast([hi - lo, HD, T])
                        else:
                            src = PQK[qk, bass.ds(i, 1), :, 0:hi - lo, :].rearrange("i d s t -> i s d t")
                        sp.dma_start(rows_, src).then_inc(S[f"stack_{s}"], 16)
                if L == "l3":
                    sp.dma_start(KS[ROW_MASK:ROW_MASK + 1, s, :], MD[bass.ds(i, 1), :]
                                 ).then_inc(S[f"stack_{s}"], 16)

            def head_v(it, e):
                if it is not None or e >= 2:
                    sp.wait_ge(*at("values", L, v(it, 8, e, -8)))
                sp.dma_start(Vc[:, e % 2, 0:HD, :], Vh[:, bass.ds(head_at(it, e), 1), :, :]
                             ).then_inc(S[f"head_v_{e % 2}"], 16)

            def store(it, e):
                sp.wait_ge(*at("out_used", L, v(it, 1, e, 1)))
                i = head_at(it, e)
                sp.dma_start(OD[bass.ds(i, 1)].rearrange("i r (j t) -> i j r t", j=4), OE[:, e % 2, :]
                             ).then_inc(S[f"stored_{e % 2}"], 16)

            def max_row(it, e):
                sp.wait_ge(*at("max_copied", L, v(it, 1, e, 1)))
                sp.dma_start(QS[ROW_MAX:ROW_MAX + 2, e % LDS, :].rearrange("p (t c) -> p t c", t=TT),
                             mrow[:, e % 4, :]).then_inc(S[f"max_row_{e % LDS}"], 16)

            def step(it, e):
                if not last_of(it, e, 3):
                    stack(it, e + 3)
                if not last_of(it, e, 1):
                    head_v(it, e + 1)
                if it is not None or e:
                    store(it, e - 1)
                if not last_of(it, e, 1):
                    max_row(it, e + 1)

            sp.wait_ge(*at("ones", L, 1))
            if L == "l1":
                for s in range(LDS):
                    sp.dma_start(KS[ROW_MASK:ROW_MASK + 1, s, :].bitcast(F32), ins["zeros"]).then_inc(S["zero_rows"], 16)
                sp.wait_ge(S["zero_rows"], 16 * LDS)
            else:
                sp.wait_ge(S["mask_dram"], 32)
            sp.wait_ge(*at("v", L, 2 * NC))
            for s in range(4):
                sp.wait_ge(*at(f"pqk_{s}", L, 16 * (NQK // 4)))
            for e in range(3):
                stack(None, e)
            head_v(None, 0)
            max_row(None, 0)
            heads_loop(sp, step)
            store(None, NH - 1)
            for s in range(2):
                sp.wait_ge(*at(f"stored_{s}", L, 16 * (NH // 2)))
            sp.dma_start(Rs, OD[:, HD, :].rearrange("i (j t) -> i j t", j=4)).then_inc(S["sums"], 16)
            for c in range(2):
                load_out(sp, L, c)
            sp.wait_ge(*at("sums_inv", L, 1))
            sp.dma_start(RD.rearrange("i (j t) -> (i j) t", j=4), Rs).then_inc(S["sums_back"], 16)
            sp.wait_ge(*at("sums_back", L, 16))
            for c in range(NC):
                if c >= 2:
                    sp.wait_ge(*at("out", XN[L], 2 * (c - 1)))
                    load_out(sp, L, c)
                b, t0 = c // CPB, (c % CPB) * CW
                for m in range(CC):
                    h0 = b * H + m * (H // 2)
                    sp.dma_start(RT[:, c % 2, m, :],
                                 RD[h0:h0 + H // 2, None, t0:t0 + CW].to_broadcast([H // 2, HD, CW])
                                 ).then_inc(S[f"heads_out_{c % 2}"], 16)

        XN = {"l1": "l1a", "l3": "l3a"}

        def load_out(sp, L, c):
            b, t0 = c // CPB, (c % CPB) * CW
            for m in range(CC):
                h0 = b * H + m * (H // 2)
                sp.dma_start(OTn[:, c % 2, m, :], OD[h0:h0 + H // 2, 0:HD, t0:t0 + CW]
                             ).then_inc(S[f"heads_out_{c % 2}"], 16)

        def dve_heads_out(dve, L):
            dve.wait_ge(*at("sums", L, 16))
            nc.vector.reciprocal(Rs, Rs).then_inc(S["sums_raw"], 1)
            dve.wait_ge(*at("sums_raw", L, 1))
            nc.vector.tensor_scalar(Rs, Rs, HEADS[L]["rsum"], None, ALU.mult).then_inc(S["sums_inv"], 1)
            for c in range(NC):
                dve.wait_ge(*at(f"heads_out_{c % 2}", L, 64 * (c // 2 + 1)))
                nc.vector.tensor_tensor(OTn[:, c % 2], OTn[:, c % 2], RT[:, c % 2], ALU.mult).then_inc(S["on"], 1)
                if c:
                    add_to_x(dve, XN[L], c - 1, 4)
            add_to_x(dve, XN[L], NC - 1, 4)

        def pe_heads_out(pe, L):
            for c in range(NC):
                pe.wait_ge(*at("on", L, c + 1))
                if c == 0:
                    pe.wait_ge(*at("max_used", L, 16 * NH))
                project_tiles(pe, XN[L], c, 4,
                              lambda k, q: OTn[:, c % 2, k, q * P:(q + 1) * P],
                              [HEADS[L]["w"][:, 3, k, :] for k in range(CC)])

        def dve_l1_post(dve):
            for c in range(NC + 2):
                if c < NC:
                    norm_stats(dve, "l1_post", X, c)
                if 1 <= c <= NC:
                    norm_apply(dve, "l1_post", X, c - 1)
                if c >= 2:
                    d = c - 2
                    sl = X[:, CT * d:CT * d + CT, :]
                    dve.wait_ge(S["l1_mod"], 2 * d + 2)
                    nc.vector.tensor_tensor(sl, sl, xh[:, d % 2], ALU.add).then_inc(S["x_l1"], 1)

        def pool_l1_post(pool):
            for c in range(NC + 1):
                if c < NC:
                    norm_rstd(pool, "l1_post", c)
                if c == 0:
                    continue
                d = c - 1
                b = d // CPB
                pool.wait_ge(*at("xh", "l1_post", d + 1))
                for j, op in ((0, ALU.mult), (1, ALU.add)):
                    if j:
                        pool.wait_ge(S["l1_mod"], 2 * d + 1)
                    nc.gpsimd.tensor_tensor(xh[:, d % 2], xh[:, d % 2],
                                            abrow[:, b, j, None, :].to_broadcast([P, CT, D]), op
                                            ).then_inc(S["l1_mod"], 1)

        def pe_l2(pe):
            pe.wait_ge(S["w_l2"], 16)
            for c in range(NC + 1):
                if c < NC:
                    norm_transpose(pe, "l2_attn", c)
                if c == 0:
                    continue
                d = c - 1
                pe.wait_ge(*at("h", "l2_attn", 2 * d + 2))
                if d == 0:
                    pe.wait_ge(*at("x", "l1a", 2 * NC))
                    pe.wait_ge(*at("out_used", "l1", NH))
                for j in range(2 * CC):
                    if d:
                        pe.wait_ge(S["l2_qk"], 4 * (d - 1) + j + 1)
                    for k in range(CC):
                        last = nc.tensor.matmul(bank(4 + j), wA[:, j // 2, k, (j % 2) * P:(j % 2 + 1) * P],
                                                h_chunk(k, d), start=(k == 0), stop=(k == CC - 1))
                    last.then_inc(S["l2_qkp"], 1)
                for p in range(2):
                    if d:
                        pe.wait_ge(S["l2_v"], 2 * (d - 1) + p + 1)
                    for q in range(2):
                        for k in range(CC):
                            last = nc.tensor.matmul(PS[:, 2 + p, q * D:(q + 1) * D],
                                                    h_tile(k, CT * d + 2 * p + q), wA[:, 2, k, :],
                                                    start=(k == 0), stop=(k == CC - 1))
                    last.then_inc(S["l2_vp"], 1)
            pe.wait_ge(S["l2_qk"], 4 * NC)
            pe.wait_ge(S["l2_v"], 2 * NC)

            def scores(n):
                if n >= 2:
                    pe.wait_ge(S["l2_exp"], n - 1)
                b = n // TT
                for half in range(2):
                    for k in range(CC):
                        last = nc.tensor.matmul(bank(2 * (n % 2) + half), QT2[:, k, n * P:(n + 1) * P],
                                                KT2[:, k, b * T + half * CW:b * T + (half + 1) * CW],
                                                start=(k == 0), stop=(k == CC - 1))
                last.then_inc(S["l2_scores"], 1)

            def turn(n):
                pe.wait_ge(S["l2_exp"], n + 1)
                if n:
                    pe.wait_ge(S["l2_turn_used"], 2 * n)
                for k in range(TT):
                    last = nc.tensor.transpose(PS[:, 4 + k // 4, (k % 4) * P:(k % 4 + 1) * P],
                                               P2[:, n % 2, k * P:(k + 1) * P], ident[:, :])
                    if k % 4 == 3:
                        last.then_inc(S["l2_turned"], 1)

            def values(c):
                b = c // CPB
                pe.wait_ge(S["l2_turn_used"], 2 * CT * (c + 1))
                for m in range(CC):
                    if c or m:
                        pe.wait_ge(S["l2_oT"], 2 * c + m)
                    for k in range(TT):
                        last = nc.tensor.matmul(bank(6), V2[:, b * TT + k, m * P:(m + 1) * P], PT4[:, k, :],
                                                start=(k == 0), stop=(k == TT - 1))
                    last.then_inc(S["l2_op"], 1)

            def project(c):
                pe.wait_ge(S["l2_oT"], 2 * c + 2)
                for q in range(CT):
                    n = CT * c + q
                    if n % 2 == 0 and n:
                        pe.wait_ge(*at("x", "l2a", n // 2))
                    for k in range(CC):
                        last = nc.tensor.matmul(PS[:, 7, (q % 2) * D:(q % 2 + 1) * D],
                                                OTn[:, c % 2, k, q * P:(q + 1) * P], wA[:, 3, k, :],
                                                start=(k == 0), stop=(k == CC - 1))
                    if n % 2:
                        last.then_inc(S["out"], 1)

            scores(0)
            for n in range(NT):
                if n + 1 < NT:
                    scores(n + 1)
                turn(n)
                if n % CT == CT - 1:
                    values(n // CT)
                    project(n // CT)

        def act_l2(act):
            for c in range(NC + 1):
                if c < NC:
                    norm_modulate(act, "l2_attn", c)
                if c:
                    for j in range(2 * CC):
                        d = c - 1
                        act.wait_ge(S["l2_qkp"], 4 * d + j + 1)
                        dst = (QT2 if j < 2 else KT2)[:, j % 2, d * CW:(d + 1) * CW]
                        nc.scalar.activation(dst, bank(4 + j), ACT.Identity,
                                             bias=cols[:, COL_L2 + j:COL_L2 + j + 1]).then_inc(S["l2_qk"], 1)
            for n in range(NT + 1):
                if n < NT:
                    act.wait_ge(S["l2_max"], n + 1)
                    if n >= 2:
                        act.wait_ge(S["l2_turned"], 2 * (n - 1))
                    nc.scalar.activation(P2[:, n % 2, :], bank2(2 * (n % 2)), ACT.Exp, scale=D ** -0.5,
                                         bias=nm2[:, n:n + 1], accum_out=sum2[:, n:n + 1]).then_inc(S["l2_exp"], 1)
                if n:
                    l2_turn_copy(act, n - 1, 1)
                if n and n % CT == 0:
                    c = n // CT - 1
                    for m in range(CC):
                        act.wait_ge(S["l2_op"], 2 * c + m + 1)
                        if c >= 2:
                            act.wait_ge(*at("out", "l2a", 2 * (c - 1)))
                        nc.scalar.copy(OTn[:, c % 2, m, :], bank(6)).then_inc(S["l2_oT"], 1)

        def l2_turn_copy(eng, n, half):
            q = n % CT
            eng.wait_ge(S["l2_turned"], 2 * n + half + 1)
            if n >= CT and q == 0:
                eng.wait_ge(S["l2_op"], 2 * (n // CT))
            src = PS[:, 4 + half, :].rearrange("p (k q) -> p k q", k=4)
            dst = PT4[:, 4 * half:4 * half + 4, q * P:(q + 1) * P]
            if half:
                nc.scalar.copy(dst, src).then_inc(S["l2_turn_used"], 1)
            else:
                nc.vector.tensor_copy(dst, src).then_inc(S["l2_turn_used"], 1)

        def dve_l2(dve):
            for c in range(NC + 2):
                if c < NC:
                    norm_stats(dve, "l2_attn", X, c)
                if 1 <= c <= NC:
                    norm_apply(dve, "l2_attn", X, c - 1)
                if c >= 2:
                    for p in range(2):
                        g = 2 * (c - 2) + p
                        dve.wait_ge(S["l2_vp"], g + 1)
                        nc.vector.tensor_tensor(V2[:, 2 * g:2 * g + 2, :], banks2t(2 + p),
                                                rows[:, ROW["bv2"], None, :].to_broadcast([P, 2, D]),
                                                ALU.add).then_inc(S["l2_v"], 1)

            def maximum(n):
                dve.wait_ge(S["l2_scores"], n + 1)
                nc.vector.tensor_reduce(nm2[:, n:n + 1], bank2(2 * (n % 2)), AX.X, ALU.max,
                                        negate=True).then_inc(S["l2_max_raw"], 1)
                dve.wait_ge(S["l2_max_raw"], n + 1)
                nc.vector.tensor_scalar(nm2[:, n:n + 1], nm2[:, n:n + 1], D ** -0.5, None,
                                        ALU.mult).then_inc(S["l2_max"], 1)

            maximum(0)
            for n in range(NT):
                if n + 1 < NT:
                    maximum(n + 1)
                dve.wait_ge(S["l2_exp"], n + 1)
                nc.vector.reciprocal(rinv2[:, n:n + 1], sum2[:, n:n + 1]).then_inc(S["l2_rinv"], 1)
                l2_turn_copy(dve, n, 0)
                if n % CT == CT - 1:
                    c = n // CT
                    dve.wait_ge(S["l2_rinv"], n + 1)
                    dve.wait_ge(*at("pre", "l2a", c + 1))
                    for p in range(2):
                        dve.wait_ge(*at("out", "l2a", 2 * c + p + 1))
                        for q in range(2):
                            k = CT * c + 2 * p + q
                            last = nc.vector.scalar_tensor_tensor(X[:, k, :], PS[:, 7, q * D:(q + 1) * D],
                                                                  rinv2[:, k:k + 1], X[:, k, :], ALU.mult, ALU.add)
                        last.then_inc(S["x"], 1)

        def pe_mlp(pe, L, site):
            pe.wait_ge(S["w_m" + L[1]], 32)
            for c in range(NC + 2):
                if c < NC:
                    norm_transpose(pe, site, c)
                if 1 <= c <= NC:
                    d = c - 1
                    pe.wait_ge(*at("h", site, 2 * d + 2))
                    if d == 0:
                        pe.wait_ge(*at("x", {"l2": "l2a", "l3": "l3a"}[L], 2 * NC))
                        if L == "l3":
                            pe.wait_ge(*at("out_used", "l3", NH))
                    for f in range(FC):
                        u = FC * d + f
                        if u >= 4:
                            pe.wait_ge(*at("gelu", L, u - 3))
                        for k in range(CC):
                            last = nc.tensor.matmul(bank(4 + u % 4), wM1[:, k, f * P:(f + 1) * P], h_chunk(k, d),
                                                    start=(k == 0), stop=(k == CC - 1))
                        last.then_inc(S["hid"], 1)
                if c >= 2:
                    d = c - 2
                    pe.wait_ge(*at("gelu", L, FC * (d + 1)))
                    project_tiles(pe, MLP[L], d, 2, lambda k, q: G[:, d % 2, k, q * P:(q + 1) * P],
                                  [wM2[:, k, :] for k in range(FC)])

        def act_mlp(act, L, site, col):
            for c in range(NC + 1):
                if c < NC:
                    norm_modulate(act, site, c)
                if c:
                    d = c - 1
                    if d >= 2:
                        act.wait_ge(*at("out", MLP[L], 2 * (d - 1)))
                    for f in range(FC):
                        act.wait_ge(*at("hid", L, FC * d + f + 1))
                        nc.scalar.activation(G[:, d % 2, f, :], bank(4 + (FC * d + f) % 4), ACT.Gelu,
                                             bias=cols[:, col + f:col + f + 1]).then_inc(S["gelu"], 1)

        def dve_mlp(dve, L, site):
            for c in range(NC + 3):
                if c < NC:
                    norm_stats(dve, site, X, c)
                if 1 <= c <= NC:
                    norm_apply(dve, site, X, c - 1)
                if c >= 3:
                    add_to_x(dve, MLP[L], c - 3, 2)

        block = ctx.enter_context(nc.Block())

        @block.sync
        def _(sp):
            sp_loads(sp)
            sp_qkv(sp, "l1")
            sp_heads(sp, "l1")
            sp.wait_ge(*at("x", "l0", 2 * NC))
            sp.dma_start(wA[:, 0:4], ins["w_l2"].rearrange("w (k p) n -> p w k n", p=P)).then_inc(S["w_l2"], 16)
            sp.wait_ge(*at("x", "l1a", 2 * NC))
            sp.dma_start(wB[:, 0:6], ins["w_l3"].rearrange("w (k p) n -> p w k n", p=P)).then_inc(S["w_l3"], 16)
            sp.wait_ge(*at("x", "l2a", 2 * NC))
            sp.dma_start(rope, ins["rope"].rearrange("a p t -> p a t")).then_inc(S["rope"], 16)
            sp.wait_ge(*at("x", "l2m", 2 * NC))
            sp.dma_start(wM1, ins["w_m3a"].rearrange("(k p) n -> p k n", p=P)).then_inc(S["w_m3"], 16)
            sp.dma_start(wM2, ins["w_m3b"].rearrange("(k p) n -> p k n", p=P)).then_inc(S["w_m3"], 16)
            sp_qkv(sp, "l3")
            sp_heads(sp, "l3")
            for c in range(NC):
                sp.wait_ge(*at("x", "l3m", 2 * c + 2))
                sp.dma_start(out.rearrange("b (n p) d -> p (b n) d", p=P)[:, CT * c:CT * c + CT, :],
                             X[:, CT * c:CT * c + CT, :]).then_inc(S["stored"], 16)
            sp.wait_ge(S["stored"], 16 * NC)

        @block.scalar
        def _(act):
            act_loads(act)
            act.wait_ge(S["small"], 64)
            nc.scalar.activation(scond[:, :, :], condT[:, :, :], ACT.Silu).then_inc(S["scond"], 1)
            act_l0(act)
            act_qkv(act, "l1")
            act_heads(act, "l1")
            act_l2(act)
            act_mlp(act, "l2", "l2_mlp", COL_M2)
            act_qkv(act, "l3")
            act_heads(act, "l3")
            act_mlp(act, "l3", "l3_mlp", COL_M3)

        @block.vector
        def _(dve):
            dve_l0(dve)
            dve_qkv(dve, "l1")
            dve_heads(dve, "l1")
            dve_heads_out(dve, "l1")
            dve_l1_post(dve)
            dve_l2(dve)
            dve_mlp(dve, "l2", "l2_mlp")
            dve_qkv(dve, "l3")
            dve_heads(dve, "l3")
            dve_heads_out(dve, "l3")
            dve_mlp(dve, "l3", "l3_mlp")

        @block.gpsimd
        def _(pool):
            def row(name):
                return lambda b: rows[:, ROW[name], :]

            def rstds(site):
                for c in range(NC):
                    norm_rstd(pool, site, c)

            pool_l0(pool)
            rstds("l1")
            add_rows(pool, "l1", "l1a", row("bp1"))
            pool_heads(pool, "l1")
            pool_l1_post(pool)
            rstds("l2_attn")
            add_rows(pool, "l2_attn", "l2a", row("bp2"))
            rstds("l2_mlp")
            add_rows(pool, "l2_mlp", "l2m", row("b22"))
            rstds("l3_attn")
            add_rows(pool, "l3_attn", "l3a", row("bo3"))
            pool_heads(pool, "l3")
            rstds("l3_mlp")
            add_rows(pool, "l3_mlp", "l3m", row("b23"))

        @block.tensor
        def _(pe):
            pe_cond(pe)
            pe_l0(pe)
            pe_qkv(pe, "l1")
            pe_heads(pe, "l1")
            pe_heads_out(pe, "l1")
            pe_l2(pe)
            pe_mlp(pe, "l2", "l2_mlp")
            pe_qkv(pe, "l3")
            pe_heads(pe, "l3")
            pe_heads_out(pe, "l3")
            pe_mlp(pe, "l3", "l3_mlp")


def kernel(**inputs):
    import concourse.bacc as bacc
    from concourse.bass_utils import run_bass_kernel_spmd

    a = {k: np.asarray(x) for k, x in inputs.items()}

    def l(n, name):
        return a[f"L{n}_cond_{name}"]

    def pairs(w):
        return w.reshape(w.shape[:-1] + (D // 2, 2))[..., ::-1].reshape(w.shape)

    def halves(w):
        return np.concatenate([w[..., D:], w[..., :D]], axis=-1)

    def columns(x):
        return x.reshape(-1, P).T

    wqkv = l(1, "Wqkv").reshape(H, HD, 3, D).transpose(2, 3, 0, 1).reshape(3, D, D)
    bqkv = l(1, "bqkv").reshape(H, HD, 3).transpose(2, 0, 1).reshape(3, D)
    zero = np.zeros(D, np.float32)
    mod_b = [l(0, "emb_b"), l(1, "bg"), l(1, "bb"), halves(l(3, "ada1_b")), halves(l(3, "ada2_b")),
             l(2, "film1_b"), l(2, "film2_b")]
    gains = [l(0, "sn_g"), l(1, "ln_g"), l(3, "ln1_g"), l(3, "ln2_g"), l(2, "norm1_w"), l(2, "norm2_w")]
    offsets = [l(0, "sn_b"), l(1, "ln_b"), l(3, "ln1_b"), l(3, "ln2_b"), zero, zero]
    cols = columns(np.concatenate(
        mod_b + gains + offsets + [l(0, "norm_g"), l(0, "norm_b"), l(0, "bk"), bqkv[0], bqkv[1],
                                   l(2, "q_b"), l(2, "k_b"), l(3, "bq"), l(3, "bk"),
                                   pairs(l(3, "bq")), pairs(l(3, "bk")), l(2, "mlp_b1"), l(3, "ff_b1")]))
    rows = np.stack([l(0, "bq"), l(0, "bv"), l(0, "out_b"), a["cond_1024"][0], a["cond_1024"][1],
                     bqkv[2], l(1, "bp"), l(1, "bg"), l(1, "bb"), l(1, "ln_g"), l(1, "ln_b"),
                     l(2, "v_b"), l(2, "proj_b"), l(2, "mlp_b2"), l(3, "bv"), l(3, "bo"), l(3, "ff_b2")])
    cond_w = np.concatenate([l(0, "emb_W"), l(1, "Wg").T, l(1, "Wb").T, halves(l(3, "ada1_w")),
                             halves(l(3, "ada2_w")), l(2, "film1_w"), l(2, "film2_w")], axis=1)
    rot = HD // 2
    inv = (1.0 / np.float32(10000.0) ** (np.arange(rot, dtype=np.float32) / np.float32(rot))).astype(np.float32)
    freq = np.arange(T, dtype=np.float32)[None, :] * inv[:, None]
    chan = np.arange(P) % HD
    sign = np.where(chan % 2 == 0, -1.0, 1.0).astype(np.float32)
    tables = np.stack([np.cos(freq)[chan // 2], np.sin(freq)[chan // 2] * sign[:, None]])
    block = np.arange(P) // HD

    arrays = {
        "x": a["x"],
        "mask": a["mask_BxS_bf1"].view(np.uint8),
        "cols": cols,
        "rows": rows,
        "condT": a["cond_1024"].T.reshape(CC, P, B).transpose(1, 0, 2),
        "cond_w": cond_w,
        "w_l0": np.stack([l(0, "Wq"), l(0, "Wk"), l(0, "Wv"), l(0, "out_W")]),
        "w_l1": np.concatenate([wqkv, l(1, "Wp").T[None]]),
        "w_l2": np.stack([l(2, "q_w"), l(2, "k_w"), l(2, "v_w"), l(2, "proj_w")]),
        "w_l3": np.stack([l(3, "wq"), l(3, "wk"), l(3, "wv"), l(3, "wo"), pairs(l(3, "wq")), pairs(l(3, "wk"))]),
        "w_m2a": l(2, "mlp_w1"), "w_m2b": l(2, "mlp_w2"), "w_m3a": l(3, "ff_w1"), "w_m3b": l(3, "ff_w2"),
        "rope": tables.astype(np.float32),
        "ident": np.eye(P, dtype=np.float32),
        "zeros": np.zeros((1, T // 2), np.float32),
        "bdmask": (block[:, None] == block[None, :]).astype(np.float32),
    }
    arrays = {f"in_{k}": np.ascontiguousarray(x) for k, x in arrays.items()}
    nc = bacc.Bacc("TRN2", target_bir_lowering=False, num_devices=1)
    ins = {k[3:]: nc.dram_tensor(k, x.shape, mybir.dt.from_np(x.dtype), kind="ExternalInput").ap()
           for k, x in arrays.items()}
    out = nc.dram_tensor("out_0", (B, T, D), F32, kind="ExternalOutput").ap()
    build(nc, ins, out)
    r = run_bass_kernel_spmd(nc, [arrays], core_ids=[0])
    return r.results[0]["out_0"]
```

```python
from contextlib import ExitStack

import numpy as np

import concourse.bass as bass
from concourse import mybir

F32 = mybir.dt.float32
F32R = mybir.dt.float32r
BF16 = mybir.dt.bfloat16
U8 = mybir.dt.uint8
ACT = mybir.ActivationFunctionType
ALU = mybir.AluOpType
AX = mybir.AxisListType

P = 128
B = 2
T = 1024
D = 256
H = 16
HD = D // H
NH = B * H
CC = D // P
NT = B * T // P
TT = T // P
CW = 512
NC = B * T // CW
CT = CW // P
CPB = T // CW
FF = 4 * D
FC = FF // P
PARTS = 3
Q_PARTS = (0, 0, 0, 1, 1, 2)
K_PARTS = (0, 1, 2, 0, 1, 0)
ROW_MASK = HD * len(Q_PARTS)
ROW_MAX = ROW_MASK + 1
MAX_ROWS = ROW_MASK + 1
EXP_ROWS = ROW_MASK + 3
LDS = 4

SITES = ("l0_out", "l1", "l3_attn", "l3_mlp", "l2_attn", "l2_mlp")
AB = {n: i for i, n in enumerate(SITES)}
AB["l0_in"] = len(SITES)
SPLIT_SITES = ("l0_in", "l1", "l2_attn", "l2_mlp", "l3_mlp")
NS = len(SITES)

COLS = ["emb_b", "sln_b", "ada1_b", "ada2_b", "film1_b", "film2_b"]
COL_MOD = 0
COL_G = 4 * NS
COL_B = COL_G + 2 * NS
COL_L0G, COL_L0B, COL_BK0 = (COL_B + 2 * NS + 2 * i for i in range(3))
COL_L1 = COL_BK0 + 2
COL_L2 = COL_L1 + 4
COL_L3 = COL_L2 + 4
COL_L3S = COL_L3 + 4
COL_M2 = COL_L3S + 4
COL_M3 = COL_M2 + FC
NCOL = COL_M3 + FC

ROWS = ["bq0", "bv0", "ob0", "gate0", "gate1", "bv1", "bp1", "bg1", "bb1", "lng1", "lnb1",
        "bv2", "bp2", "b22", "bv3", "bo3", "b23"]
ROW = {n: i for i, n in enumerate(ROWS)}
EARLY_ROWS = 5


def build(nc, ins, out):
    ctx = ExitStack()
    with ctx:
        def sb(name, shape, dt=F32):
            return ctx.enter_context(nc.sbuf_tensor(name, shape, dt))

        def sb_r(name, shape):
            base = nc.sbuf_base
            return sb(name, shape), nc.alloc_sbuf_tensor_at(name + "_r", shape, F32R, offset=base)

        class Sems(dict):
            def __missing__(self, name):
                self[name] = ctx.enter_context(nc.semaphore(name))
                return self[name]

        S = Sems()

        MLP = {"l2": "l2m", "l3": "l3m"}
        NORMS = ("l0_in", "l0_out", "l1", "l1_post", "l2_attn", "l2_mlp", "l3_attn", "l3_mlp")
        ADDS = ("l0", "l1a", "l2a", "l2m", "l3a", "l3m")
        HEADED = ("l1", "l3")
        NQK = 2 * CC * NC
        TURNED = tuple(n for n in NORMS if n != "l1_post")
        COUNTS = {
            "h_low": (SPLIT_SITES, 2 * NC), "gelu_low": (("l2", "l3"), FC * NC), "mlp_w_high": (("l2", "l3"), 2),
            "xh": (NORMS, NC), "transposed": (TURNED, 2 * NC), "h": (TURNED, 2 * NC),
            "pre": (ADDS, NC), "out": (ADDS, 2 * NC), "x": (ADDS, 2 * NC),
            "hid": (("l2", "l3"), FC * NC), "gelu": (("l2", "l3"), FC * NC),
            "v": (HEADED, 2 * NC), "vp": (HEADED, 2 * NC),
            "max_used": (HEADED, 2 * TT * NH), "max_scores": (HEADED, 2 * TT * NH),
            "exp": (HEADED, TT * NH), "scores": (HEADED, TT * NH), "values": (HEADED, TT * NH),
            "sums": (HEADED, 16 * B), "sums_inv": (HEADED, B), "sums_back": (HEADED, 16 * B),
            "sums_raw": (HEADED, B), "on": (HEADED, NC), "ones": (HEADED, 1), "rot": (("l3",), NQK),
        }
        for n in ("qkp", "qk_used", "r1", "part0", "part1", "part2"):
            COUNTS[n] = (HEADED, NQK)
        for n in ("out_used", "max_turned", "max_split", "max_copied", "max_min", "max_hi"):
            COUNTS[n] = (HEADED, NH)
        for i in range(LDS):
            COUNTS[f"pqk_{i}"] = (HEADED, 16 * (NQK // 4))
            COUNTS[f"max_row_{i}"] = (HEADED, 16 * (NH // LDS))
            COUNTS[f"stack_{i}"] = (HEADED, 16 * 6 * (NH // LDS))
        for i in range(2):
            COUNTS[f"head_v_{i}"] = (HEADED, 16 * (NH // 2))
            COUNTS[f"stored_{i}"] = (HEADED, 16 * (NH // 2))
            COUNTS[f"heads_out_{i}"] = (HEADED, 64 * (NC // 2))

        def at(name, stage, value):
            stages, per_stage = COUNTS[name]
            return S[name], value + stages.index(stage) * per_stage

        X = sb("X", [P, NT, D])
        hT, hT_r = sb_r("hT", [P, 2, 2, CC, CW])
        xh = sb("xh", [P, 2, CT, D])
        arena, arena_r = sb_r("arena", [P, 4 * NT * D])
        aux, aux_r = sb_r("aux", [P, NT * D])
        work, work_r = sb_r("work", [P, 4, CW])
        split, split_r = sb_r("split", [P, 4 * PARTS * CW // 2])
        wA, wA_r = sb_r("wA", [P, 4, CC, D])
        wB, wB_r = sb_r("wB", [P, 6, CC, D])
        wM, wM_r = sb_r("wM", [P, 8, CC * D])
        cols = sb("cols", [P, NCOL])
        rows = sb("rows", [P, len(ROWS), D])
        ident = sb("ident", [P, P])
        identb = sb("identb", [P, P], BF16)
        bdmask = sb("bdmask", [P, P])
        condT = sb("condT", [P, CC, B])
        scond = sb("scond", [P, CC, B])
        mods = sb("mods", [P, 4 * NS, B])
        modg = sb("modg", [P, NS, CC, B])
        ab = sb("ab", [P, NS + 1, 2, CC, B])
        abrow = sb("abrow", [P, B, 2, D])
        stats = sb("stats", [P, NT, 6])
        mv = sb("mv", [P, NT, 2])
        ve = sb("ve", [P, NT])
        rstd = sb("rstd", [P, NT])
        mhalf = sb("mhalf", [P, NT])
        nmx = sb("nmx", [P, 4, 16])
        mx = sb("mx", [P, 4, 8])
        zeros8 = sb("zeros8", [P, 8])
        msplit = sb("msplit", [P, 4, 16], BF16)
        mrow = sb("mrow", [16, 4, P], BF16)
        nm2 = sb("nm2", [P, NT])
        sum2 = sb("sum2", [P, NT])
        rinv2 = sb("rinv2", [P, NT])
        Vc = sb("Vc", [P, 2, 2 * HD, TT])
        OE = sb("OE", [P, 2, 256])
        k_nmax = sb("k_nmax", [P, CC * B])
        k_sum = sb("k_sum", [P, CC * B])

        Q4 = NT * D
        condW = (wM[:, :, :].rearrange("p a b -> p (a b)").rearrange("p (k n) -> p k n", k=CC),
                 aux[:, 0:CC * 4 * D].rearrange("p (k n) -> p k n", k=CC))
        condBC = arena[:, 3 * Q4:3 * Q4 + CC * B * P].rearrange("p (k b m) -> p k b m", k=CC, b=B)
        maskf = arena[:, 3 * Q4 + 1024:3 * Q4 + 2048]
        masku = arena[:, 3 * Q4 + 2048:3 * Q4 + 2304].bitcast(U8)
        maskb = arena[:, 3 * Q4 + 2304:3 * Q4 + 2816].bitcast(BF16)
        kTs = arena[:, 0:Q4].rearrange("p (m t) -> p m t", m=CC)
        q_sb = arena[:, Q4:2 * Q4].rearrange("p (n d) -> p n d", d=D)
        v_sb = arena[:, 2 * Q4:3 * Q4].rearrange("p (n d) -> p n d", d=D)
        ekt = arena[:, 3 * Q4:].rearrange("p (n d) -> p n d", d=D)
        qTs = aux[:, :].rearrange("p (m t) -> p m t", m=CC)
        ctx_sb = work[:, 0, :].rearrange("p (b m d) -> p b m d", b=B, m=CC)
        wo_g = work[:, 2:4, :].rearrange("p b (k d) -> p b k d", k=CC)
        gbias = split[:, 0:B * D].rearrange("p (b d) -> p b d", b=B)
        q_red = split[:, B * D:B * D + NT * 2 * H].rearrange("p (n s h) -> p n s h", n=NT, s=2)
        parts = split[:, :].bitcast(BF16).rearrange("p (s i t) -> p s i t", s=4, i=PARTS)
        rope = wA[:, :, :, :].rearrange("p w k n -> p (w k n)").rearrange("p (a t) -> p a t", a=2)
        QS = arena[:, 0:Q4 // 2].bitcast(BF16).rearrange("p (s t) -> p s t", s=LDS)
        KS = arena[:, Q4 // 2:Q4].bitcast(BF16).rearrange("p (s t) -> p s t", s=LDS)
        PT = arena[:, Q4:2 * Q4].rearrange("p (s t) -> p s t", s=4)
        Vh = arena[:, 2 * Q4:3 * Q4].rearrange("p (i d k) -> p i d k", i=NH, d=HD)
        OTn = aux[:, 0:2 * CC * CW].rearrange("p (s m t) -> p s m t", s=2, m=CC)
        RT = aux[:, 2 * CC * CW:].rearrange("p (s m t) -> p s m t", s=2, m=CC)
        Rs = arena[:, 3 * Q4:3 * Q4 + B * P].rearrange("p (b t) -> p b t", b=B)
        QT2 = arena[:, 0:Q4].rearrange("p (m t) -> p m t", m=CC)
        KT2 = arena[:, Q4:2 * Q4].rearrange("p (m t) -> p m t", m=CC)
        V2 = arena[:, 2 * Q4:3 * Q4].rearrange("p (n d) -> p n d", d=D)
        PT4 = arena[:, 3 * Q4:].rearrange("p (k q) -> p k q", k=TT)
        P2 = work[:, :, :].rearrange("p (s h) t -> p s (h t)", s=2)
        G = arena[:, :].rearrange("p (s l f t) -> p s l f t", s=2, l=2, f=FC)
        G_r = arena_r[:, :].rearrange("p (s l f t) -> p s l f t", s=2, l=2, f=FC)
        wM1_r = wM_r[:, 0:4, :].rearrange("p a b -> p (a b)").rearrange("p (k n) -> p k n", k=CC)
        wM2_r = wM_r[:, 4:8, :].rearrange("p a b -> p (a b)").rearrange("p (f d) -> p f d", f=FC)
        wM1_high = {"l2": aux_r[:, 2 * CC * CW:].rearrange("p (k n) -> p k n", k=CC),
                    "l3": work_r[:, :, :].rearrange("p a b -> p (a b)").rearrange("p (k n) -> p k n", k=CC)}
        wM2_high = split_r[:, 0:FC * D].rearrange("p (f d) -> p f d", f=FC)
        QKV_W = 3 * CC * D
        w_high = {"l0": split_r[:, 2 * B * D:2 * B * D + QKV_W].rearrange("p (w k n) -> p w k n", w=3, k=CC),
                  "l1": wM_r[:, :, :].rearrange("p a b -> p (a b)")[:, 0:QKV_W].rearrange("p (w k n) -> p w k n", w=3, k=CC),
                  "l2": split_r[:, 0:QKV_W].rearrange("p (w k n) -> p w k n", w=3, k=CC)}
        w_low = {"l0": wA_r, "l1": wB_r, "l2": wA_r}
        wM1 = wM[:, 0:4, :].rearrange("p a b -> p (a b)").rearrange("p (k n) -> p k n", k=CC)
        wM2 = wM[:, 4:8, :].rearrange("p a b -> p (a b)").rearrange("p (f d) -> p f d", f=FC)

        PQK = nc.dram_tensor("pqk", (2, NH, HD, PARTS, T), BF16, kind="Internal").ap()
        OD = nc.dram_tensor("od", (NH, 2 * HD, T), F32, kind="Internal").ap()
        RD = nc.dram_tensor("rd", (NH, T), F32, kind="Internal").ap()
        MD = nc.dram_tensor("md", (NH, T), BF16, kind="Internal").ap()

        PS = ctx.enter_context(nc.psum_tensor("PS", [P, 8, CW], F32))

        def bank(i):
            return PS[:, i, :]

        def bank2(i):
            return PS[:, i:i + 2, :].rearrange("p a b -> p (a b)")

        def banks2t(i):
            return PS[:, i, :].rearrange("p (t d) -> p t d", t=2)

        ready = {
            "l0_in": lambda e, c: e.wait_ge(S[f"x_{c}"], 16),
            "l0_out": lambda e, c: e.wait_ge(S["l0_y"], 2 * c + 2),
            "l1": lambda e, c: e.wait_ge(*at("x", "l0", 2 * c + 2)),
            "l1_post": lambda e, c: e.wait_ge(*at("x", "l1a", 2 * c + 2)),
            "l2_attn": lambda e, c: e.wait_ge(S["x_l1"], c + 1),
            "l2_mlp": lambda e, c: e.wait_ge(*at("x", "l2a", 2 * c + 2)),
            "l3_attn": lambda e, c: e.wait_ge(*at("x", "l2m", 2 * c + 2)),
            "l3_mlp": lambda e, c: e.wait_ge(*at("x", "l3a", 2 * c + 2)),
        }
        ORDER = ["l0_in", "l0_out", "l1", "l1_post", "l2_attn", "l2_mlp", "l3_attn", "l3_mlp"]
        RMS = {"l2_attn": True, "l2_mlp": True}

        def norm_stats(dve, site, src, c):
            ready[site](dve, c)
            for k in range(CT):
                n = CT * c + k
                nc.vector.bn_stats(stats[:, n, :], src[:, n, :]).then_inc(S["stats"], 1)
            done = NT * ORDER.index(site) + CT * (c + 1)
            dve.wait_ge(S["stats"], done)
            for k in range(CT):
                n = CT * c + k
                last = nc.vector.bn_aggr(mv[:, n, :], stats[:, n, :])
            last.then_inc(S["moments"], 1)
            if site in RMS:
                sl = slice(CT * c, CT * c + CT)
                dve.wait_ge(S["moments"], NC * ORDER.index(site) + c + 1)
                nc.vector.tensor_tensor(ve[:, sl], mv[:, sl, 0], mv[:, sl, 0], ALU.mult).then_inc(S["msq"], 1)
                r = 2 * (NC * (site == "l2_mlp") + c)
                dve.wait_ge(S["msq"], r + 1)
                nc.vector.tensor_tensor(mv[:, sl, 1], mv[:, sl, 1], ve[:, sl], ALU.add).then_inc(S["msq"], 1)

        def norm_rstd(pool, site, c):
            k = NC * ORDER.index(site) + c
            sl = slice(CT * c, CT * c + CT)
            if site in RMS:
                pool.wait_ge(S["msq"], 2 * (NC * (site == "l2_mlp") + c) + 2)
            else:
                pool.wait_ge(S["moments"], k + 1)
            nc.gpsimd.tensor_scalar(ve[:, sl], mv[:, sl, 1], 1e-6 if site in RMS else 1e-5, None,
                                    ALU.add).then_inc(S["var_eps"], 1)
            pool.wait_ge(S["var_eps"], k + 1)
            nc.gpsimd.tensor_tensor(rstd[:, sl], ve[:, sl], mhalf[:, sl], ALU.pow).then_inc(S["rstd"], 1)

        def norm_apply(dve, site, src, c):
            i = NC * ORDER.index(site) + c
            dve.wait_ge(S["rstd"], i + 1)
            if site == "l1_post" and c >= 2:
                dve.wait_ge(S["x_l1"], c - 1)
            elif c >= 2:
                dve.wait_ge(*at("transposed", site, 2 * (c - 1)))
            for k in range(CT):
                n = CT * c + k
                if site in RMS:
                    last = nc.vector.tensor_scalar(xh[:, c % 2, k, :], src[:, n, :], rstd[:, n:n + 1],
                                                   None, ALU.mult)
                else:
                    last = nc.vector.tensor_scalar(xh[:, c % 2, k, :], src[:, n, :], mv[:, n, 0:1],
                                                   rstd[:, n:n + 1], ALU.subtract, ALU.mult)
            last.then_inc(S["xh"], 1)

        def norm_ahead(dve, site, src, c, lag=1):
            norm_stats(dve, site, src, c)
            if 0 <= c - lag < 2:
                norm_apply(dve, site, src, c - lag)

        def norm_rest(dve, site, src, c):
            if 2 <= c < NC:
                norm_apply(dve, site, src, c)

        def norm_transpose(pe, site, c):
            pe.wait_ge(*at("xh", site, c + 1))
            for m in range(CC):
                if c:
                    pe.wait_ge(*at("h", site, 2 * (c - 1) + m + 1))
                for k in range(CT):
                    last = nc.tensor.transpose(PS[:, m, k * P:(k + 1) * P],
                                               xh[:, c % 2, k, m * P:(m + 1) * P], ident[:, :])
                last.then_inc(S["transposed"], 1)

        def norm_modulate(act, site, c, func=ACT.Identity):
            b = c // CPB
            i = AB[site]
            for m in range(CC):
                act.wait_ge(*at("transposed", site, 2 * c + m + 1))
                dst = [hT[:, c % 2, 1, m, :]]
                if site in SPLIT_SITES:
                    dst.append(hT_r[:, c % 2, 0, m, :])
                for d in dst:
                    last = nc.scalar.activation(d, bank(m), func, bias=ab[:, i, 1, m, b:b + 1],
                                                scale=ab[:, i, 0, m, b:b + 1])
                last.then_inc(S["h"], 1)

        def norm_low(pool, site, c):
            for m in range(CC):
                pool.wait_ge(*at("h", site, 2 * c + m + 1))
                nc.gpsimd.tensor_tensor(hT_r[:, c % 2, 1, m, :], hT[:, c % 2, 1, m, :],
                                        hT_r[:, c % 2, 0, m, :].bitcast(F32), ALU.subtract).then_inc(S["h_low"], 1)

        def h_ready(pe, site, c):
            pe.wait_ge(*at("h_low" if site in SPLIT_SITES else "h", site, 2 * c + 2))

        def h_chunk(site, m, c):
            if site in SPLIT_SITES:
                return [hT_r[:, c % 2, l, m, :] for l in range(2)]
            return [hT[:, c % 2, 1, m, :]]

        def h_tile(site, m, n):
            c, q = n // CT, n % CT
            return [x[:, q * P:(q + 1) * P] for x in h_chunk(site, m, c)]

        def product(out, lhs, rhs, start, stop):
            if len(lhs) == 1:
                return nc.tensor.matmul(out, lhs[0], rhs[0], start=start, stop=stop)
            nc.tensor.matmul(out, lhs[0], rhs[0], start=start, stop=False)
            nc.tensor.matmul(out, lhs[0], rhs[1], start=False, stop=False)
            return nc.tensor.matmul(out, lhs[1], rhs[0], start=False, stop=stop)

        def qkv_w(L, j, k, m=None):
            sl = slice(0, D) if m is None else slice(m * P, (m + 1) * P)
            return [w_high[L][:, j, k, sl], w_low[L][:, j, k, sl]]

        def split_weights(pool, raw, high, low, done):
            nc.gpsimd.tensor_copy(high, raw).then_inc(S["w_high"], 1)
            w_split[0] += 1
            pool.wait_ge(S["w_high"], w_split[0])
            nc.gpsimd.tensor_tensor(low, raw, high.bitcast(F32), ALU.subtract).then_inc(done, 1)

        w_split = [0]

        def add_rows(pool, site, row):
            for c in range(NC):
                add_row(pool, site, c, row)

        def add_row(pool, site, c, row):
            pool.wait_ge(*at("xh", site, c + 1))
            bias = row(c // CPB)
            nc.gpsimd.tensor_tensor(X[:, CT * c:CT * c + CT, :], X[:, CT * c:CT * c + CT, :],
                                    bias[:, None, :].to_broadcast([P, CT, D]),
                                    ALU.add).then_inc(S["pre"], 1)

        def norms(pool, site, row=None):
            for c in range(2):
                norm_rstd(pool, site, c)
            for c in range(NC):
                norm_low(pool, site, c)
                if c + 2 < NC:
                    norm_rstd(pool, site, c + 2)
                if row:
                    add_row(pool, site, c, row)

        def add_to_x(dve, name, c, b0):
            dve.wait_ge(*at("pre", name, c + 1))
            for p in range(2):
                n = CT * c + 2 * p
                dve.wait_ge(*at("out", name, 2 * c + p + 1))
                nc.vector.tensor_tensor(X[:, n:n + 2, :], banks2t(b0 + p), X[:, n:n + 2, :],
                                        ALU.add).then_inc(S["x"], 1)

        def project_tiles(pe, name, c, b0, lhs, w, wait_bank=True):
            nk = len(w)
            for p in range(2):
                if c and wait_bank:
                    pe.wait_ge(*at("x", name, 2 * (c - 1) + p + 1))
                for q in range(2):
                    for k in range(nk):
                        last = product(PS[:, b0 + p, q * D:(q + 1) * D], lhs(k, 2 * p + q), w[k],
                                       k == 0, k == nk - 1)
                last.then_inc(S["out"], 1)

        def sp_loads(sp):
            for c in range(NC):
                sp.dma_start(X[:, CT * c:CT * c + CT, :],
                             ins["x"].rearrange("b (n p) d -> p (b n) d", p=P)[:, CT * c:CT * c + CT, :]
                             ).then_inc(S[f"x_{c}"], 16)
            sp.dma_start(wA[:, 0:4], ins["w_l0"].rearrange("w (k p) n -> p w k n", p=P)).then_inc(S["w_l0"], 16)
            for part, w in enumerate(condW):
                sp.dma_start(w, ins["cond_w"].rearrange("(k p) n -> p k n", p=P)[:, :, part * 8 * D:part * 8 * D + w.shape[2]]
                             ).then_inc(S["w_cond"], 16)
            sp.dma_start(rows[:, EARLY_ROWS:, :], ins["rows"][EARLY_ROWS:].partition_broadcast(P)
                         ).then_inc(S["more_rows"], 16)
            sp.dma_start(masku[0:1], ins["mask"][0:1, :]).then_inc(S["mask_u8"], 16)
            sp.dma_start(masku[32:33], ins["mask"][1:2, :]).then_inc(S["mask_u8"], 16)
            sp.dma_start(wB[:, 0:4], ins["w_l1"].rearrange("w (k p) n -> p w k n", p=P)).then_inc(S["w_l1"], 16)
            sp.wait_ge(S["mask_bias"], 1)
            for b in range(B):
                sp.dma_start(MD[b * H:(b + 1) * H, :],
                             maskb[32 * b:32 * b + 1, None, :].to_broadcast([1, H, T])).then_inc(S["mask_dram"], 16)

        def sp_loads_later(sp):
            sp.wait_ge(*at("x", "l0", 2 * NC))
            sp.dma_start(wA[:, 0:4], ins["w_l2"].rearrange("w (k p) n -> p w k n", p=P)).then_inc(S["w_l2"], 16)
            sp.wait_ge(*at("vp", "l1", 2 * NC))
            sp.dma_start(wM1, ins["w_m2a"].rearrange("(k p) n -> p k n", p=P)).then_inc(S["w_m2"], 16)
            sp.dma_start(wM2, ins["w_m2b"].rearrange("(k p) n -> p k n", p=P)).then_inc(S["w_m2"], 16)

        def act_loads(act):
            act.dma_start(cols[:, :], ins["cols"]).then_inc(S["small"], 16)
            act.dma_start(condT[:, :, :], ins["condT"]).then_inc(S["small"], 16)
            act.dma_start(ident[:, :], ins["ident"]).then_inc(S["small"], 16)
            act.dma_start(bdmask[:, :], ins["bdmask"]).then_inc(S["small"], 16)
            act.dma_start(rows[:, 0:EARLY_ROWS, :], ins["rows"][0:EARLY_ROWS].partition_broadcast(P)
                          ).then_inc(S["rows"], 16)

        def pe_cond(pe):
            pe.wait_ge(S["w_cond"], 32)
            pe.wait_ge(S["l0_kT"], 2 * NC)
            pe.wait_ge(S["l0_qv"], 4 * NC)
            pe.wait_ge(S["small"], 64)
            pe.wait_ge(S["scond"], 1)
            pe.wait_ge(S["cond_bc"], 1)
            for b in range(B):
                for k in range(CC):
                    last = nc.tensor.matmul(bank(6 + b), condBC[:, k, b, :],
                                            condW[0][:, k, 2 * D:4 * D], start=(k == 0), stop=(k == CC - 1))
            last.then_inc(S["cond_rows"], 1)
            for i in range(4 * NS):
                c = scond if i < 4 else condT
                w, j = (condW[0], i) if i < 16 else (condW[1], i - 16)
                for k in range(CC):
                    last = nc.tensor.matmul(PS[:, 5, i * B:(i + 1) * B], w[:, k, j * P:(j + 1) * P],
                                            c[:, k, :], start=(k == 0), stop=(k == CC - 1))
            last.then_inc(S["cond_cols"], 1)

        def dve_cond(dve):
            nc.vector.memset(mhalf[:, :], -0.5)
            nc.vector.memset(zeros8[:, :], 0.0)
            nc.vector.memset(Vc[:, :, :, :], 1.0).then_inc(S["consts"], 1)

        def dve_small(dve):
            dve.wait_ge(S["small"], 64)
            nc.vector.tensor_copy(identb[:, :], ident[:, :]).then_inc(S["consts"], 1)
            nc.vector.tensor_copy(condBC, condT[:, :, :, None].to_broadcast([P, CC, B, P])).then_inc(S["cond_bc"], 1)
            nc.vector.tensor_copy(ab[:, NS, 0], cols[:, COL_L0G:COL_L0G + 2, None].to_broadcast([P, CC, B]))
            nc.vector.tensor_copy(ab[:, NS, 1], cols[:, COL_L0B:COL_L0B + 2, None].to_broadcast([P, CC, B])
                                  ).then_inc(S["ab_in"], 1)

        def dve_cond2(dve):
            dve.wait_ge(S["mask_u8"], 32)
            for q in (0, 32):
                nc.vector.tensor_scalar(maskf[q:q + 1, :], masku[q:q + 1, :], 1.0, 3e38, ALU.subtract,
                                        ALU.mult).then_inc(S["mask_f32"], 1)
            dve.wait_ge(S["mask_f32"], 2)
            for q in (0, 32):
                last = nc.vector.tensor_scalar(maskb[q:q + 1, :], maskf[q:q + 1, :], 10.0, None, ALU.mult)
            last.then_inc(S["mask_bias"], 1)
            dve.wait_ge(S["cond_cols"], 1)
            nc.vector.tensor_tensor(mods[:, :, :], PS[:, 5, 0:4 * NS * B].rearrange("p (i b) -> p i b", b=B),
                                    cols[:, 0:4 * NS, None].to_broadcast([P, 4 * NS, B]), ALU.add).then_inc(S["mod"], 1)
            dve.wait_ge(S["mod"], 1)
            m4 = mods[:, :, :].rearrange("p (s h c) b -> p s h c b", s=NS, h=2)
            nc.vector.tensor_scalar(modg[:, :], m4[:, :, 0], 1.0, None, ALU.add).then_inc(S["mod"], 1)
            dve.wait_ge(S["mod"], 2)
            nc.vector.tensor_copy(modg[:, 1], m4[:, 1, 0]).then_inc(S["mod"], 1)
            dve.wait_ge(S["mod"], 3)
            g = cols[:, COL_G:COL_G + 2 * NS].rearrange("p (s c) -> p s c", s=NS)
            bb = cols[:, COL_B:COL_B + 2 * NS].rearrange("p (s c) -> p s c", s=NS)
            for b in range(B):
                nc.vector.tensor_tensor(ab[:, 0:NS, 0, :, b], modg[:, :, :, b], g, ALU.mult)
                nc.vector.tensor_tensor(ab[:, 0:4, 1, :, b], modg[:, 0:4, :, b], bb[:, 0:4], ALU.mult).then_inc(S["mod"], 1)
            dve.wait_ge(S["mod"], 5)
            for b in range(B):
                nc.vector.tensor_tensor(ab[:, 0:4, 1, :, b], ab[:, 0:4, 1, :, b], m4[:, 0:4, 1, :, b], ALU.add)
                last = nc.vector.tensor_copy(ab[:, 4:6, 1, :, b], m4[:, 4:6, 1, :, b])
            last.then_inc(S["ab"], 1)
            dve.wait_ge(S["cond_rows"], 1)
            dve.wait_ge(S["more_rows"], 16)
            for b in range(B):
                r = rows[:, ROW["bg1"]:ROW["bb1"] + 1, :]
                nc.vector.tensor_tensor(abrow[:, b], banks2t(6 + b), r, ALU.add).then_inc(S["abrow"], 1)
                dve.wait_ge(S["abrow"], 3 * b + 1)
                nc.vector.tensor_tensor(xh[:, 1, b, :], abrow[:, b, 0], rows[:, ROW["lnb1"], :], ALU.mult).then_inc(S["abrow"], 1)
                dve.wait_ge(S["abrow"], 3 * b + 2)
                nc.vector.tensor_tensor(abrow[:, b, 0], abrow[:, b, 0], rows[:, ROW["lng1"], :], ALU.mult)
                nc.vector.tensor_tensor(abrow[:, b, 1], abrow[:, b, 1], xh[:, 1, b, :], ALU.add).then_inc(S["abrow"], 1)
            dve.wait_ge(S["w_l0"], 16)
            for b in range(B):
                gate = rows[:, ROW["gate0"] + b, :]
                nc.vector.tensor_tensor(gbias[:, b], rows[:, ROW["ob0"], :], gate, ALU.mult)
                last = nc.vector.tensor_tensor(wo_g[:, b], wA[:, 3], gate[:, None, :].to_broadcast([P, CC, D]), ALU.mult)
            last.then_inc(S["gated"], 1)

        def pe_l0(pe):
            pe.wait_ge(S["consts"], 2)
            for c in range(NC + 1):
                if c < NC:
                    norm_transpose(pe, "l0_in", c)
                if c == 0:
                    continue
                d = c - 1
                if d == 0:
                    pe.wait_ge(S["w_l0_low"], 1)
                h_ready(pe, "l0_in", d)
                for m in range(CC):
                    if d:
                        pe.wait_ge(S["l0_kT"], 2 * (d - 1) + m + 1)
                    for k in range(CC):
                        last = product(bank(4 + m), qkv_w("l0", 1, k, m), h_chunk("l0_in", k, d),
                                       k == 0, k == CC - 1)
                    last.then_inc(S["l0_kp"], 1)
                for p in range(2):
                    for j, w in ((0, 0), (1, 2)):
                        u = 2 * (2 * d + p) + j
                        if u >= 2:
                            pe.wait_ge(S["l0_qv"], u - 1)
                        for q in range(2):
                            for k in range(CC):
                                last = product(PS[:, 6 + j, q * D:(q + 1) * D],
                                               h_tile("l0_in", k, CT * d + 2 * p + q), qkv_w("l0", w, k),
                                               k == 0, k == CC - 1)
                        last.then_inc(S["l0_qvp"], 1)
            pe_cond(pe)
            for c in range(NC):
                pe.wait_ge(S["l0_qn"], 2 * c + 2)
                for m in range(CC):
                    pe.wait_ge(*at("h", "l0_in", 2 * NC)) if c == 0 else pe.wait_ge(S["l0_qT"], 2 * (c - 1) + m + 1)
                    for k in range(CT):
                        last = nc.tensor.transpose(PS[:, m, k * P:(k + 1) * P],
                                                   q_sb[:, CT * c + k, m * P:(m + 1) * P], ident[:, :])
                    last.then_inc(S["l0_qTp"], 1)
            for g in range(NT // 2):
                pe.wait_ge(S["l0_kexp"], 2 * (g // (TT // 2)) + 2)
                if g >= 2:
                    pe.wait_ge(S["l0_ekt"], g - 1)
                for q in range(2):
                    for m in range(CC):
                        n = 2 * g + q
                        last = nc.tensor.transpose(PS[:, 2 + g % 2, q * D + m * P:q * D + (m + 1) * P],
                                                   kTs[:, m, n * P:(n + 1) * P], ident[:, :])
                last.then_inc(S["l0_ektp"], 1)
            pe.wait_ge(S["l0_kT"], 2 * NC)
            pe.wait_ge(S["l0_ekt"], NT // 2)
            for b in range(B):
                for m in range(CC):
                    for k in range(TT):
                        n = TT * b + k
                        last = nc.tensor.matmul(PS[:, 4, (CC * b + m) * P:(CC * b + m + 1) * P],
                                                ekt[:, n, m * P:(m + 1) * P], v_sb[:, n, m * P:(m + 1) * P],
                                                start=(k == 0), stop=(k == TT - 1))
            last.then_inc(S["l0_ctxp"], 1)
            pe.wait_ge(S["l0_ctx"], 4)
            pe.wait_ge(S["abrow"], 6)
            pe.wait_ge(S["l0_qT"], 2 * NC)
            pe.wait_ge(S["l0_qv"], 4 * NC)
            for g in range(NT // 2):
                if g >= 2:
                    pe.wait_ge(S["l0_y"], g - 1)
                for q in range(2):
                    n = 2 * g + q
                    for m in range(CC):
                        last = nc.tensor.matmul(PS[:, 6 + g % 2, q * D + m * P:q * D + (m + 1) * P],
                                                qTs[:, m, n * P:(n + 1) * P], ctx_sb[:, n // TT, m, :],
                                                start=True, stop=True)
                last.then_inc(S["l0_yp"], 1)
            for c in range(NC + 1):
                if c < NC:
                    norm_transpose(pe, "l0_out", c)
                if c:
                    d = c - 1
                    h_ready(pe, "l0_out", d)
                    if d == 0:
                        pe.wait_ge(S["gated"], 1)
                    project_tiles(pe, "l0", d, 2, lambda k, q: h_tile("l0_out", k, CT * d + q),
                                  [[wo_g[:, d // CPB, k, :]] for k in range(CC)])

        def act_l0(act):
            act.wait_ge(S["w_l0"], 16)
            nc.scalar.copy(w_high["l0"], wA[:, 0:3]).then_inc(S["w_l0_high"], 1)
            act.wait_ge(S["ab_in"], 1)
            for c in range(NC + 1):
                if c < NC:
                    norm_modulate(act, "l0_in", c)
                if c:
                    d = c - 1
                    for m in range(CC):
                        act.wait_ge(S["l0_kp"], 2 * d + m + 1)
                        nc.scalar.activation(kTs[:, m, d * CW:(d + 1) * CW], bank(4 + m), ACT.Identity,
                                             bias=cols[:, COL_BK0 + m:COL_BK0 + m + 1]).then_inc(S["l0_kT"], 1)
            for g in range(NT // 2):
                act.wait_ge(S["l0_qsub"], g + 1)
                nc.scalar.activation(q_sb[:, 2 * g:2 * g + 2, :], q_sb[:, 2 * g:2 * g + 2, :],
                                     ACT.Exp).then_inc(S["l0_qexp"], 1)
            for b in range(B):
                for m in range(CC):
                    i = CC * b + m
                    act.wait_ge(S["l0_kmax"], i + 1)
                    kk = kTs[:, m, b * T:(b + 1) * T]
                    nc.scalar.activation(kk, kk, ACT.Exp, bias=k_nmax[:, i:i + 1],
                                         accum_out=k_sum[:, i:i + 1]).then_inc(S["l0_kexp"], 1)
            for c in range(NC):
                for m in range(CC):
                    act.wait_ge(S["l0_qTp"], 2 * c + m + 1)
                    nc.scalar.copy(qTs[:, m, c * CW:(c + 1) * CW], bank(m)).then_inc(S["l0_qT"], 1)
            for g in range(NT // 2):
                act.wait_ge(S["l0_yp"], g + 1)
                nc.scalar.copy(q_sb[:, 2 * g:2 * g + 2, :], banks2t(6 + g % 2)).then_inc(S["l0_y"], 1)
            act.wait_ge(S["ab"], 1)
            for c in range(NC):
                norm_modulate(act, "l0_out", c, ACT.Silu)

        def q_heads(g):
            return q_sb[:, 2 * g:2 * g + 2, :].rearrange("p n (h d) -> p n h d", h=H)

        def dve_l0(dve):
            dve_cond(dve)
            for c in range(NC + 2):
                if c < NC:
                    norm_stats(dve, "l0_in", X, c)
                if c == 0:
                    dve_small(dve)
                if 1 <= c <= NC:
                    norm_apply(dve, "l0_in", X, c - 1)
                if c == 1:
                    dve.wait_ge(S["w_l0_high"], 1)
                    nc.vector.tensor_tensor(wA_r[:, 0:3], wA[:, 0:3], w_high["l0"].bitcast(F32),
                                            ALU.subtract).then_inc(S["w_l0_low"], 1)
                if c < 2:
                    continue
                d = c - 2
                if d == 0:
                    dve.wait_ge(S["rows"], 16)
                for p in range(2):
                    g = 2 * d + p
                    for j, (dst, r) in enumerate(((q_sb, "bq0"), (v_sb, "bv0"))):
                        dve.wait_ge(S["l0_qvp"], 2 * g + j + 1)
                        nc.vector.tensor_tensor(dst[:, 2 * g:2 * g + 2, :], banks2t(6 + j),
                                                rows[:, ROW[r], None, :].to_broadcast([P, 2, D]),
                                                ALU.add).then_inc(S["l0_qv"], 1)
                    dve.wait_ge(S["l0_qv"], 2 * g + 1)
                    nc.vector.tensor_reduce(q_red[:, 2 * g:2 * g + 2, 0, :], q_heads(g), AX.X,
                                            ALU.max).then_inc(S["l0_qmax"], 1)
            for b in range(B):
                for m in range(CC):
                    i = CC * b + m
                    dve.wait_ge(S["l0_kT"], 2 * (CPB * b + CPB - 1) + m + 1)
                    nc.vector.tensor_reduce(k_nmax[:, i:i + 1], kTs[:, m, b * T:(b + 1) * T], AX.X, ALU.max,
                                            negate=True).then_inc(S["l0_kmax"], 1)
            for g in range(NT // 2):
                sl = q_red[:, 2 * g:2 * g + 2, 1, :]
                dve.wait_ge(S["l0_qexp"], g + 1)
                nc.vector.tensor_reduce(sl, q_heads(g), AX.X, ALU.add).then_inc(S["l0_qsum"], 1)
                dve.wait_ge(S["l0_qsum"], g + 1)
                nc.vector.reciprocal(sl, sl).then_inc(S["l0_qinv"], 1)
            dve_cond2(dve)
            dve.wait_ge(S["mask_dram"], 32)
            for g in range(NT // 2):
                dve.wait_ge(S["l0_ektp"], g + 1)
                nc.vector.tensor_copy(ekt[:, 2 * g:2 * g + 2, :], banks2t(2 + g % 2)).then_inc(S["l0_ekt"], 1)
            dve.wait_ge(S["l0_kexp"], B * CC)
            nc.vector.reciprocal(k_sum[:, :], k_sum[:, :]).then_inc(S["l0_kinv"], 1)
            dve.wait_ge(S["l0_kinv"], 1)
            dve.wait_ge(S["l0_ctxp"], 1)
            for b in range(B):
                for m in range(CC):
                    i = CC * b + m
                    nc.vector.scalar_tensor_tensor(ctx_sb[:, b, m, :], PS[:, 4, i * P:(i + 1) * P],
                                                   k_sum[:, i:i + 1], bdmask[:, :], ALU.mult,
                                                   ALU.mult).then_inc(S["l0_ctx"], 1)
            for c in range(NC + 3):
                if c < NC:
                    norm_stats(dve, "l0_out", q_sb, c)
                if 1 <= c <= NC:
                    norm_apply(dve, "l0_out", q_sb, c - 1)
                if c >= 3:
                    add_to_x(dve, "l0", c - 3, 2)
                    norm_ahead(dve, "l1", X, c - 3)

        def pool_l0(pool):
            pool.wait_ge(S["consts"], 1)
            norms(pool, "l0_in")
            for g in range(NT // 2):
                pool.wait_ge(S["l0_qmax"], g + 1)
                nc.gpsimd.tensor_tensor(q_heads(g), q_heads(g),
                                        q_red[:, 2 * g:2 * g + 2, 0, :, None].to_broadcast([P, 2, H, HD]),
                                        ALU.subtract).then_inc(S["l0_qsub"], 1)
            for g in range(NT // 2):
                pool.wait_ge(S["l0_qinv"], g + 1)
                nc.gpsimd.tensor_tensor(q_heads(g), q_heads(g),
                                        q_red[:, 2 * g:2 * g + 2, 1, :, None].to_broadcast([P, 2, H, HD]),
                                        ALU.mult).then_inc(S["l0_qn"], 1)
            pool.wait_ge(S["cond_cols"], 1)
            pool.wait_ge(S["cond_rows"], 1)
            pool.wait_ge(S["w_l1"], 16)
            split_weights(pool, wB[:, 0:3], w_high["l1"], wB_r[:, 0:3], S["w_l1_low"])
            pool.wait_ge(S["gated"], 1)
            add_rows(pool, "l0_in", lambda b: gbias[:, b, :])
            for c in range(NC):
                norm_rstd(pool, "l0_out", c)

        HEADS = {
            "l1": dict(w=wB, col=COL_L1, bv="bv1", scale=1.0, rope=False, loads=6, rsum=1.0 / 16.0),
            "l3": dict(w=wB, col=COL_L3, bv="bv3", scale=HD ** -0.5, rope=True, loads=7, rsum=1.0),
        }
        SITE = {"l1": "l1", "l3": "l3_attn"}
        LAYER = {"l1": 0, "l3": 1}

        def pe_qkv(pe, L):
            w, rot = HEADS[L]["w"], HEADS[L]["rope"]
            if L == "l1":
                pe.wait_ge(S["w_l1_low"], 1)
            pe.wait_ge(S["w_" + L], 16)

            def weights(j, k, m=None):
                if L == "l1":
                    return qkv_w(L, j, k, m)
                return [w[:, j, k, :] if m is None else w[:, j, k, m * P:(m + 1) * P]]

            for c in range(NC + 1):
                if c < NC:
                    norm_transpose(pe, SITE[L], c)
                if c == 0:
                    continue
                d = c - 1
                h_ready(pe, SITE[L], d)
                if d == 0 and L == "l1":
                    pe.wait_ge(S["l0_y"], NT // 2)
                    pe.wait_ge(*at("x", "l0", 2 * NC))
                if d == 0 and L == "l3":
                    pe.wait_ge(*at("x", "l2m", 2 * NC))
                    pe.wait_ge(*at("gelu", "l2", FC * NC))
                for j in range(2 * CC):
                    i = 2 * CC * d + j
                    b0 = 4 + 2 * (i % 2)
                    if i >= 2:
                        pe.wait_ge(*at("qk_used", L, i - 1))
                    for k in range(CC):
                        last = product(bank(b0), weights(j // 2, k, j % 2), h_chunk(SITE[L], k, d),
                                       k == 0, k == CC - 1)
                    if rot:
                        for k in range(CC):
                            last = product(bank(b0 + 1), weights(4 + j // 2, k, j % 2), h_chunk(SITE[L], k, d),
                                           k == 0, k == CC - 1)
                    last.then_inc(S["qkp"], 1)
                for p in range(2):
                    if d:
                        pe.wait_ge(*at("v", L, 2 * (d - 1) + p + 1))
                    for q in range(2):
                        for k in range(CC):
                            last = product(PS[:, 2 + p, q * D:(q + 1) * D],
                                           h_tile(SITE[L], k, CT * d + 2 * p + q), weights(2, k),
                                           k == 0, k == CC - 1)
                    last.then_inc(S["vp"], 1)

        def act_split(act, L, i, stage):
            if stage == 0:
                if not HEADS[L]["rope"]:
                    act.wait_ge(*at("qkp", L, i + 1))
                    if i >= 2:
                        act.wait_ge(*at("r1", L, i - 1))
                    col = HEADS[L]["col"] + i % (2 * CC)
                    nc.scalar.activation(work[:, i % 2, :], bank(4 + 2 * (i % 2)), ACT.Identity,
                                         bias=cols[:, col:col + 1]).then_inc(S["qk_used"], 1)
                    act.wait_ge(*at("qk_used", L, i + 1))
                else:
                    act.wait_ge(*at("rot", L, i + 1))
                if i >= 4:
                    act.wait_ge(*at(f"pqk_{i % 4}", L, 16 * (i // 4)))
                nc.scalar.copy(parts[:, i % 4, 0, :], work[:, i % 2, :]).then_inc(S["part0"], 1)
            else:
                act.wait_ge(*at("r1", L, i + 1))
                nc.scalar.copy(parts[:, i % 4, 1, :], work[:, 2 + i % 2, :]).then_inc(S["part1"], 1)

        def dve_split(dve, L, i, stage):
            if stage == 0:
                if HEADS[L]["rope"]:
                    j, c = i % (2 * CC), i // (2 * CC)
                    t0 = (c % CPB) * CW
                    if i == 0:
                        dve.wait_ge(S["rope"], 16)
                    dve.wait_ge(*at("qkp", L, i + 1))
                    if i >= 2:
                        dve.wait_ge(*at("part2", L, i - 1))
                    nc.vector.scalar_tensor_tensor(work[:, i % 2, :], bank(4 + 2 * (i % 2)),
                                                   cols[:, COL_L3 + j:COL_L3 + j + 1],
                                                   rope[:, 0, t0:t0 + CW], ALU.add, ALU.mult)
                    nc.vector.scalar_tensor_tensor(work[:, 2 + i % 2, :], bank(5 + 2 * (i % 2)),
                                                   cols[:, COL_L3S + j:COL_L3S + j + 1],
                                                   rope[:, 1, t0:t0 + CW], ALU.add,
                                                   ALU.mult).then_inc(S["qk_used"], 1)
                    dve.wait_ge(*at("qk_used", L, i + 1))
                    nc.vector.tensor_tensor(work[:, i % 2, :], work[:, i % 2, :], work[:, 2 + i % 2, :],
                                            ALU.add).then_inc(S["rot"], 1)
            elif stage == 1:
                dve.wait_ge(*at("part0", L, i + 1))
                if i >= 2:
                    dve.wait_ge(*at("part2", L, i - 1))
                nc.vector.tensor_tensor(work[:, 2 + i % 2, :], work[:, i % 2, :], parts[:, i % 4, 0, :],
                                        ALU.subtract).then_inc(S["r1"], 1)
            else:
                dve.wait_ge(*at("part1", L, i + 1))
                nc.vector.tensor_tensor(parts[:, i % 4, 2, :], work[:, 2 + i % 2, :], parts[:, i % 4, 1, :],
                                        ALU.subtract).then_inc(S["part2"], 1)

        def act_qkv(act, L):
            for c in range(NC + 1):
                if c < NC:
                    norm_modulate(act, SITE[L], c)
                if c:
                    for j in range(2 * CC):
                        i = 2 * CC * (c - 1) + j
                        act_split(act, L, i, 0)
                        if i:
                            act_split(act, L, i - 1, 1)
            act_split(act, L, NQK - 1, 1)

        def dve_qkv(dve, L):
            two_ones = float(np.array([0x3F803F80], np.uint32).view(np.float32)[0])
            nc.vector.memset(arena[ROW_MASK:EXP_ROWS, 0:Q4], two_ones).then_inc(S["ones"], 1)
            for c in range(NC + 2):
                norm_rest(dve, SITE[L], X, c)
                if c < 2:
                    continue
                d = c - 2
                for j in range(2 * CC):
                    i = 2 * CC * d + j
                    dve_split(dve, L, i, 0)
                    dve_split(dve, L, i, 1)
                    if i:
                        dve_split(dve, L, i - 1, 2)
                b = d // CPB
                for p in range(2):
                    dve.wait_ge(*at("vp", L, 2 * d + p + 1))
                    for q in range(2):
                        k = (CT * d + 2 * p + q) % TT
                        last = nc.vector.tensor_tensor(
                            Vh[:, b * H:(b + 1) * H, :, k],
                            PS[:, 2 + p, q * D:(q + 1) * D].rearrange("p (h d) -> p h d", h=H),
                            rows[:, ROW[HEADS[L]["bv"]], :].rearrange("p (h d) -> p h d", h=H), ALU.add)
                    last.then_inc(S["v"], 1)
            dve_split(dve, L, NQK - 1, 2)

        def sp_parts(sp, L, pieces):
            for i in pieces:
                j, c = i % (2 * CC), i // (2 * CC)
                qk, m = j // 2, j % 2
                h0 = (c // CPB) * H + m * (H // 2)
                t0 = (c % CPB) * CW
                sp.wait_ge(*at("part2", L, i + 1))
                sp.dma_start(PQK[qk, h0:h0 + H // 2, :, :, t0:t0 + CW].rearrange("h d s t -> (h d) s t"),
                             parts[:, i % 4, :, :]).then_inc(S[f"pqk_{i % 4}"], 16)

        def v(it, per_head, e, const=0):
            k = per_head * e + const
            return k if it is None else it * (4 * per_head) + k

        def v4(it, e, n):
            k = n * (e // 4 + 1)
            return k if it is None else it * n + k

        def v2(it, e, n):
            k = n * (e // 2 + 1)
            return k if it is None else it * (2 * n) + k

        def heads_loop(eng, step):
            step(None, 0)
            with eng.Fori(0, NH // 4 - 1) as it:
                for e in range(1, 5):
                    step(it, e)
            for e in range(NH - 3, NH):
                step(None, e)

        def head_at(it, e):
            return e if it is None else it * 4 + e

        def last_of(it, e, ahead):
            return it is None and e + ahead >= NH

        def pe_heads(pe, L):
            def max_tile(it, e, t, half):
                s = e % LDS
                if t == 0 and half == 0:
                    pe.wait_ge(*at(f"stack_{s}", L, v4(it, e, 16 * HEADS[L]["loads"])))
                r = 2 * t + half
                if it is not None or 16 * e + r >= 2:
                    pe.wait_ge(*at("max_used", L, v(it, 16, e, r - 1)))
                nc.tensor.matmul(bank(4 + half), QS[0:MAX_ROWS, s, t * P:(t + 1) * P],
                                 KS[0:MAX_ROWS, s, half * CW:(half + 1) * CW],
                                 start=True, stop=True).then_inc(S["max_scores"], 1)

            def max_turn(it, e):
                pe.wait_ge(*at("max_split", L, v(it, 1, e, 1)))
                if it is not None or e >= 2:
                    pe.wait_ge(*at("out_used", L, v(it, 1, e, -1)))
                nc.tensor.transpose(PS[:, 6 + e % 2, 256:320].bitcast(BF16)[0:16, 0:P], msplit[:, e % 4, :],
                                    identb[:, :]).then_inc(S["max_turned"], 1)

            def scores(it, e, t):
                s = e % LDS
                if t == 0:
                    pe.wait_ge(*at(f"max_row_{s}", L, v4(it, e, 16)))
                if it is not None or 8 * e + t >= 2:
                    pe.wait_ge(*at("exp", L, v(it, 8, e, t - 1)))
                for half in range(2):
                    last = nc.tensor.matmul(bank(2 * (t % 2) + half), KS[0:EXP_ROWS, s, t * P:(t + 1) * P],
                                            QS[0:EXP_ROWS, s, half * CW:(half + 1) * CW], start=True, stop=True)
                last.then_inc(S["scores"], 1)

            def values(it, e, t):
                pe.wait_ge(*at("exp", L, v(it, 8, e, t + 1)))
                if t == 0:
                    pe.wait_ge(*at(f"head_v_{e % 2}", L, v2(it, e, 16)))
                    if it is not None or e >= 2:
                        pe.wait_ge(*at("out_used", L, v(it, 1, e, -1)))
                for j in range(4):
                    last = nc.tensor.matmul(PS[32 * j:32 * j + 32, 6 + e % 2, 0:256], Vc[:, e % 2, :, t],
                                            PT[:, t % 4, 256 * j:256 * j + 256], start=(t == 0), stop=(t == TT - 1))
                last.then_inc(S["values"], 1)

            def step(it, e):
                for t in range(TT):
                    if not last_of(it, e, 2):
                        max_tile(it, e + 2, t, 0)
                    scores(it, e, t)
                    if not last_of(it, e, 2):
                        max_tile(it, e + 2, t, 1)
                    if t:
                        values(it, e, t - 1)
                    elif it is not None or e:
                        values(it, e - 1, TT - 1)
                    if t == 3 and not last_of(it, e, 1):
                        max_turn(it, e + 1)

            if L == "l1":
                pe.wait_ge(S["consts"], 2)
            pe.wait_ge(*at("ones", L, 1))
            pe.wait_ge(*at("qk_used", L, NQK))
            for e in range(2):
                for t in range(TT):
                    for half in range(2):
                        max_tile(None, e, t, half)
                if e == 0:
                    max_turn(None, 0)
            pe.wait_ge(*at("h", SITE[L], 2 * NC))
            pe.wait_ge(*at("v", L, 2 * NC))
            heads_loop(pe, step)
            values(None, NH - 1, TT - 1)

        def act_heads(act, L):
            def turned(it, e):
                act.wait_ge(*at("max_turned", L, v(it, 1, e, 1)))
                nc.scalar.copy(mrow[:, e % 4, :], PS[:, 6 + e % 2, 256:320].bitcast(BF16)[0:16, 0:P]
                               ).then_inc(S["max_copied"], 1)

            def out_copy(it, e):
                act.wait_ge(*at("values", L, v(it, 8, e, 8)))
                if it is not None or e >= 2:
                    act.wait_ge(*at(f"stored_{e % 2}", L, v2(it, e - 2, 16)))
                nc.scalar.copy(OE[:, e % 2, :], PS[:, 6 + e % 2, 0:256]).then_inc(S["out_used"], 1)

            def step(it, e):
                for t in range(TT):
                    act.wait_ge(*at("scores", L, v(it, 8, e, t + 1)))
                    if it is not None or 8 * e + t >= 4:
                        act.wait_ge(*at("values", L, v(it, 8, e, t - 3)))
                    nc.scalar.activation(PT[:, t % 4, :], bank2(2 * (t % 2)), ACT.Exp,
                                         scale=HEADS[L]["scale"]).then_inc(S["exp"], 1)
                    if t == 1 and (it is not None or e):
                        out_copy(it, e - 1)
                    if t == 4 and not last_of(it, e, 1):
                        turned(it, e + 1)

            turned(None, 0)
            heads_loop(act, step)
            out_copy(None, NH - 1)

        def dve_heads(dve, L):
            def head(it, e):
                for r in range(2 * TT):
                    dve.wait_ge(*at("max_scores", L, v(it, 16, e, r + 1)))
                    nc.vector.tensor_reduce(nmx[:, e, r:r + 1], bank(4 + r % 2), AX.X, ALU.max,
                                            negate=True).then_inc(S["max_used"], 1)
                dve.wait_ge(*at("max_used", L, v(it, 16, e, 16)))
                halves = nmx[:, e, :].rearrange("p (t h) -> p t h", h=2)
                nc.vector.tensor_tensor(mx[:, e, :], halves[:, :, 0], halves[:, :, 1],
                                        ALU.min).then_inc(S["max_min"], 1)
            with dve.Fori(0, NH // 4) as it:
                for e in range(4):
                    head(it, e)

        def pool_heads(pool, L):
            with pool.Fori(0, NH // 4) as it:
                for e in range(4):
                    pool.wait_ge(*at("max_min", L, v(it, 1, e, 1)))
                    nc.gpsimd.tensor_tensor(msplit[:, e, 0:8], mx[:, e, :], zeros8[:, :],
                                            ALU.add).then_inc(S["max_hi"], 1)
                    pool.wait_ge(*at("max_hi", L, v(it, 1, e, 1)))
                    nc.gpsimd.tensor_tensor(msplit[:, e, 8:16], mx[:, e, :], msplit[:, e, 0:8],
                                            ALU.subtract).then_inc(S["max_split"], 1)

        def sp_heads(sp, L):
            def stack(it, e):
                s = e % LDS
                i = head_at(it, e)
                if it is not None or e >= LDS:
                    sp.wait_ge(*at("scores", L, v(it, 8, e, 8 - 8 * LDS)))
                for qk, dst in ((0, QS), (1, KS)):
                    groups = [(0, 3), (3, 5), (5, 6)]
                    for lo, hi in groups:
                        rows_ = dst[HD * lo:HD * hi, s, :]
                        if qk == 0:
                            src = PQK[qk, bass.ds(i, 1), :, Q_PARTS[lo], :].to_broadcast([hi - lo, HD, T])
                        else:
                            src = PQK[qk, bass.ds(i, 1), :, 0:hi - lo, :].rearrange("i d s t -> i s d t")
                        sp.dma_start(rows_, src).then_inc(S[f"stack_{s}"], 16)
                if L == "l3":
                    sp.dma_start(KS[ROW_MASK:ROW_MASK + 1, s, :], MD[bass.ds(i, 1), :]
                                 ).then_inc(S[f"stack_{s}"], 16)

            def head_v(it, e):
                if it is not None or e >= 2:
                    sp.wait_ge(*at("values", L, v(it, 8, e, -8)))
                sp.dma_start(Vc[:, e % 2, 0:HD, :], Vh[:, bass.ds(head_at(it, e), 1), :, :]
                             ).then_inc(S[f"head_v_{e % 2}"], 16)

            def store(it, e):
                sp.wait_ge(*at("out_used", L, v(it, 1, e, 1)))
                i = head_at(it, e)
                sp.dma_start(OD[bass.ds(i, 1)].rearrange("i r (j t) -> i j r t", j=4), OE[:, e % 2, :]
                             ).then_inc(S[f"stored_{e % 2}"], 16)

            def max_row(it, e):
                sp.wait_ge(*at("max_copied", L, v(it, 1, e, 1)))
                sp.dma_start(QS[ROW_MAX:ROW_MAX + 2, e % LDS, :].rearrange("p (t c) -> p t c", t=TT),
                             mrow[:, e % 4, :]).then_inc(S[f"max_row_{e % LDS}"], 16)

            def sums(b):
                sp.dma_start(Rs[:, b, :], OD[b * H:(b + 1) * H, HD, :].rearrange("i (j t) -> i j t", j=TT)
                             ).then_inc(S["sums"], 16)

            def sums_back(b):
                sp.wait_ge(*at("sums_inv", L, b + 1))
                sp.dma_start(RD[b * H:(b + 1) * H, :].rearrange("i (j t) -> i j t", j=TT), Rs[:, b, :]
                             ).then_inc(S["sums_back"], 16)
                sp.wait_ge(*at("sums_back", L, 16 * (b + 1)))
                for c in range(b * CPB, (b + 1) * CPB):
                    t0 = (c % CPB) * CW
                    for m in range(CC):
                        h0 = b * H + m * (H // 2)
                        sp.dma_start(RT[:, c % 2, m, :],
                                     RD[h0:h0 + H // 2, None, t0:t0 + CW].to_broadcast([H // 2, HD, CW])
                                     ).then_inc(S[f"heads_out_{c % 2}"], 16)

            def step(it, e):
                if it is None and e == NH - 3:
                    for s in range(2):
                        sp.wait_ge(*at(f"stored_{s}", L, 16 * (H // 2)))
                    sums(0)
                    for c in range(CPB):
                        load_out(sp, L, c)
                if it is None and e == NH - 1:
                    sums_back(0)
                if not last_of(it, e, 3):
                    stack(it, e + 3)
                if not last_of(it, e, 1):
                    head_v(it, e + 1)
                if it is not None or e:
                    store(it, e - 1)
                if not last_of(it, e, 1):
                    max_row(it, e + 1)

            sp.wait_ge(*at("ones", L, 1))
            if L == "l1":
                for s in range(LDS):
                    sp.dma_start(KS[ROW_MASK:ROW_MASK + 1, s, :].bitcast(F32), ins["zeros"]
                                 ).then_inc(S["zero_rows"], 16)
            sp_parts(sp, L, range(NQK // B))
            if L == "l1":
                sp.wait_ge(S["zero_rows"], 16 * LDS)
            else:
                sp.wait_ge(S["mask_dram"], 32)
            for s in range(4):
                sp.wait_ge(*at(f"pqk_{s}", L, 16 * (NQK // B // 4)))
            i = NQK // B
            for e in range(3):
                stack(None, e)
                sp_parts(sp, L, range(i, i + 2))
                i += 2
            sp.wait_ge(*at("v", L, NC))
            head_v(None, 0)
            sp_parts(sp, L, range(i, NQK))
            for s in range(4):
                sp.wait_ge(*at(f"pqk_{s}", L, 16 * (NQK // 4)))
            sp.wait_ge(*at("v", L, 2 * NC))
            max_row(None, 0)
            if L == "l1":
                sp_loads_later(sp)
            heads_loop(sp, step)
            store(None, NH - 1)
            for s in range(2):
                sp.wait_ge(*at(f"stored_{s}", L, 16 * (NH // 2)))
            sums(1)
            for c in range(CPB, NC):
                sp.wait_ge(*at("out", XN[L], 2 * (c - 1)))
                load_out(sp, L, c)
            sums_back(1)

        XN = {"l1": "l1a", "l3": "l3a"}

        def load_out(sp, L, c):
            b, t0 = c // CPB, (c % CPB) * CW
            for m in range(CC):
                h0 = b * H + m * (H // 2)
                sp.dma_start(OTn[:, c % 2, m, :], OD[h0:h0 + H // 2, 0:HD, t0:t0 + CW]
                             ).then_inc(S[f"heads_out_{c % 2}"], 16)

        def dve_heads_out(dve, L, after):
            def invert(b):
                r = Rs[:, b, :]
                dve.wait_ge(*at("sums", L, 16 * (b + 1)))
                nc.vector.reciprocal(r, r).then_inc(S["sums_raw"], 1)
                dve.wait_ge(*at("sums_raw", L, b + 1))
                nc.vector.tensor_scalar(r, r, HEADS[L]["rsum"], None, ALU.mult).then_inc(S["sums_inv"], 1)

            def divide(c):
                dve.wait_ge(*at(f"heads_out_{c % 2}", L, 64 * (c // 2 + 1)))
                nc.vector.tensor_tensor(OTn[:, c % 2], OTn[:, c % 2], RT[:, c % 2], ALU.mult).then_inc(S["on"], 1)

            invert(0)
            for c in range(CPB):
                divide(c)
            for c in range(CPB):
                add_to_x(dve, XN[L], c, 4)
            invert(1)
            for c in range(CPB):
                norm_ahead(dve, after, X, c)
            for c in range(CPB, NC):
                divide(c)
            for c in range(CPB, NC):
                add_to_x(dve, XN[L], c, 4)
                norm_ahead(dve, after, X, c)

        def pe_heads_out(pe, L):
            for c in range(NC):
                pe.wait_ge(*at("on", L, c + 1))
                if c == 0:
                    pe.wait_ge(*at("max_used", L, 16 * NH))
                project_tiles(pe, XN[L], c, 4,
                              lambda k, q: [OTn[:, c % 2, k, q * P:(q + 1) * P]],
                              [[HEADS[L]["w"][:, 3, k, :]] for k in range(CC)])

        def dve_l1_post(dve):
            for c in range(NC + 2):
                norm_rest(dve, "l1_post", X, c - 1)
                if c >= 2:
                    d = c - 2
                    sl = X[:, CT * d:CT * d + CT, :]
                    dve.wait_ge(S["l1_mod"], 2 * d + 2)
                    nc.vector.tensor_tensor(sl, sl, xh[:, d % 2], ALU.add).then_inc(S["x_l1"], 1)
                    norm_ahead(dve, "l2_attn", X, d, lag=2)

        def pool_l1_post(pool):
            for c in range(NC + 1):
                if c < NC:
                    norm_rstd(pool, "l1_post", c)
                if c == 0:
                    continue
                d = c - 1
                b = d // CPB
                pool.wait_ge(*at("xh", "l1_post", d + 1))
                for j, op in ((0, ALU.mult), (1, ALU.add)):
                    if j:
                        pool.wait_ge(S["l1_mod"], 2 * d + 1)
                    nc.gpsimd.tensor_tensor(xh[:, d % 2], xh[:, d % 2],
                                            abrow[:, b, j, None, :].to_broadcast([P, CT, D]), op
                                            ).then_inc(S["l1_mod"], 1)

        def pe_l2(pe):
            pe.wait_ge(S["w_l2"], 16)
            pe.wait_ge(S["w_l2_low"], 1)
            for c in range(NC + 1):
                if c < NC:
                    norm_transpose(pe, "l2_attn", c)
                if c == 0:
                    continue
                d = c - 1
                h_ready(pe, "l2_attn", d)
                if d == 0:
                    pe.wait_ge(*at("x", "l1a", 2 * NC))
                    pe.wait_ge(*at("out_used", "l1", NH))
                for j in range(2 * CC):
                    if d:
                        pe.wait_ge(S["l2_qk"], 4 * (d - 1) + j + 1)
                    for k in range(CC):
                        last = product(bank(4 + j), qkv_w("l2", j // 2, k, j % 2), h_chunk("l2_attn", k, d),
                                       k == 0, k == CC - 1)
                    last.then_inc(S["l2_qkp"], 1)
                for p in range(2):
                    if d:
                        pe.wait_ge(S["l2_v"], 2 * (d - 1) + p + 1)
                    for q in range(2):
                        for k in range(CC):
                            last = product(PS[:, 2 + p, q * D:(q + 1) * D],
                                           h_tile("l2_attn", k, CT * d + 2 * p + q), qkv_w("l2", 2, k),
                                           k == 0, k == CC - 1)
                    last.then_inc(S["l2_vp"], 1)
            pe.wait_ge(S["l2_qk"], 4 * NC)
            pe.wait_ge(S["l2_v"], 2 * NC)

            def scores(n):
                if n >= 2:
                    pe.wait_ge(S["l2_exp"], n - 1)
                b = n // TT
                for half in range(2):
                    for k in range(CC):
                        last = nc.tensor.matmul(bank(2 * (n % 2) + half), QT2[:, k, n * P:(n + 1) * P],
                                                KT2[:, k, b * T + half * CW:b * T + (half + 1) * CW],
                                                start=(k == 0), stop=(k == CC - 1))
                last.then_inc(S["l2_scores"], 1)

            def turn(n):
                pe.wait_ge(S["l2_exp"], n + 1)
                if n:
                    pe.wait_ge(S["l2_turn_used"], 2 * n)
                for k in range(TT):
                    last = nc.tensor.transpose(PS[:, 4 + k // 4, (k % 4) * P:(k % 4 + 1) * P],
                                               P2[:, n % 2, k * P:(k + 1) * P], ident[:, :])
                    if k % 4 == 3:
                        last.then_inc(S["l2_turned"], 1)

            def values(c):
                b = c // CPB
                pe.wait_ge(S["l2_turn_used"], 2 * CT * (c + 1))
                for m in range(CC):
                    if c or m:
                        pe.wait_ge(S["l2_oT"], 2 * c + m)
                    for k in range(TT):
                        last = nc.tensor.matmul(bank(6), V2[:, b * TT + k, m * P:(m + 1) * P], PT4[:, k, :],
                                                start=(k == 0), stop=(k == TT - 1))
                    last.then_inc(S["l2_op"], 1)

            def project(c):
                pe.wait_ge(S["l2_oT"], 2 * c + 2)
                for q in range(CT):
                    n = CT * c + q
                    if n % 2 == 0 and n:
                        pe.wait_ge(*at("x", "l2a", n // 2))
                    for k in range(CC):
                        last = nc.tensor.matmul(PS[:, 7, (q % 2) * D:(q % 2 + 1) * D],
                                                OTn[:, c % 2, k, q * P:(q + 1) * P], wA[:, 3, k, :],
                                                start=(k == 0), stop=(k == CC - 1))
                    if n % 2:
                        last.then_inc(S["out"], 1)

            scores(0)
            for n in range(NT):
                if n + 1 < NT:
                    scores(n + 1)
                turn(n)
                if n % CT == CT - 1:
                    values(n // CT)
                    project(n // CT)

        def act_l2(act):
            for c in range(NC + 1):
                if c < NC:
                    norm_modulate(act, "l2_attn", c)
                if c:
                    for j in range(2 * CC):
                        d = c - 1
                        act.wait_ge(S["l2_qkp"], 4 * d + j + 1)
                        dst = (QT2 if j < 2 else KT2)[:, j % 2, d * CW:(d + 1) * CW]
                        nc.scalar.activation(dst, bank(4 + j), ACT.Identity,
                                             bias=cols[:, COL_L2 + j:COL_L2 + j + 1]).then_inc(S["l2_qk"], 1)
            for n in range(NT + 1):
                if n < NT:
                    act.wait_ge(S["l2_max"], n + 1)
                    if n >= 2:
                        act.wait_ge(S["l2_turned"], 2 * (n - 1))
                    nc.scalar.activation(P2[:, n % 2, :], bank2(2 * (n % 2)), ACT.Exp, scale=D ** -0.5,
                                         bias=nm2[:, n:n + 1], accum_out=sum2[:, n:n + 1]).then_inc(S["l2_exp"], 1)
                if n:
                    l2_turn_copy(act, n - 1, 1)
                if n and n % CT == 0:
                    c = n // CT - 1
                    for m in range(CC):
                        act.wait_ge(S["l2_op"], 2 * c + m + 1)
                        if c >= 2:
                            act.wait_ge(*at("out", "l2a", 2 * (c - 1)))
                        nc.scalar.copy(OTn[:, c % 2, m, :], bank(6)).then_inc(S["l2_oT"], 1)

        def l2_turn_copy(eng, n, half):
            q = n % CT
            eng.wait_ge(S["l2_turned"], 2 * n + half + 1)
            if n >= CT and q == 0:
                eng.wait_ge(S["l2_op"], 2 * (n // CT))
            src = PS[:, 4 + half, :].rearrange("p (k q) -> p k q", k=4)
            dst = PT4[:, 4 * half:4 * half + 4, q * P:(q + 1) * P]
            if half:
                nc.scalar.copy(dst, src).then_inc(S["l2_turn_used"], 1)
            else:
                nc.vector.tensor_copy(dst, src).then_inc(S["l2_turn_used"], 1)

        def dve_l2(dve):
            for c in range(NC + 2):
                norm_rest(dve, "l2_attn", X, c)
                if c >= 2:
                    for p in range(2):
                        g = 2 * (c - 2) + p
                        dve.wait_ge(S["l2_vp"], g + 1)
                        nc.vector.tensor_tensor(V2[:, 2 * g:2 * g + 2, :], banks2t(2 + p),
                                                rows[:, ROW["bv2"], None, :].to_broadcast([P, 2, D]),
                                                ALU.add).then_inc(S["l2_v"], 1)

            def maximum(n):
                dve.wait_ge(S["l2_scores"], n + 1)
                nc.vector.tensor_reduce(nm2[:, n:n + 1], bank2(2 * (n % 2)), AX.X, ALU.max,
                                        negate=True).then_inc(S["l2_max_raw"], 1)
                dve.wait_ge(S["l2_max_raw"], n + 1)
                nc.vector.tensor_scalar(nm2[:, n:n + 1], nm2[:, n:n + 1], D ** -0.5, None,
                                        ALU.mult).then_inc(S["l2_max"], 1)

            maximum(0)
            for n in range(NT):
                if n + 1 < NT:
                    maximum(n + 1)
                dve.wait_ge(S["l2_exp"], n + 1)
                nc.vector.reciprocal(rinv2[:, n:n + 1], sum2[:, n:n + 1]).then_inc(S["l2_rinv"], 1)
                l2_turn_copy(dve, n, 0)
                if n % CT == CT - 1:
                    c = n // CT
                    dve.wait_ge(S["l2_rinv"], n + 1)
                    dve.wait_ge(*at("pre", "l2a", c + 1))
                    for p in range(2):
                        dve.wait_ge(*at("out", "l2a", 2 * c + p + 1))
                        for q in range(2):
                            k = CT * c + 2 * p + q
                            last = nc.vector.scalar_tensor_tensor(X[:, k, :], PS[:, 7, q * D:(q + 1) * D],
                                                                  rinv2[:, k:k + 1], X[:, k, :], ALU.mult, ALU.add)
                        last.then_inc(S["x"], 1)
                    norm_ahead(dve, "l2_mlp", X, c)

        def pe_mlp(pe, L, site):
            pe.wait_ge(*at("mlp_w_high", L, 2))
            for c in range(NC + 2):
                if c < NC:
                    norm_transpose(pe, site, c)
                if 1 <= c <= NC:
                    d = c - 1
                    h_ready(pe, site, d)
                    if d == 0:
                        pe.wait_ge(*at("x", {"l2": "l2a", "l3": "l3a"}[L], 2 * NC))
                        if L == "l3":
                            pe.wait_ge(*at("out_used", "l3", NH))
                    for f in range(FC):
                        u = FC * d + f
                        if u >= 4:
                            pe.wait_ge(*at("gelu", L, u - 3))
                        for k in range(CC):
                            last = product(bank(4 + u % 4), [w[:, k, f * P:(f + 1) * P] for w in (wM1_high[L], wM1_r)],
                                           h_chunk(site, k, d), k == 0, k == CC - 1)
                        last.then_inc(S["hid"], 1)
                if c >= 2:
                    d = c - 2
                    pe.wait_ge(*at("gelu_low", L, FC * (d + 1)))
                    project_tiles(pe, MLP[L], d, 2,
                                  lambda k, q: [G_r[:, d % 2, l, k, q * P:(q + 1) * P] for l in range(2)],
                                  [[wM2_high[:, k, :], wM2_r[:, k, :]] for k in range(FC)])

        def act_mlp(act, L, site, col):
            for c in range(NC + 1):
                if c < NC:
                    norm_modulate(act, site, c)
                if c:
                    d = c - 1
                    if d >= 2:
                        act.wait_ge(*at("out", MLP[L], 2 * (d - 1)))
                    for f in range(FC):
                        act.wait_ge(*at("hid", L, FC * d + f + 1))
                        for dst in (G[:, d % 2, 1, f, :], G_r[:, d % 2, 0, f, :]):
                            last = nc.scalar.activation(dst, bank(4 + (FC * d + f) % 4), ACT.Gelu,
                                                        bias=cols[:, col + f:col + f + 1])
                        last.then_inc(S["gelu"], 1)

        def dve_mlp(dve, L, site):
            for c in range(NC + 2):
                norm_rest(dve, site, X, c)
                if 1 <= c <= NC:
                    d = c - 1
                    for f in range(FC):
                        dve.wait_ge(*at("gelu", L, FC * d + f + 1))
                        nc.vector.tensor_tensor(G_r[:, d % 2, 1, f, :], G[:, d % 2, 1, f, :],
                                                G_r[:, d % 2, 0, f, :].bitcast(F32),
                                                ALU.subtract).then_inc(S["gelu_low"], 1)
                if c >= 2:
                    add_to_x(dve, MLP[L], c - 2, 2)
                    if L == "l2":
                        norm_ahead(dve, "l3_attn", X, c - 2)

        block = ctx.enter_context(nc.Block())

        @block.sync
        def _(sp):
            sp_loads(sp)
            sp_heads(sp, "l1")
            sp.wait_ge(*at("x", "l1a", 2 * NC))
            sp.dma_start(wB[:, 0:6], ins["w_l3"].rearrange("w (k p) n -> p w k n", p=P)).then_inc(S["w_l3"], 16)
            sp.wait_ge(*at("x", "l2a", 2 * NC))
            sp.dma_start(rope, ins["rope"].rearrange("a p t -> p a t")).then_inc(S["rope"], 16)
            sp.wait_ge(*at("x", "l2m", 2 * NC))
            sp.dma_start(wM1, ins["w_m3a"].rearrange("(k p) n -> p k n", p=P)).then_inc(S["w_m3"], 16)
            sp.dma_start(wM2, ins["w_m3b"].rearrange("(k p) n -> p k n", p=P)).then_inc(S["w_m3"], 16)
            sp_heads(sp, "l3")
            for c in range(NC):
                sp.wait_ge(*at("x", "l3m", 2 * c + 2))
                sp.dma_start(out.rearrange("b (n p) d -> p (b n) d", p=P)[:, CT * c:CT * c + CT, :],
                             X[:, CT * c:CT * c + CT, :]).then_inc(S["stored"], 16)
            sp.wait_ge(S["stored"], 16 * NC)

        @block.scalar
        def _(act):
            act_loads(act)
            act.wait_ge(S["small"], 64)
            nc.scalar.activation(scond[:, :, :], condT[:, :, :], ACT.Silu).then_inc(S["scond"], 1)
            act_l0(act)
            act_qkv(act, "l1")
            act_heads(act, "l1")
            act_l2(act)
            act_mlp(act, "l2", "l2_mlp", COL_M2)
            act_qkv(act, "l3")
            act_heads(act, "l3")
            act_mlp(act, "l3", "l3_mlp", COL_M3)

        @block.vector
        def _(dve):
            dve_l0(dve)
            dve_qkv(dve, "l1")
            dve_heads(dve, "l1")
            dve_heads_out(dve, "l1", "l1_post")
            dve_l1_post(dve)
            dve_l2(dve)
            dve_mlp(dve, "l2", "l2_mlp")
            dve_qkv(dve, "l3")
            dve_heads(dve, "l3")
            dve_heads_out(dve, "l3", "l3_mlp")
            dve_mlp(dve, "l3", "l3_mlp")

        @block.gpsimd
        def _(pool):
            def row(name):
                return lambda b: rows[:, ROW[name], :]

            def rstds(site):
                for c in range(NC):
                    norm_rstd(pool, site, c)

            def split_mlp(L):
                done, _ = at("mlp_w_high", L, 0)
                split_weights(pool, wM1, wM1_high[L], wM1_r, done)
                split_weights(pool, wM2, wM2_high, wM2_r, done)

            pool_l0(pool)
            norms(pool, "l1", row("bp1"))
            pool_heads(pool, "l1")
            pool.wait_ge(S["w_l2"], 16)
            split_weights(pool, wA[:, 0:3], w_high["l2"], wA_r[:, 0:3], S["w_l2_low"])
            pool_l1_post(pool)
            norms(pool, "l2_attn", row("bp2"))
            pool.wait_ge(S["l2_vp"], 2 * NC)
            pool.wait_ge(S["w_m2"], 32)
            split_mlp("l2")
            norms(pool, "l2_mlp", row("b22"))
            rstds("l3_attn")
            add_rows(pool, "l3_attn", row("bo3"))
            pool_heads(pool, "l3")
            pool.wait_ge(S["w_m3"], 32)
            split_mlp("l3")
            norms(pool, "l3_mlp", row("b23"))

        @block.tensor
        def _(pe):
            pe_l0(pe)
            pe_qkv(pe, "l1")
            pe_heads(pe, "l1")
            pe_heads_out(pe, "l1")
            pe_l2(pe)
            pe_mlp(pe, "l2", "l2_mlp")
            pe_qkv(pe, "l3")
            pe_heads(pe, "l3")
            pe_heads_out(pe, "l3")
            pe_mlp(pe, "l3", "l3_mlp")


def kernel(**inputs):
    import concourse.bacc as bacc
    from concourse.bass_utils import run_bass_kernel_spmd

    a = {k: np.asarray(x) for k, x in inputs.items()}

    def l(n, name):
        return a[f"L{n}_cond_{name}"]

    def pairs(w):
        return w.reshape(w.shape[:-1] + (D // 2, 2))[..., ::-1].reshape(w.shape)

    def halves(w):
        return np.concatenate([w[..., D:], w[..., :D]], axis=-1)

    def columns(x):
        return x.reshape(-1, P).T

    wqkv = l(1, "Wqkv").reshape(H, HD, 3, D).transpose(2, 3, 0, 1).reshape(3, D, D)
    bqkv = l(1, "bqkv").reshape(H, HD, 3).transpose(2, 0, 1).reshape(3, D)
    zero = np.zeros(D, np.float32)
    mod_b = [l(0, "emb_b"), l(1, "bg"), l(1, "bb"), halves(l(3, "ada1_b")), halves(l(3, "ada2_b")),
             l(2, "film1_b"), l(2, "film2_b")]
    gains = [l(0, "sn_g"), l(1, "ln_g"), l(3, "ln1_g"), l(3, "ln2_g"), l(2, "norm1_w"), l(2, "norm2_w")]
    offsets = [l(0, "sn_b"), l(1, "ln_b"), l(3, "ln1_b"), l(3, "ln2_b"), zero, zero]
    cols = columns(np.concatenate(
        mod_b + gains + offsets + [l(0, "norm_g"), l(0, "norm_b"), l(0, "bk"), bqkv[0], bqkv[1],
                                   l(2, "q_b"), l(2, "k_b"), l(3, "bq"), l(3, "bk"),
                                   pairs(l(3, "bq")), pairs(l(3, "bk")), l(2, "mlp_b1"), l(3, "ff_b1")]))
    rows = np.stack([l(0, "bq"), l(0, "bv"), l(0, "out_b"), a["cond_1024"][0], a["cond_1024"][1],
                     bqkv[2], l(1, "bp"), l(1, "bg"), l(1, "bb"), l(1, "ln_g"), l(1, "ln_b"),
                     l(2, "v_b"), l(2, "proj_b"), l(2, "mlp_b2"), l(3, "bv"), l(3, "bo"), l(3, "ff_b2")])
    cond_w = np.concatenate([l(0, "emb_W"), l(1, "Wg").T, l(1, "Wb").T, halves(l(3, "ada1_w")),
                             halves(l(3, "ada2_w")), l(2, "film1_w"), l(2, "film2_w")], axis=1)
    rot = HD // 2
    inv = (1.0 / np.float32(10000.0) ** (np.arange(rot, dtype=np.float32) / np.float32(rot))).astype(np.float32)
    freq = np.arange(T, dtype=np.float32)[None, :] * inv[:, None]
    chan = np.arange(P) % HD
    sign = np.where(chan % 2 == 0, -1.0, 1.0).astype(np.float32)
    tables = np.stack([np.cos(freq)[chan // 2], np.sin(freq)[chan // 2] * sign[:, None]])
    block = np.arange(P) // HD

    arrays = {
        "x": a["x"],
        "mask": a["mask_BxS_bf1"].view(np.uint8),
        "cols": cols,
        "rows": rows,
        "condT": a["cond_1024"].T.reshape(CC, P, B).transpose(1, 0, 2),
        "cond_w": cond_w,
        "w_l0": np.stack([l(0, "Wq"), l(0, "Wk"), l(0, "Wv"), l(0, "out_W")]),
        "w_l1": np.concatenate([wqkv, l(1, "Wp").T[None]]),
        "w_l2": np.stack([l(2, "q_w"), l(2, "k_w"), l(2, "v_w"), l(2, "proj_w")]),
        "w_l3": np.stack([l(3, "wq"), l(3, "wk"), l(3, "wv"), l(3, "wo"), pairs(l(3, "wq")), pairs(l(3, "wk"))]),
        "w_m2a": l(2, "mlp_w1"), "w_m2b": l(2, "mlp_w2"), "w_m3a": l(3, "ff_w1"), "w_m3b": l(3, "ff_w2"),
        "rope": tables.astype(np.float32),
        "ident": np.eye(P, dtype=np.float32),
        "zeros": np.zeros((1, T // 2), np.float32),
        "bdmask": (block[:, None] == block[None, :]).astype(np.float32),
    }
    arrays = {f"in_{k}": np.ascontiguousarray(x) for k, x in arrays.items()}
    nc = bacc.Bacc("TRN2", target_bir_lowering=False, num_devices=1)
    ins = {k[3:]: nc.dram_tensor(k, x.shape, mybir.dt.from_np(x.dtype), kind="ExternalInput").ap()
           for k, x in arrays.items()}
    out = nc.dram_tensor("out_0", (B, T, D), F32, kind="ExternalOutput").ap()
    build(nc, ins, out)
    r = run_bass_kernel_spmd(nc, [arrays], core_ids=[0])
    return r.results[0]["out_0"]
```

```python
from contextlib import ExitStack

import numpy as np

import concourse.bass as bass
from concourse import mybir

F32 = mybir.dt.float32
F32R = mybir.dt.float32r
BF16 = mybir.dt.bfloat16
U8 = mybir.dt.uint8
ACT = mybir.ActivationFunctionType
ALU = mybir.AluOpType
AX = mybir.AxisListType

P = 128
B = 2
T = 1024
D = 256
H = 16
HD = D // H
NH = B * H
CC = D // P
NT = B * T // P
TT = T // P
CW = 512
NC = B * T // CW
CT = CW // P
CPB = T // CW
FF = 4 * D
FC = FF // P
PARTS = 3
Q_PARTS = (0, 0, 0, 1, 1, 2)
K_PARTS = (0, 1, 2, 0, 1, 0)
ROW_MASK = HD * len(Q_PARTS)
ROW_MAX = ROW_MASK + 1
MAX_ROWS = ROW_MASK + 1
EXP_ROWS = ROW_MASK + 3
LDS = 4

SITES = ("l0_out", "l1", "l3_attn", "l3_mlp", "l2_attn", "l2_mlp")
AB = {n: i for i, n in enumerate(SITES)}
AB["l0_in"] = len(SITES)
SPLIT_SITES = ("l0_in", "l1", "l2_attn", "l2_mlp", "l3_attn", "l3_mlp")
NS = len(SITES)

COLS = ["emb_b", "sln_b", "ada1_b", "ada2_b", "film1_b", "film2_b"]
COL_MOD = 0
COL_G = 4 * NS
COL_B = COL_G + 2 * NS
COL_L0G, COL_L0B, COL_BK0 = (COL_B + 2 * NS + 2 * i for i in range(3))
COL_L1 = COL_BK0 + 2
COL_L2 = COL_L1 + 4
COL_L3 = COL_L2 + 4
COL_L3S = COL_L3 + 4
COL_M2 = COL_L3S + 4
COL_M3 = COL_M2 + FC
NCOL = COL_M3 + FC

ROWS = ["bq0", "bv0", "ob0", "gate0", "gate1", "bv1", "bp1", "bg1", "bb1", "lng1", "lnb1",
        "bv2", "bp2", "b22", "bv3", "bo3", "b23"]
ROW = {n: i for i, n in enumerate(ROWS)}
EARLY_ROWS = 5


def build(nc, ins, out):
    ctx = ExitStack()
    with ctx:
        def sb(name, shape, dt=F32):
            return ctx.enter_context(nc.sbuf_tensor(name, shape, dt))

        def sb_r(name, shape):
            base = nc.sbuf_base
            return sb(name, shape), nc.alloc_sbuf_tensor_at(name + "_r", shape, F32R, offset=base)

        class Sems(dict):
            def __missing__(self, name):
                self[name] = ctx.enter_context(nc.semaphore(name))
                return self[name]

        S = Sems()

        MLP = {"l2": "l2m", "l3": "l3m"}
        NORMS = ("l0_in", "l0_out", "l1", "l1_post", "l2_attn", "l2_mlp", "l3_attn", "l3_mlp")
        ADDS = ("l0", "l1a", "l2a", "l2m", "l3a", "l3m")
        HEADED = ("l1", "l3")
        NQK = 2 * CC * NC
        TURNED = tuple(n for n in NORMS if n != "l1_post")
        COUNTS = {
            "h_low": (SPLIT_SITES, 2 * NC), "gelu_low": (("l2", "l3"), FC * NC), "mlp_w_high": (("l2", "l3"), 2),
            "transposed": (TURNED, 2 * NC), "h": (TURNED, 2 * NC),
            "pre": (ADDS, NC), "out": (ADDS, 2 * NC), "x": (ADDS, 2 * NC),
            "hid": (("l2", "l3"), FC * NC), "gelu": (("l2", "l3"), FC * NC),
            "v": (HEADED, 2 * NC), "vp": (HEADED, 2 * NC),
            "max_used": (HEADED, 2 * TT * NH), "max_scores": (HEADED, 2 * TT * NH),
            "exp": (HEADED, TT * NH), "scores": (HEADED, TT * NH), "values": (HEADED, TT * NH),
            "sums": (HEADED, 16 * B), "sums_inv": (HEADED, B), "sums_back": (HEADED, 16 * B),
            "sums_raw": (HEADED, B), "on": (HEADED, NC), "ones": (HEADED, 1), "rot": (("l3",), NQK),
        }
        for n in ("qkp", "qk_used", "r1", "part0", "part1", "part2"):
            COUNTS[n] = (HEADED, NQK)
        for n in ("out_used", "max_turned", "max_split", "max_copied", "max_min", "max_hi"):
            COUNTS[n] = (HEADED, NH)
        for i in range(LDS):
            COUNTS[f"pqk_{i}"] = (HEADED, 16 * (NQK // 4))
            COUNTS[f"max_row_{i}"] = (HEADED, 16 * (NH // LDS))
            COUNTS[f"stack_{i}"] = (HEADED, 16 * 6 * (NH // LDS))
        for i in range(2):
            COUNTS[f"head_v_{i}"] = (HEADED, 16 * (NH // 2))
            COUNTS[f"stored_{i}"] = (HEADED, 16 * (NH // 2))
            COUNTS[f"heads_out_{i}"] = (HEADED, 64 * (NC // 2))

        def at(name, stage, value):
            stages, per_stage = COUNTS[name]
            return S[name], value + stages.index(stage) * per_stage

        X = sb("X", [P, NT, D])
        hT, hT_r = sb_r("hT", [P, 2, 2, CC, CW])
        xh = sb("xh", [P, 2, CT, D])
        arena, arena_r = sb_r("arena", [P, 4 * NT * D])
        aux, aux_r = sb_r("aux", [P, NT * D])
        work, work_r = sb_r("work", [P, 4, CW])
        split, split_r = sb_r("split", [P, 4 * PARTS * CW // 2])
        wA, wA_r = sb_r("wA", [P, 4, CC, D])
        wB, wB_r = sb_r("wB", [P, 6, CC, D])
        wM, wM_r = sb_r("wM", [P, 8, CC * D])
        cols = sb("cols", [P, NCOL])
        rows = sb("rows", [P, len(ROWS), D])
        ident = sb("ident", [P, P])
        identb = sb("identb", [P, P], BF16)
        bdmask = sb("bdmask", [P, P])
        condT = sb("condT", [P, CC, B])
        scond = sb("scond", [P, CC, B])
        mods = sb("mods", [P, 4 * NS, B])
        modg = sb("modg", [P, NS, CC, B])
        ab = sb("ab", [P, NS + 1, 2, CC, B])
        abrow = sb("abrow", [P, B, 2, D])
        stats = sb("stats", [P, NT, 6])
        mv = sb("mv", [P, NT, 2])
        ve = sb("ve", [P, NT])
        rstd = sb("rstd", [P, NT])
        mhalf = sb("mhalf", [P, NT])
        nmx = sb("nmx", [P, 4, 16])
        mx = sb("mx", [P, 4, 8])
        zeros8 = sb("zeros8", [P, 8])
        msplit = sb("msplit", [P, 4, 16], BF16)
        mrow = sb("mrow", [16, 4, P], BF16)
        nm2 = sb("nm2", [P, NT])
        sum2 = sb("sum2", [P, NT])
        rinv2 = sb("rinv2", [P, NT])
        Vc = sb("Vc", [P, 2, 2 * HD, TT])
        OE = sb("OE", [P, 2, 256])
        k_nmax = sb("k_nmax", [P, CC * B])
        k_sum = sb("k_sum", [P, CC * B])

        Q4 = NT * D
        condW = (wM[:, :, :].rearrange("p a b -> p (a b)").rearrange("p (k n) -> p k n", k=CC),
                 aux[:, 0:CC * 4 * D].rearrange("p (k n) -> p k n", k=CC))
        condBC = arena[:, 3 * Q4:3 * Q4 + CC * B * P].rearrange("p (k b m) -> p k b m", k=CC, b=B)
        maskf = arena[:, 3 * Q4 + 1024:3 * Q4 + 2048]
        masku = arena[:, 3 * Q4 + 2048:3 * Q4 + 2304].bitcast(U8)
        maskb = arena[:, 3 * Q4 + 2304:3 * Q4 + 2816].bitcast(BF16)
        kTs = arena[:, 0:Q4].rearrange("p (m t) -> p m t", m=CC)
        q_sb = arena[:, Q4:2 * Q4].rearrange("p (n d) -> p n d", d=D)
        v_sb = arena[:, 2 * Q4:3 * Q4].rearrange("p (n d) -> p n d", d=D)
        ekt = arena[:, 3 * Q4:].rearrange("p (n d) -> p n d", d=D)
        qTs = aux[:, :].rearrange("p (m t) -> p m t", m=CC)
        ctx_sb = work[:, 0, :].rearrange("p (b m d) -> p b m d", b=B, m=CC)
        wo_g = work[:, 2:4, :].rearrange("p b (k d) -> p b k d", k=CC)
        gbias = split[:, 0:B * D].rearrange("p (b d) -> p b d", b=B)
        q_red = split[:, B * D:B * D + NT * 2 * H].rearrange("p (n s h) -> p n s h", n=NT, s=2)
        parts = split[:, :].bitcast(BF16).rearrange("p (s i t) -> p s i t", s=4, i=PARTS)
        rope = wA[:, :, :, :].rearrange("p w k n -> p (w k n)").rearrange("p (a t) -> p a t", a=2)
        QS = arena[:, 0:Q4 // 2].bitcast(BF16).rearrange("p (s t) -> p s t", s=LDS)
        KS = arena[:, Q4 // 2:Q4].bitcast(BF16).rearrange("p (s t) -> p s t", s=LDS)
        PT = arena[:, Q4:2 * Q4].rearrange("p (s t) -> p s t", s=4)
        qk_f32, rest = (arena[:, Q4 + n * 4 * CW:Q4 + (n + 1) * 4 * CW].rearrange("p (s t) -> p s t", s=4)
                        for n in range(2))
        Vh = arena[:, 2 * Q4:3 * Q4].rearrange("p (i d k) -> p i d k", i=NH, d=HD)
        OTn = aux[:, 0:2 * CC * CW].rearrange("p (s m t) -> p s m t", s=2, m=CC)
        RT = aux[:, 2 * CC * CW:].rearrange("p (s m t) -> p s m t", s=2, m=CC)
        Rs = arena[:, 3 * Q4:3 * Q4 + B * P].rearrange("p (b t) -> p b t", b=B)
        QT2 = arena[:, 0:Q4].rearrange("p (m t) -> p m t", m=CC)
        KT2 = arena[:, Q4:2 * Q4].rearrange("p (m t) -> p m t", m=CC)
        V2 = arena[:, 2 * Q4:3 * Q4].rearrange("p (n d) -> p n d", d=D)
        PT4 = arena[:, 3 * Q4:].rearrange("p (k q) -> p k q", k=TT)
        V2_r = arena_r[:, 2 * Q4:3 * Q4].rearrange("p (n d) -> p n d", d=D)
        V2_high = hT_r[:, :, :, :, :].rearrange("p s l k t -> p (s l k t)").rearrange("p (n d) -> p n d", d=D)
        PT4_r = arena_r[:, 3 * Q4:].rearrange("p (k q) -> p k q", k=TT)
        PT4_high = [x.rearrange("p (k q) -> p k q", k=TT // 2)
                    for x in (aux_r[:, 2 * CC * CW:], split_r[:, 0:TT // 2 * CW])]
        P2 = work[:, :, :].rearrange("p (s h) t -> p s (h t)", s=2)
        G = arena[:, :].rearrange("p (s l f t) -> p s l f t", s=2, l=2, f=FC)
        G_r = arena_r[:, :].rearrange("p (s l f t) -> p s l f t", s=2, l=2, f=FC)
        wM1_r = wM_r[:, 0:4, :].rearrange("p a b -> p (a b)").rearrange("p (k n) -> p k n", k=CC)
        wM2_r = wM_r[:, 4:8, :].rearrange("p a b -> p (a b)").rearrange("p (f d) -> p f d", f=FC)
        wM1_high = work_r[:, :, :].rearrange("p a b -> p (a b)").rearrange("p (k n) -> p k n", k=CC)
        wM2_high = split_r[:, 0:FC * D].rearrange("p (f d) -> p f d", f=FC)
        QKV_W = 3 * CC * D
        w_high = {"l0": split_r[:, 2 * B * D:2 * B * D + QKV_W].rearrange("p (w k n) -> p w k n", w=3, k=CC),
                  "l1": wM_r[:, :, :].rearrange("p a b -> p (a b)")[:, 0:QKV_W].rearrange("p (w k n) -> p w k n", w=3, k=CC),
                  "l2": split_r[:, 0:QKV_W].rearrange("p (w k n) -> p w k n", w=3, k=CC)}
        w_low = {"l0": wA_r, "l1": wB_r, "l2": wA_r, "l3": wB_r}
        qk_high, v_high, qks_high = (aux_r[:, n * CC * D:(n + 2) * CC * D].rearrange("p (w k n) -> p w k n", w=2, k=CC)
                                     for n in (0, 4, 2))
        l3_high = {0: qk_high[:, 0], 1: qk_high[:, 1], 2: v_high[:, 0], 4: qks_high[:, 0], 5: qks_high[:, 1]}
        wM1 = wM[:, 0:4, :].rearrange("p a b -> p (a b)").rearrange("p (k n) -> p k n", k=CC)
        wM2 = wM[:, 4:8, :].rearrange("p a b -> p (a b)").rearrange("p (f d) -> p f d", f=FC)

        PQK = nc.dram_tensor("pqk", (2, NH, HD, PARTS, T), BF16, kind="Internal").ap()
        OD = nc.dram_tensor("od", (NH, 2 * HD, T), F32, kind="Internal").ap()
        RD = nc.dram_tensor("rd", (NH, T), F32, kind="Internal").ap()
        MD = nc.dram_tensor("md", (NH, T), BF16, kind="Internal").ap()

        PS = ctx.enter_context(nc.psum_tensor("PS", [P, 8, CW], F32))

        def bank(i):
            return PS[:, i, :]

        def bank2(i):
            return PS[:, i:i + 2, :].rearrange("p a b -> p (a b)")

        def banks2t(i):
            return PS[:, i, :].rearrange("p (t d) -> p t d", t=2)

        ready = {
            "l0_in": lambda e, c: e.wait_ge(S[f"x_{c}"], 16),
            "l0_out": lambda e, c: e.wait_ge(S["l0_y"], 2 * c + 2),
            "l1": lambda e, c: e.wait_ge(*at("x", "l0", 2 * c + 2)),
            "l1_post": lambda e, c: e.wait_ge(*at("x", "l1a", 2 * c + 2)),
            "l2_attn": lambda e, c: e.wait_ge(S["x_l1"], c + 1),
            "l2_mlp": lambda e, c: e.wait_ge(*at("x", "l2a", 2 * c + 2)),
            "l3_attn": lambda e, c: e.wait_ge(*at("x", "l2m", 2 * c + 2)),
            "l3_mlp": lambda e, c: e.wait_ge(*at("x", "l3a", 2 * c + 2)),
        }
        NORM_CHUNKS = [(n, c) for n in NORMS[:3] for c in range(NC)]
        NORM_CHUNKS += [(n, c) for b in range(B) for n in ("l1_post", "l2_attn") for c in range(b * CPB, (b + 1) * CPB)]
        NORM_CHUNKS += [(n, c) for n in NORMS[5:] for c in range(NC)]

        def nth(site, c):
            return NORM_CHUNKS.index((site, c)) + 1

        RMS = {"l2_attn": True, "l2_mlp": True}

        def norm_stats(dve, site, src, c):
            ready[site](dve, c)
            for k in range(CT):
                n = CT * c + k
                nc.vector.bn_stats(stats[:, n, :], src[:, n, :]).then_inc(S["stats"], 1)
            dve.wait_ge(S["stats"], CT * nth(site, c))
            for k in range(CT):
                n = CT * c + k
                last = nc.vector.bn_aggr(mv[:, n, :], stats[:, n, :])
            last.then_inc(S["moments"], 1)
            if site in RMS:
                sl = slice(CT * c, CT * c + CT)
                dve.wait_ge(S["moments"], nth(site, c))
                nc.vector.tensor_tensor(ve[:, sl], mv[:, sl, 0], mv[:, sl, 0], ALU.mult).then_inc(S["msq"], 1)
                r = 2 * (NC * (site == "l2_mlp") + c)
                dve.wait_ge(S["msq"], r + 1)
                nc.vector.tensor_tensor(mv[:, sl, 1], mv[:, sl, 1], ve[:, sl], ALU.add).then_inc(S["msq"], 1)

        def norm_rstd(pool, site, c):
            sl = slice(CT * c, CT * c + CT)
            if site in RMS:
                pool.wait_ge(S["msq"], 2 * (NC * (site == "l2_mlp") + c) + 2)
            else:
                pool.wait_ge(S["moments"], nth(site, c))
            nc.gpsimd.tensor_scalar(ve[:, sl], mv[:, sl, 1], 1e-6 if site in RMS else 1e-5, None,
                                    ALU.add).then_inc(S["var_eps"], 1)
            pool.wait_ge(S["var_eps"], nth(site, c))
            nc.gpsimd.tensor_tensor(rstd[:, sl], ve[:, sl], mhalf[:, sl], ALU.pow).then_inc(S["rstd"], 1)

        def norm_apply(dve, site, src, c):
            dve.wait_ge(S["rstd"], nth(site, c))
            if c >= 2:
                site2 = "l2_attn" if site == "l1_post" else site
                dve.wait_ge(*at("transposed", site2, 2 * (c - 1)))
            for k in range(CT):
                n = CT * c + k
                if site in RMS:
                    last = nc.vector.tensor_scalar(xh[:, c % 2, k, :], src[:, n, :], rstd[:, n:n + 1],
                                                   None, ALU.mult)
                else:
                    last = nc.vector.tensor_scalar(xh[:, c % 2, k, :], src[:, n, :], mv[:, n, 0:1],
                                                   rstd[:, n:n + 1], ALU.subtract, ALU.mult)
            last.then_inc(S["xh"], 1)

        def norm_ahead(dve, site, src, c):
            norm_stats(dve, site, src, c)
            if 1 <= c < 3:
                norm_apply(dve, site, src, c - 1)

        def norm_rest(dve, site, src, c):
            if 2 <= c < NC:
                norm_apply(dve, site, src, c)

        def norm_transpose(pe, site, c):
            pe.wait_ge(S["xh"], nth(site, c))
            for m in range(CC):
                if c:
                    pe.wait_ge(*at("h", site, 2 * (c - 1) + m + 1))
                for k in range(CT):
                    last = nc.tensor.transpose(PS[:, m, k * P:(k + 1) * P],
                                               xh[:, c % 2, k, m * P:(m + 1) * P], ident[:, :])
                last.then_inc(S["transposed"], 1)

        def norm_modulate(act, site, c, func=ACT.Identity):
            b = c // CPB
            i = AB[site]
            for m in range(CC):
                act.wait_ge(*at("transposed", site, 2 * c + m + 1))
                dst = [hT[:, c % 2, 1, m, :]]
                if site in SPLIT_SITES:
                    dst.append(hT_r[:, c % 2, 0, m, :])
                for d in dst:
                    last = nc.scalar.activation(d, bank(m), func, bias=ab[:, i, 1, m, b:b + 1],
                                                scale=ab[:, i, 0, m, b:b + 1])
                last.then_inc(S["h"], 1)

        def norm_low(pool, site, c):
            for m in range(CC):
                pool.wait_ge(*at("h", site, 2 * c + m + 1))
                nc.gpsimd.tensor_tensor(hT_r[:, c % 2, 1, m, :], hT[:, c % 2, 1, m, :],
                                        hT_r[:, c % 2, 0, m, :].bitcast(F32), ALU.subtract).then_inc(S["h_low"], 1)

        def h_ready(pe, site, c):
            pe.wait_ge(*at("h_low" if site in SPLIT_SITES else "h", site, 2 * c + 2))

        def h_chunk(site, m, c):
            if site in SPLIT_SITES:
                return [hT_r[:, c % 2, l, m, :] for l in range(2)]
            return [hT[:, c % 2, 1, m, :]]

        def h_tile(site, m, n):
            c, q = n // CT, n % CT
            return [x[:, q * P:(q + 1) * P] for x in h_chunk(site, m, c)]

        def product(out, lhs, rhs, start, stop):
            if len(lhs) == 1:
                return nc.tensor.matmul(out, lhs[0], rhs[0], start=start, stop=stop)
            nc.tensor.matmul(out, lhs[0], rhs[0], start=start, stop=False)
            nc.tensor.matmul(out, lhs[0], rhs[1], start=False, stop=False)
            return nc.tensor.matmul(out, lhs[1], rhs[0], start=False, stop=stop)

        def qkv_w(L, j, k, m=None):
            sl = slice(0, D) if m is None else slice(m * P, (m + 1) * P)
            high = l3_high[j] if L == "l3" else w_high[L][:, j]
            return [high[:, k, sl], w_low[L][:, j, k, sl]]

        def split_weights(pool, raw, high, low, done):
            nc.gpsimd.tensor_copy(high, raw).then_inc(S["w_high"], 1)
            w_split[0] += 1
            pool.wait_ge(S["w_high"], w_split[0])
            nc.gpsimd.tensor_tensor(low, raw, high.bitcast(F32), ALU.subtract).then_inc(done, 1)

        w_split = [0]

        def add_rows(pool, site, row):
            for c in range(NC):
                add_row(pool, site, c, row)

        def add_row(pool, site, c, row):
            pool.wait_ge(S["xh"], nth(site, c))
            bias = row(c // CPB)
            nc.gpsimd.tensor_tensor(X[:, CT * c:CT * c + CT, :], X[:, CT * c:CT * c + CT, :],
                                    bias[:, None, :].to_broadcast([P, CT, D]),
                                    ALU.add).then_inc(S["pre"], 1)

        def norms(pool, site, row=None):
            for c in range(2):
                norm_rstd(pool, site, c)
            for c in range(NC):
                norm_low(pool, site, c)
                if c + 2 < NC:
                    norm_rstd(pool, site, c + 2)
                if row:
                    add_row(pool, site, c, row)

        def norms_of(pool, site, b, row):
            for c in range(b * CPB, (b + 1) * CPB):
                norm_rstd(pool, site, c)
            for c in range(b * CPB, (b + 1) * CPB):
                norm_low(pool, site, c)
                add_row(pool, site, c, row)

        def add_to_x(dve, name, c, b0):
            dve.wait_ge(*at("pre", name, c + 1))
            for p in range(2):
                n = CT * c + 2 * p
                dve.wait_ge(*at("out", name, 2 * c + p + 1))
                nc.vector.tensor_tensor(X[:, n:n + 2, :], banks2t(b0 + p), X[:, n:n + 2, :],
                                        ALU.add).then_inc(S["x"], 1)

        def project_tiles(pe, name, c, b0, lhs, w, wait_bank=True):
            nk = len(w)
            for p in range(2):
                if c and wait_bank:
                    pe.wait_ge(*at("x", name, 2 * (c - 1) + p + 1))
                for q in range(2):
                    for k in range(nk):
                        last = product(PS[:, b0 + p, q * D:(q + 1) * D], lhs(k, 2 * p + q), w[k],
                                       k == 0, k == nk - 1)
                last.then_inc(S["out"], 1)

        def sp_loads(sp):
            for c in range(NC):
                sp.dma_start(X[:, CT * c:CT * c + CT, :],
                             ins["x"].rearrange("b (n p) d -> p (b n) d", p=P)[:, CT * c:CT * c + CT, :]
                             ).then_inc(S[f"x_{c}"], 16)
            sp.dma_start(wA[:, 0:4], ins["w_l0"].rearrange("w (k p) n -> p w k n", p=P)).then_inc(S["w_l0"], 16)
            for part, w in enumerate(condW):
                sp.dma_start(w, ins["cond_w"].rearrange("(k p) n -> p k n", p=P)[:, :, part * 8 * D:part * 8 * D + w.shape[2]]
                             ).then_inc(S["w_cond"], 16)
            sp.dma_start(rows[:, EARLY_ROWS:, :], ins["rows"][EARLY_ROWS:].partition_broadcast(P)
                         ).then_inc(S["more_rows"], 16)
            sp.dma_start(masku[0:1], ins["mask"][0:1, :]).then_inc(S["mask_u8"], 16)
            sp.dma_start(masku[32:33], ins["mask"][1:2, :]).then_inc(S["mask_u8"], 16)
            sp.dma_start(wB[:, 0:4], ins["w_l1"].rearrange("w (k p) n -> p w k n", p=P)).then_inc(S["w_l1"], 16)
            sp.wait_ge(S["mask_bias"], 1)
            for b in range(B):
                sp.dma_start(MD[b * H:(b + 1) * H, :],
                             maskb[32 * b:32 * b + 1, None, :].to_broadcast([1, H, T])).then_inc(S["mask_dram"], 16)

        def sp_loads_later(sp):
            sp.wait_ge(*at("x", "l0", 2 * NC))
            sp.dma_start(wA[:, 0:4], ins["w_l2"].rearrange("w (k p) n -> p w k n", p=P)).then_inc(S["w_l2"], 16)
            sp.wait_ge(*at("vp", "l1", 2 * NC))
            sp.dma_start(wM1, ins["w_m2a"].rearrange("(k p) n -> p k n", p=P)).then_inc(S["w_m2"], 16)
            sp.dma_start(wM2, ins["w_m2b"].rearrange("(k p) n -> p k n", p=P)).then_inc(S["w_m2"], 16)

        def act_loads(act):
            act.dma_start(ident[:, :], ins["ident"]).then_inc(S["ident"], 16)
            act.dma_start(cols[:, :], ins["cols"]).then_inc(S["small"], 16)
            act.dma_start(condT[:, :, :], ins["condT"]).then_inc(S["small"], 16)
            act.dma_start(rows[:, 0:EARLY_ROWS, :], ins["rows"][0:EARLY_ROWS].partition_broadcast(P)
                          ).then_inc(S["rows"], 16)
            act.dma_start(bdmask[:, :], ins["bdmask"]).then_inc(S["bdmask"], 16)

        def pe_cond(pe):
            pe.wait_ge(S["w_cond"], 32)
            pe.wait_ge(S["l0_kT"], 2 * NC)
            pe.wait_ge(S["l0_qv"], 4 * NC)
            pe.wait_ge(S["small"], 32)
            pe.wait_ge(S["scond"], 1)
            pe.wait_ge(S["cond_bc"], 1)
            for b in range(B):
                for k in range(CC):
                    last = nc.tensor.matmul(bank(6 + b), condBC[:, k, b, :],
                                            condW[0][:, k, 2 * D:4 * D], start=(k == 0), stop=(k == CC - 1))
            last.then_inc(S["cond_rows"], 1)
            for i in range(4 * NS):
                c = scond if i < 4 else condT
                w, j = (condW[0], i) if i < 16 else (condW[1], i - 16)
                for k in range(CC):
                    last = nc.tensor.matmul(PS[:, 5, i * B:(i + 1) * B], w[:, k, j * P:(j + 1) * P],
                                            c[:, k, :], start=(k == 0), stop=(k == CC - 1))
            last.then_inc(S["cond_cols"], 1)

        def dve_cond(dve):
            nc.vector.memset(mhalf[:, :], -0.5)
            nc.vector.memset(zeros8[:, :], 0.0)
            nc.vector.memset(Vc[:, :, :, :], 1.0).then_inc(S["consts"], 1)

        def dve_small(dve):
            dve.wait_ge(S["small"], 32)
            dve.wait_ge(S["ident"], 16)
            nc.vector.tensor_copy(identb[:, :], ident[:, :]).then_inc(S["consts"], 1)
            nc.vector.tensor_copy(condBC, condT[:, :, :, None].to_broadcast([P, CC, B, P])).then_inc(S["cond_bc"], 1)
            nc.vector.tensor_copy(ab[:, NS, 0], cols[:, COL_L0G:COL_L0G + 2, None].to_broadcast([P, CC, B]))
            nc.vector.tensor_copy(ab[:, NS, 1], cols[:, COL_L0B:COL_L0B + 2, None].to_broadcast([P, CC, B])
                                  ).then_inc(S["ab_in"], 1)

        def dve_cond2(dve):
            dve.wait_ge(S["mask_u8"], 32)
            for q in (0, 32):
                nc.vector.tensor_scalar(maskf[q:q + 1, :], masku[q:q + 1, :], 1.0, 3e38, ALU.subtract,
                                        ALU.mult).then_inc(S["mask_f32"], 1)
            dve.wait_ge(S["mask_f32"], 2)
            for q in (0, 32):
                last = nc.vector.tensor_scalar(maskb[q:q + 1, :], maskf[q:q + 1, :], 10.0, None, ALU.mult)
            last.then_inc(S["mask_bias"], 1)
            dve.wait_ge(S["cond_cols"], 1)
            nc.vector.tensor_tensor(mods[:, :, :], PS[:, 5, 0:4 * NS * B].rearrange("p (i b) -> p i b", b=B),
                                    cols[:, 0:4 * NS, None].to_broadcast([P, 4 * NS, B]), ALU.add).then_inc(S["mod"], 1)
            dve.wait_ge(S["mod"], 1)
            m4 = mods[:, :, :].rearrange("p (s h c) b -> p s h c b", s=NS, h=2)
            nc.vector.tensor_scalar(modg[:, :], m4[:, :, 0], 1.0, None, ALU.add).then_inc(S["mod"], 1)
            dve.wait_ge(S["mod"], 2)
            nc.vector.tensor_copy(modg[:, 1], m4[:, 1, 0]).then_inc(S["mod"], 1)
            dve.wait_ge(S["mod"], 3)
            g = cols[:, COL_G:COL_G + 2 * NS].rearrange("p (s c) -> p s c", s=NS)
            bb = cols[:, COL_B:COL_B + 2 * NS].rearrange("p (s c) -> p s c", s=NS)
            for b in range(B):
                nc.vector.tensor_tensor(ab[:, 0:NS, 0, :, b], modg[:, :, :, b], g, ALU.mult)
                nc.vector.tensor_tensor(ab[:, 0:4, 1, :, b], modg[:, 0:4, :, b], bb[:, 0:4], ALU.mult).then_inc(S["mod"], 1)
            dve.wait_ge(S["mod"], 5)
            for b in range(B):
                nc.vector.tensor_tensor(ab[:, 0:4, 1, :, b], ab[:, 0:4, 1, :, b], m4[:, 0:4, 1, :, b], ALU.add)
                last = nc.vector.tensor_copy(ab[:, 4:6, 1, :, b], m4[:, 4:6, 1, :, b])
            last.then_inc(S["ab"], 1)
            dve.wait_ge(S["cond_rows"], 1)
            dve.wait_ge(S["more_rows"], 16)
            for b in range(B):
                r = rows[:, ROW["bg1"]:ROW["bb1"] + 1, :]
                nc.vector.tensor_tensor(abrow[:, b], banks2t(6 + b), r, ALU.add).then_inc(S["abrow"], 1)
                dve.wait_ge(S["abrow"], 3 * b + 1)
                nc.vector.tensor_tensor(xh[:, 1, b, :], abrow[:, b, 0], rows[:, ROW["lnb1"], :], ALU.mult).then_inc(S["abrow"], 1)
                dve.wait_ge(S["abrow"], 3 * b + 2)
                nc.vector.tensor_tensor(abrow[:, b, 0], abrow[:, b, 0], rows[:, ROW["lng1"], :], ALU.mult)
                nc.vector.tensor_tensor(abrow[:, b, 1], abrow[:, b, 1], xh[:, 1, b, :], ALU.add).then_inc(S["abrow"], 1)
            dve.wait_ge(S["w_l0"], 16)
            for b in range(B):
                gate = rows[:, ROW["gate0"] + b, :]
                nc.vector.tensor_tensor(gbias[:, b], rows[:, ROW["ob0"], :], gate, ALU.mult)
                last = nc.vector.tensor_tensor(wo_g[:, b], wA[:, 3], gate[:, None, :].to_broadcast([P, CC, D]), ALU.mult)
            last.then_inc(S["gated"], 1)

        def pe_l0(pe):
            pe.wait_ge(S["ident"], 16)
            for c in range(NC + 1):
                if c < NC:
                    norm_transpose(pe, "l0_in", c)
                if c == 0:
                    continue
                d = c - 1
                if d == 0:
                    pe.wait_ge(S["w_l0_low"], 1)
                h_ready(pe, "l0_in", d)
                for m in range(CC):
                    if d:
                        pe.wait_ge(S["l0_kT"], 2 * (d - 1) + m + 1)
                    for k in range(CC):
                        last = product(bank(4 + m), qkv_w("l0", 1, k, m), h_chunk("l0_in", k, d),
                                       k == 0, k == CC - 1)
                    last.then_inc(S["l0_kp"], 1)
                for p in range(2):
                    for j, w in ((0, 0), (1, 2)):
                        u = 2 * (2 * d + p) + j
                        if u >= 2:
                            pe.wait_ge(S["l0_qv"], u - 1)
                        for q in range(2):
                            for k in range(CC):
                                last = product(PS[:, 6 + j, q * D:(q + 1) * D],
                                               h_tile("l0_in", k, CT * d + 2 * p + q), qkv_w("l0", w, k),
                                               k == 0, k == CC - 1)
                        last.then_inc(S["l0_qvp"], 1)
            pe_cond(pe)
            for c in range(NC):
                pe.wait_ge(S["l0_qn"], 2 * c + 2)
                for m in range(CC):
                    pe.wait_ge(*at("h", "l0_in", 2 * NC)) if c == 0 else pe.wait_ge(S["l0_qT"], 2 * (c - 1) + m + 1)
                    for k in range(CT):
                        last = nc.tensor.transpose(PS[:, m, k * P:(k + 1) * P],
                                                   q_sb[:, CT * c + k, m * P:(m + 1) * P], ident[:, :])
                    last.then_inc(S["l0_qTp"], 1)
            for g in range(NT // 2):
                pe.wait_ge(S["l0_kexp"], 2 * (g // (TT // 2)) + 2)
                if g >= 2:
                    pe.wait_ge(S["l0_ekt"], g - 1)
                for q in range(2):
                    for m in range(CC):
                        n = 2 * g + q
                        last = nc.tensor.transpose(PS[:, 2 + g % 2, q * D + m * P:q * D + (m + 1) * P],
                                                   kTs[:, m, n * P:(n + 1) * P], ident[:, :])
                last.then_inc(S["l0_ektp"], 1)
            pe.wait_ge(S["l0_kT"], 2 * NC)
            pe.wait_ge(S["l0_ekt"], NT // 2)
            for b in range(B):
                for m in range(CC):
                    for k in range(TT):
                        n = TT * b + k
                        last = nc.tensor.matmul(PS[:, 4, (CC * b + m) * P:(CC * b + m + 1) * P],
                                                ekt[:, n, m * P:(m + 1) * P], v_sb[:, n, m * P:(m + 1) * P],
                                                start=(k == 0), stop=(k == TT - 1))
            last.then_inc(S["l0_ctxp"], 1)
            pe.wait_ge(S["l0_ctx"], 4)
            pe.wait_ge(S["abrow"], 6)
            pe.wait_ge(S["l0_qT"], 2 * NC)
            pe.wait_ge(S["l0_qv"], 4 * NC)
            for g in range(NT // 2):
                if g >= 2:
                    pe.wait_ge(S["l0_y"], g - 1)
                for q in range(2):
                    n = 2 * g + q
                    for m in range(CC):
                        last = nc.tensor.matmul(PS[:, 6 + g % 2, q * D + m * P:q * D + (m + 1) * P],
                                                qTs[:, m, n * P:(n + 1) * P], ctx_sb[:, n // TT, m, :],
                                                start=True, stop=True)
                last.then_inc(S["l0_yp"], 1)
            for c in range(NC + 1):
                if c < NC:
                    norm_transpose(pe, "l0_out", c)
                if c:
                    d = c - 1
                    h_ready(pe, "l0_out", d)
                    if d == 0:
                        pe.wait_ge(S["gated"], 1)
                    project_tiles(pe, "l0", d, 2, lambda k, q: h_tile("l0_out", k, CT * d + q),
                                  [[wo_g[:, d // CPB, k, :]] for k in range(CC)])

        def act_l0(act):
            act.wait_ge(S["ab_in"], 1)
            for c in range(NC + 1):
                if c < NC:
                    norm_modulate(act, "l0_in", c)
                if c == 0:
                    act.wait_ge(S["w_l0"], 16)
                    nc.scalar.copy(w_high["l0"], wA[:, 0:3]).then_inc(S["w_l0_high"], 1)
                if c:
                    d = c - 1
                    for m in range(CC):
                        act.wait_ge(S["l0_kp"], 2 * d + m + 1)
                        nc.scalar.activation(kTs[:, m, d * CW:(d + 1) * CW], bank(4 + m), ACT.Identity,
                                             bias=cols[:, COL_BK0 + m:COL_BK0 + m + 1]).then_inc(S["l0_kT"], 1)
            for g in range(NT // 2):
                act.wait_ge(S["l0_qsub"], g + 1)
                nc.scalar.activation(q_sb[:, 2 * g:2 * g + 2, :], q_sb[:, 2 * g:2 * g + 2, :],
                                     ACT.Exp).then_inc(S["l0_qexp"], 1)
            for b in range(B):
                for m in range(CC):
                    i = CC * b + m
                    act.wait_ge(S["l0_kmax"], i + 1)
                    kk = kTs[:, m, b * T:(b + 1) * T]
                    nc.scalar.activation(kk, kk, ACT.Exp, bias=k_nmax[:, i:i + 1],
                                         accum_out=k_sum[:, i:i + 1]).then_inc(S["l0_kexp"], 1)
            for c in range(NC):
                for m in range(CC):
                    act.wait_ge(S["l0_qTp"], 2 * c + m + 1)
                    nc.scalar.copy(qTs[:, m, c * CW:(c + 1) * CW], bank(m)).then_inc(S["l0_qT"], 1)
            for g in range(NT // 2):
                act.wait_ge(S["l0_yp"], g + 1)
                nc.scalar.copy(q_sb[:, 2 * g:2 * g + 2, :], banks2t(6 + g % 2)).then_inc(S["l0_y"], 1)
            act.wait_ge(S["ab"], 1)
            for c in range(NC):
                norm_modulate(act, "l0_out", c, ACT.Silu)

        def q_heads(g):
            return q_sb[:, 2 * g:2 * g + 2, :].rearrange("p n (h d) -> p n h d", h=H)

        def dve_l0(dve):
            dve_cond(dve)
            norm_stats(dve, "l0_in", X, 0)
            for c in range(NC + 2):
                if c + 1 < NC:
                    norm_stats(dve, "l0_in", X, c + 1)
                if c < NC:
                    norm_apply(dve, "l0_in", X, c)
                if c == 0:
                    dve_small(dve)
                if c == 1:
                    dve.wait_ge(S["w_l0_high"], 1)
                    nc.vector.tensor_tensor(wA_r[:, 0:3], wA[:, 0:3], w_high["l0"].bitcast(F32),
                                            ALU.subtract).then_inc(S["w_l0_low"], 1)
                if c < 2:
                    continue
                d = c - 2
                if d == 0:
                    dve.wait_ge(S["rows"], 16)
                for p in range(2):
                    g = 2 * d + p
                    for j, (dst, r) in enumerate(((q_sb, "bq0"), (v_sb, "bv0"))):
                        dve.wait_ge(S["l0_qvp"], 2 * g + j + 1)
                        nc.vector.tensor_tensor(dst[:, 2 * g:2 * g + 2, :], banks2t(6 + j),
                                                rows[:, ROW[r], None, :].to_broadcast([P, 2, D]),
                                                ALU.add).then_inc(S["l0_qv"], 1)
                    dve.wait_ge(S["l0_qv"], 2 * g + 1)
                    nc.vector.tensor_reduce(q_red[:, 2 * g:2 * g + 2, 0, :], q_heads(g), AX.X,
                                            ALU.max).then_inc(S["l0_qmax"], 1)
            for b in range(B):
                for m in range(CC):
                    i = CC * b + m
                    dve.wait_ge(S["l0_kT"], 2 * (CPB * b + CPB - 1) + m + 1)
                    nc.vector.tensor_reduce(k_nmax[:, i:i + 1], kTs[:, m, b * T:(b + 1) * T], AX.X, ALU.max,
                                            negate=True).then_inc(S["l0_kmax"], 1)
            for g in range(NT // 2):
                sl = q_red[:, 2 * g:2 * g + 2, 1, :]
                dve.wait_ge(S["l0_qexp"], g + 1)
                nc.vector.tensor_reduce(sl, q_heads(g), AX.X, ALU.add).then_inc(S["l0_qsum"], 1)
                dve.wait_ge(S["l0_qsum"], g + 1)
                nc.vector.reciprocal(sl, sl).then_inc(S["l0_qinv"], 1)
            dve_cond2(dve)
            dve.wait_ge(S["mask_dram"], 32)
            for g in range(NT // 2):
                dve.wait_ge(S["l0_ektp"], g + 1)
                nc.vector.tensor_copy(ekt[:, 2 * g:2 * g + 2, :], banks2t(2 + g % 2)).then_inc(S["l0_ekt"], 1)
            dve.wait_ge(S["l0_kexp"], B * CC)
            nc.vector.reciprocal(k_sum[:, :], k_sum[:, :]).then_inc(S["l0_kinv"], 1)
            dve.wait_ge(S["l0_kinv"], 1)
            dve.wait_ge(S["l0_ctxp"], 1)
            dve.wait_ge(S["bdmask"], 16)
            for b in range(B):
                for m in range(CC):
                    i = CC * b + m
                    nc.vector.scalar_tensor_tensor(ctx_sb[:, b, m, :], PS[:, 4, i * P:(i + 1) * P],
                                                   k_sum[:, i:i + 1], bdmask[:, :], ALU.mult,
                                                   ALU.mult).then_inc(S["l0_ctx"], 1)
            for c in range(NC + 3):
                if c < NC:
                    norm_stats(dve, "l0_out", q_sb, c)
                if 1 <= c <= NC:
                    norm_apply(dve, "l0_out", q_sb, c - 1)
                if c >= 3:
                    add_to_x(dve, "l0", c - 3, 2)
                    norm_ahead(dve, "l1", X, c - 3)

        def pool_l0(pool):
            pool.wait_ge(S["consts"], 1)
            norms(pool, "l0_in")
            for g in range(NT // 2):
                pool.wait_ge(S["l0_qmax"], g + 1)
                nc.gpsimd.tensor_tensor(q_heads(g), q_heads(g),
                                        q_red[:, 2 * g:2 * g + 2, 0, :, None].to_broadcast([P, 2, H, HD]),
                                        ALU.subtract).then_inc(S["l0_qsub"], 1)
            for g in range(NT // 2):
                pool.wait_ge(S["l0_qinv"], g + 1)
                nc.gpsimd.tensor_tensor(q_heads(g), q_heads(g),
                                        q_red[:, 2 * g:2 * g + 2, 1, :, None].to_broadcast([P, 2, H, HD]),
                                        ALU.mult).then_inc(S["l0_qn"], 1)
            pool.wait_ge(S["cond_cols"], 1)
            pool.wait_ge(S["cond_rows"], 1)
            pool.wait_ge(S["w_l1"], 16)
            split_weights(pool, wB[:, 0:3], w_high["l1"], wB_r[:, 0:3], S["w_l1_low"])
            pool.wait_ge(S["gated"], 1)
            add_rows(pool, "l0_in", lambda b: gbias[:, b, :])
            for c in range(NC):
                norm_rstd(pool, "l0_out", c)

        HEADS = {
            "l1": dict(w=wB, col=COL_L1, bv="bv1", scale=1.0, rope=False, loads=6, rsum=1.0 / 16.0),
            "l3": dict(w=wB, col=COL_L3, bv="bv3", scale=HD ** -0.5, rope=True, loads=7, rsum=1.0),
        }
        SITE = {"l1": "l1", "l3": "l3_attn"}

        def pe_qkv(pe, L):
            rot = HEADS[L]["rope"]
            pe.wait_ge(S[f"w_{L}_low"], 3 if rot else 1)
            pe.wait_ge(S["w_" + L], 16)

            for c in range(NC + 1):
                if c < NC:
                    norm_transpose(pe, SITE[L], c)
                if c == 0:
                    continue
                d = c - 1
                h_ready(pe, SITE[L], d)
                if d == 0 and L == "l1":
                    pe.wait_ge(S["l0_y"], NT // 2)
                    pe.wait_ge(*at("x", "l0", 2 * NC))
                if d == 0 and L == "l3":
                    pe.wait_ge(*at("x", "l2m", 2 * NC))
                    pe.wait_ge(*at("gelu", "l2", FC * NC))
                for j in range(2 * CC):
                    i = 2 * CC * d + j
                    b0 = 4 + 2 * (i % 2)
                    if i >= 2:
                        pe.wait_ge(*at("qk_used", L, i - 1))
                    for k in range(CC):
                        last = product(bank(b0), qkv_w(L, j // 2, k, j % 2), h_chunk(SITE[L], k, d),
                                       k == 0, k == CC - 1)
                    if rot:
                        for k in range(CC):
                            last = product(bank(b0 + 1), qkv_w(L, 4 + j // 2, k, j % 2), h_chunk(SITE[L], k, d),
                                           k == 0, k == CC - 1)
                    last.then_inc(S["qkp"], 1)
                for p in range(2):
                    if d:
                        pe.wait_ge(*at("v", L, 2 * (d - 1) + p + 1))
                    for q in range(2):
                        for k in range(CC):
                            last = product(PS[:, 2 + p, q * D:(q + 1) * D],
                                           h_tile(SITE[L], k, CT * d + 2 * p + q), qkv_w(L, 2, k),
                                           k == 0, k == CC - 1)
                    last.then_inc(S["vp"], 1)

        def act_split(act, L, i, stage):
            if stage == 0:
                if not HEADS[L]["rope"]:
                    act.wait_ge(*at("qkp", L, i + 1))
                    if i >= 4:
                        act.wait_ge(*at("r1", L, i - 3))
                    col = HEADS[L]["col"] + i % (2 * CC)
                    nc.scalar.activation(qk_f32[:, i % 4, :], bank(4 + 2 * (i % 2)), ACT.Identity,
                                         bias=cols[:, col:col + 1]).then_inc(S["qk_used"], 1)
                    act.wait_ge(*at("qk_used", L, i + 1))
                else:
                    act.wait_ge(*at("rot", L, i + 1))
                if i >= 4:
                    act.wait_ge(*at(f"pqk_{i % 4}", L, 16 * (i // 4)))
                nc.scalar.copy(parts[:, i % 4, 0, :], qk_f32[:, i % 4, :]).then_inc(S["part0"], 1)
            else:
                act.wait_ge(*at("r1", L, i + 1))
                nc.scalar.copy(parts[:, i % 4, 1, :], rest[:, i % 4, :]).then_inc(S["part1"], 1)

        def dve_split(dve, L, i, stage):
            if stage == 0:
                if HEADS[L]["rope"]:
                    j, c = i % (2 * CC), i // (2 * CC)
                    t0 = (c % CPB) * CW
                    if i == 0:
                        dve.wait_ge(S["rope"], 16)
                    dve.wait_ge(*at("qkp", L, i + 1))
                    if i >= 4:
                        dve.wait_ge(*at("part2", L, i - 3))
                    nc.vector.scalar_tensor_tensor(qk_f32[:, i % 4, :], bank(4 + 2 * (i % 2)),
                                                   cols[:, COL_L3 + j:COL_L3 + j + 1],
                                                   rope[:, 0, t0:t0 + CW], ALU.add, ALU.mult)
                    nc.vector.scalar_tensor_tensor(rest[:, i % 4, :], bank(5 + 2 * (i % 2)),
                                                   cols[:, COL_L3S + j:COL_L3S + j + 1],
                                                   rope[:, 1, t0:t0 + CW], ALU.add,
                                                   ALU.mult).then_inc(S["qk_used"], 1)
                    dve.wait_ge(*at("qk_used", L, i + 1))
                    nc.vector.tensor_tensor(qk_f32[:, i % 4, :], qk_f32[:, i % 4, :], rest[:, i % 4, :],
                                            ALU.add).then_inc(S["rot"], 1)
            else:
                dve.wait_ge(*at("part0", L, i + 1))
                if i >= 4:
                    dve.wait_ge(*at("part2", L, i - 3))
                nc.vector.tensor_tensor(rest[:, i % 4, :], qk_f32[:, i % 4, :], parts[:, i % 4, 0, :],
                                        ALU.subtract).then_inc(S["r1"], 1)

        def pool_split(pool, L, i):
            pool.wait_ge(*at("part1", L, i + 1))
            nc.gpsimd.tensor_tensor(parts[:, i % 4, 2, :], rest[:, i % 4, :], parts[:, i % 4, 1, :],
                                    ALU.subtract).then_inc(S["part2"], 1)

        def pool_qkv(pool, L, row, prepare=None):
            for c in range(2):
                norm_rstd(pool, SITE[L], c)
            if prepare:
                prepare()
            for c in range(NC + 1):
                if c < NC:
                    norm_low(pool, SITE[L], c)
                    if c + 2 < NC:
                        norm_rstd(pool, SITE[L], c + 2)
                if c:
                    for i in range(2 * CC * (c - 1), 2 * CC * c):
                        pool_split(pool, L, i)
                if c < NC:
                    add_row(pool, SITE[L], c, row)

        def act_qkv(act, L):
            for c in range(NC + 1):
                if c < NC:
                    norm_modulate(act, SITE[L], c)
                if c:
                    for j in range(2 * CC):
                        i = 2 * CC * (c - 1) + j
                        act_split(act, L, i, 0)
                        if i:
                            act_split(act, L, i - 1, 1)
            act_split(act, L, NQK - 1, 1)

        def dve_qkv(dve, L):
            lag = 1 if HEADS[L]["rope"] else 0
            two_ones = float(np.array([0x3F803F80], np.uint32).view(np.float32)[0])
            nc.vector.memset(arena[ROW_MASK:EXP_ROWS, 0:Q4], two_ones).then_inc(S["ones"], 1)
            for c in range(NC + 2):
                norm_rest(dve, SITE[L], X, c)
                if c < 2:
                    continue
                d = c - 2
                for j in range(2 * CC):
                    i = 2 * CC * d + j
                    dve_split(dve, L, i, 0)
                    if i >= lag:
                        dve_split(dve, L, i - lag, 1)
                b = d // CPB
                for p in range(2):
                    dve.wait_ge(*at("vp", L, 2 * d + p + 1))
                    for q in range(2):
                        k = (CT * d + 2 * p + q) % TT
                        last = nc.vector.tensor_tensor(
                            Vh[:, b * H:(b + 1) * H, :, k],
                            PS[:, 2 + p, q * D:(q + 1) * D].rearrange("p (h d) -> p h d", h=H),
                            rows[:, ROW[HEADS[L]["bv"]], :].rearrange("p (h d) -> p h d", h=H), ALU.add)
                    last.then_inc(S["v"], 1)
            if lag:
                dve_split(dve, L, NQK - 1, 1)

        def sp_parts(sp, L, pieces):
            for i in pieces:
                j, c = i % (2 * CC), i // (2 * CC)
                qk, m = j // 2, j % 2
                h0 = (c // CPB) * H + m * (H // 2)
                t0 = (c % CPB) * CW
                sp.wait_ge(*at("part2", L, i + 1))
                sp.dma_start(PQK[qk, h0:h0 + H // 2, :, :, t0:t0 + CW].rearrange("h d s t -> (h d) s t"),
                             parts[:, i % 4, :, :]).then_inc(S[f"pqk_{i % 4}"], 16)

        def v(it, per_head, e, const=0):
            k = per_head * e + const
            return k if it is None else it * (4 * per_head) + k

        def v4(it, e, n):
            k = n * (e // 4 + 1)
            return k if it is None else it * n + k

        def v2(it, e, n):
            k = n * (e // 2 + 1)
            return k if it is None else it * (2 * n) + k

        def heads_loop(eng, step):
            step(None, 0)
            with eng.Fori(0, NH // 4 - 1) as it:
                for e in range(1, 5):
                    step(it, e)
            for e in range(NH - 3, NH):
                step(None, e)

        def head_at(it, e):
            return e if it is None else it * 4 + e

        def last_of(it, e, ahead):
            return it is None and e + ahead >= NH

        def pe_heads(pe, L):
            def max_tile(it, e, t, half):
                s = e % LDS
                if t == 0 and half == 0:
                    pe.wait_ge(*at(f"stack_{s}", L, v4(it, e, 16 * HEADS[L]["loads"])))
                r = 2 * t + half
                if it is not None or 16 * e + r >= 2:
                    pe.wait_ge(*at("max_used", L, v(it, 16, e, r - 1)))
                nc.tensor.matmul(bank(4 + half), QS[0:MAX_ROWS, s, t * P:(t + 1) * P],
                                 KS[0:MAX_ROWS, s, half * CW:(half + 1) * CW],
                                 start=True, stop=True).then_inc(S["max_scores"], 1)

            def max_turn(it, e):
                pe.wait_ge(*at("max_split", L, v(it, 1, e, 1)))
                if it is not None or e >= 2:
                    pe.wait_ge(*at("out_used", L, v(it, 1, e, -1)))
                nc.tensor.transpose(PS[:, 6 + e % 2, 256:320].bitcast(BF16)[0:16, 0:P], msplit[:, e % 4, :],
                                    identb[:, :]).then_inc(S["max_turned"], 1)

            def scores(it, e, t):
                s = e % LDS
                if t == 0:
                    pe.wait_ge(*at(f"max_row_{s}", L, v4(it, e, 16)))
                if it is not None or 8 * e + t >= 2:
                    pe.wait_ge(*at("exp", L, v(it, 8, e, t - 1)))
                for half in range(2):
                    last = nc.tensor.matmul(bank(2 * (t % 2) + half), KS[0:EXP_ROWS, s, t * P:(t + 1) * P],
                                            QS[0:EXP_ROWS, s, half * CW:(half + 1) * CW], start=True, stop=True)
                last.then_inc(S["scores"], 1)

            def values(it, e, t):
                pe.wait_ge(*at("exp", L, v(it, 8, e, t + 1)))
                if t == 0:
                    pe.wait_ge(*at(f"head_v_{e % 2}", L, v2(it, e, 16)))
                    if it is not None or e >= 2:
                        pe.wait_ge(*at("out_used", L, v(it, 1, e, -1)))
                for j in range(4):
                    last = nc.tensor.matmul(PS[32 * j:32 * j + 32, 6 + e % 2, 0:256], Vc[:, e % 2, :, t],
                                            PT[:, t % 4, 256 * j:256 * j + 256], start=(t == 0), stop=(t == TT - 1))
                last.then_inc(S["values"], 1)

            def step(it, e):
                for t in range(TT):
                    ahead, u = (1, t + TT // 2) if t < TT // 2 else (2, t - TT // 2)
                    if it is None and e == NH - 2 and t == TT - 2:
                        pe.wait_ge(*at("max_used", L, 16 * NH))
                        pe_heads_out(pe, L, 0)
                    if not last_of(it, e, ahead):
                        max_tile(it, e + ahead, u, 0)
                    scores(it, e, t)
                    if not last_of(it, e, ahead):
                        max_tile(it, e + ahead, u, 1)
                    if t:
                        values(it, e, t - 1)
                    elif it is not None or e:
                        values(it, e - 1, TT - 1)
                    if t == 5 and not last_of(it, e, 1):
                        max_turn(it, e + 1)

            if L == "l1":
                pe.wait_ge(S["consts"], 2)
            pe.wait_ge(*at("ones", L, 1))
            pe.wait_ge(*at("qk_used", L, NQK))
            for e, t in [(0, t) for t in range(TT)] + [(1, t) for t in range(TT // 2)]:
                for half in range(2):
                    max_tile(None, e, t, half)
                if (e, t) == (1, 1):
                    max_turn(None, 0)
            pe.wait_ge(*at("h", SITE[L], 2 * NC))
            pe.wait_ge(*at("v", L, 2 * NC))
            heads_loop(pe, step)
            values(None, NH - 1, TT - 1)

        def act_heads(act, L):
            def turned(it, e):
                act.wait_ge(*at("max_turned", L, v(it, 1, e, 1)))
                nc.scalar.copy(mrow[:, e % 4, :], PS[:, 6 + e % 2, 256:320].bitcast(BF16)[0:16, 0:P]
                               ).then_inc(S["max_copied"], 1)

            def out_copy(it, e):
                act.wait_ge(*at("values", L, v(it, 8, e, 8)))
                if it is not None or e >= 2:
                    act.wait_ge(*at(f"stored_{e % 2}", L, v2(it, e - 2, 16)))
                nc.scalar.copy(OE[:, e % 2, :], PS[:, 6 + e % 2, 0:256]).then_inc(S["out_used"], 1)

            def step(it, e):
                for t in range(TT):
                    act.wait_ge(*at("scores", L, v(it, 8, e, t + 1)))
                    if it is not None or 8 * e + t >= 4:
                        act.wait_ge(*at("values", L, v(it, 8, e, t - 3)))
                    nc.scalar.activation(PT[:, t % 4, :], bank2(2 * (t % 2)), ACT.Exp,
                                         scale=HEADS[L]["scale"]).then_inc(S["exp"], 1)
                    if t == 1 and (it is not None or e):
                        out_copy(it, e - 1)
                    if t == 5 and not last_of(it, e, 1):
                        turned(it, e + 1)

            turned(None, 0)
            heads_loop(act, step)
            out_copy(None, NH - 1)

        def dve_heads(dve, L):
            def head(it, e):
                for r in range(2 * TT):
                    dve.wait_ge(*at("max_scores", L, v(it, 16, e, r + 1)))
                    nc.vector.tensor_reduce(nmx[:, e % 4, r:r + 1], bank(4 + r % 2), AX.X, ALU.max,
                                            negate=True).then_inc(S["max_used"], 1)
                dve.wait_ge(*at("max_used", L, v(it, 16, e, 16)))
                halves = nmx[:, e % 4, :].rearrange("p (t h) -> p t h", h=2)
                nc.vector.tensor_tensor(mx[:, e % 4, :], halves[:, :, 0], halves[:, :, 1],
                                        ALU.min).then_inc(S["max_min"], 1)
            with dve.Fori(0, NH // 4 - 1) as it:
                for e in range(4):
                    head(it, e)
            for e in range(NH - 4, NH):
                head(None, e)
                if e == NH - 2:
                    dve_invert(dve, L, 0)

        def pool_heads(pool, L, loaded, pieces):
            def head(it, e):
                pool.wait_ge(*at("max_min", L, v(it, 1, e, 1)))
                nc.gpsimd.tensor_tensor(msplit[:, e % 4, 0:8], mx[:, e % 4, :], zeros8[:, :],
                                        ALU.add).then_inc(S["max_hi"], 1)
                pool.wait_ge(*at("max_hi", L, v(it, 1, e, 1)))
                nc.gpsimd.tensor_tensor(msplit[:, e % 4, 8:16], mx[:, e % 4, :], msplit[:, e % 4, 0:8],
                                        ALU.subtract).then_inc(S["max_split"], 1)

            with pool.Fori(0, NH // 4 - 1) as it:
                for e in range(4):
                    head(it, e)
            pool.wait_ge(*loaded)
            for e in range(NH - 4, NH):
                head(None, e)
                if e - (NH - 4) < len(pieces):
                    split_weights(pool, *pieces[e - (NH - 4)])

        def sp_heads(sp, L):
            def stack(it, e):
                s = e % LDS
                i = head_at(it, e)
                if it is not None or e >= LDS:
                    sp.wait_ge(*at("scores", L, v(it, 8, e, 8 - 8 * LDS)))
                for qk, dst in ((0, QS), (1, KS)):
                    groups = [(0, 3), (3, 5), (5, 6)]
                    for lo, hi in groups:
                        rows_ = dst[HD * lo:HD * hi, s, :]
                        if qk == 0:
                            src = PQK[qk, bass.ds(i, 1), :, Q_PARTS[lo], :].to_broadcast([hi - lo, HD, T])
                        else:
                            src = PQK[qk, bass.ds(i, 1), :, 0:hi - lo, :].rearrange("i d s t -> i s d t")
                        sp.dma_start(rows_, src).then_inc(S[f"stack_{s}"], 16)
                if L == "l3":
                    sp.dma_start(KS[ROW_MASK:ROW_MASK + 1, s, :], MD[bass.ds(i, 1), :]
                                 ).then_inc(S[f"stack_{s}"], 16)

            def head_v(it, e):
                if it is not None or e >= 2:
                    sp.wait_ge(*at("values", L, v(it, 8, e, -8)))
                sp.dma_start(Vc[:, e % 2, 0:HD, :], Vh[:, bass.ds(head_at(it, e), 1), :, :]
                             ).then_inc(S[f"head_v_{e % 2}"], 16)

            def store(it, e):
                sp.wait_ge(*at("out_used", L, v(it, 1, e, 1)))
                i = head_at(it, e)
                sp.dma_start(OD[bass.ds(i, 1)].rearrange("i r (j t) -> i j r t", j=4), OE[:, e % 2, :]
                             ).then_inc(S[f"stored_{e % 2}"], 16)

            def max_row(it, e):
                sp.wait_ge(*at("max_copied", L, v(it, 1, e, 1)))
                sp.dma_start(QS[ROW_MAX:ROW_MAX + 2, e % LDS, :].rearrange("p (t c) -> p t c", t=TT),
                             mrow[:, e % 4, :]).then_inc(S[f"max_row_{e % LDS}"], 16)

            def sums(b):
                sp.dma_start(Rs[:, b, :], OD[b * H:(b + 1) * H, HD, :].rearrange("i (j t) -> i j t", j=TT)
                             ).then_inc(S["sums"], 16)

            def sums_back(b):
                sp.wait_ge(*at("sums_inv", L, b + 1))
                sp.dma_start(RD[b * H:(b + 1) * H, :].rearrange("i (j t) -> i j t", j=TT), Rs[:, b, :]
                             ).then_inc(S["sums_back"], 16)
                sp.wait_ge(*at("sums_back", L, 16 * (b + 1)))
                for c in range(b * CPB, (b + 1) * CPB):
                    t0 = (c % CPB) * CW
                    for m in range(CC):
                        h0 = b * H + m * (H // 2)
                        sp.dma_start(RT[:, c % 2, m, :],
                                     RD[h0:h0 + H // 2, None, t0:t0 + CW].to_broadcast([H // 2, HD, CW])
                                     ).then_inc(S[f"heads_out_{c % 2}"], 16)

            def step(it, e):
                if it is None and e == NH - 3:
                    for s in range(2):
                        sp.wait_ge(*at(f"stored_{s}", L, 16 * (H // 2)))
                    sums(0)
                    for c in range(CPB):
                        load_out(sp, L, c)
                if not last_of(it, e, 3):
                    stack(it, e + 3)
                if not last_of(it, e, 1):
                    head_v(it, e + 1)
                if it is not None or e:
                    store(it, e - 1)
                if not last_of(it, e, 1):
                    max_row(it, e + 1)
                if it is None and e == NH - 3:
                    sums_back(0)

            sp.wait_ge(*at("ones", L, 1))
            if L == "l1":
                for s in range(LDS):
                    sp.dma_start(KS[ROW_MASK:ROW_MASK + 1, s, :].bitcast(F32), ins["zeros"]
                                 ).then_inc(S["zero_rows"], 16)
            sp_parts(sp, L, range(NQK // B + 2))
            if L == "l1":
                sp.wait_ge(S["zero_rows"], 16 * LDS)
            else:
                sp.wait_ge(S["mask_dram"], 32)
            for s in range(4):
                sp.wait_ge(*at(f"pqk_{s}", L, 16 * (NQK // B // 4)))
            i = NQK // B + 2
            for e in range(3):
                stack(None, e)
                sp_parts(sp, L, range(i, i + 2))
                i += 2
            sp.wait_ge(*at("v", L, NC))
            head_v(None, 0)
            sp_parts(sp, L, range(i, NQK))
            for s in range(4):
                sp.wait_ge(*at(f"pqk_{s}", L, 16 * (NQK // 4)))
            sp.wait_ge(*at("v", L, 2 * NC))
            max_row(None, 0)
            if L == "l1":
                sp_loads_later(sp)
            heads_loop(sp, step)
            store(None, NH - 1)
            for s in range(2):
                sp.wait_ge(*at(f"stored_{s}", L, 16 * (NH // 2)))
            sums(1)
            for c in range(CPB, NC):
                sp.wait_ge(*at("out", XN[L], 2 * (c - 1)))
                load_out(sp, L, c)
            sums_back(1)

        XN = {"l1": "l1a", "l3": "l3a"}

        def load_out(sp, L, c):
            b, t0 = c // CPB, (c % CPB) * CW
            for m in range(CC):
                h0 = b * H + m * (H // 2)
                sp.dma_start(OTn[:, c % 2, m, :], OD[h0:h0 + H // 2, 0:HD, t0:t0 + CW]
                             ).then_inc(S[f"heads_out_{c % 2}"], 16)

        def dve_invert(dve, L, b):
            r = Rs[:, b, :]
            dve.wait_ge(*at("sums", L, 16 * (b + 1)))
            nc.vector.reciprocal(r, r).then_inc(S["sums_raw"], 1)
            dve.wait_ge(*at("sums_raw", L, b + 1))
            nc.vector.tensor_scalar(r, r, HEADS[L]["rsum"], None, ALU.mult).then_inc(S["sums_inv"], 1)

        def dve_heads_out(dve, L, b):
            for c in range(b * CPB, (b + 1) * CPB):
                dve.wait_ge(*at(f"heads_out_{c % 2}", L, 64 * (c // 2 + 1)))
                nc.vector.tensor_tensor(OTn[:, c % 2], OTn[:, c % 2], RT[:, c % 2], ALU.mult).then_inc(S["on"], 1)

        def pe_heads_out(pe, L, b):
            for c in range(b * CPB, (b + 1) * CPB):
                pe.wait_ge(*at("on", L, c + 1))
                project_tiles(pe, XN[L], c, 4,
                              lambda k, q: [OTn[:, c % 2, k, q * P:(q + 1) * P]],
                              [[HEADS[L]["w"][:, 3, k, :]] for k in range(CC)])

        def dve_l1_post(dve, b):
            def scale(c):
                dve.wait_ge(S["xh"], nth("l1_post", c))
                nc.vector.tensor_tensor(xh[:, c % 2], xh[:, c % 2],
                                        abrow[:, b, 0, None, :].to_broadcast([P, CT, D]),
                                        ALU.mult).then_inc(S["l1_scaled"], 1)

            def add(c):
                sl = X[:, CT * c:CT * c + CT, :]
                dve.wait_ge(S["l1_scaled"], c + 1)
                dve.wait_ge(S["l1_shifted"], c + 1)
                nc.vector.tensor_tensor(sl, sl, xh[:, c % 2], ALU.add).then_inc(S["x_l1"], 1)
                norm_stats(dve, "l2_attn", X, c)

            first, second = b * CPB, b * CPB + 1
            for c in (first, second):
                add_to_x(dve, "l1a", c, 4)
                norm_stats(dve, "l1_post", X, c)
            norm_apply(dve, "l1_post", X, first)
            scale(first)
            norm_apply(dve, "l1_post", X, second)
            add(first)
            scale(second)
            norm_apply(dve, "l2_attn", X, first)
            add(second)
            if b == 0:
                dve_invert(dve, "l1", 1)
            norm_apply(dve, "l2_attn", X, second)

        def pool_l1_post(pool, b):
            for c in range(b * CPB, (b + 1) * CPB):
                norm_rstd(pool, "l1_post", c)
            for c in range(b * CPB, (b + 1) * CPB):
                sl = X[:, CT * c:CT * c + CT, :]
                pool.wait_ge(S["xh"], nth("l1_post", c))
                nc.gpsimd.tensor_tensor(sl, sl, abrow[:, b, 1, None, :].to_broadcast([P, CT, D]),
                                        ALU.add).then_inc(S["l1_shifted"], 1)
                if c % CPB:
                    norm_low(pool, "l2_attn", c - 1)
                norm_rstd(pool, "l2_attn", c)
            for c in range(b * CPB, (b + 1) * CPB):
                if c % CPB:
                    norm_low(pool, "l2_attn", c)
                add_row(pool, "l2_attn", c, lambda b: rows[:, ROW["bp2"], :])

        def pe_l2(pe):
            pe.wait_ge(S["w_l2"], 16)
            pe.wait_ge(S["w_l2_low"], 3)
            for c in range(NC + 1):
                if c < NC and c not in (1, CPB):
                    norm_transpose(pe, "l2_attn", c)
                if c == 0:
                    continue
                d = c - 1
                if c == CPB:
                    pe.wait_ge(S["l2_qk"], 4)
                    pe_heads_out(pe, "l1", 1)
                h_ready(pe, "l2_attn", d)
                if d == 0:
                    pe.wait_ge(*at("out_used", "l1", NH))
                pe.wait_ge(*at("x", "l1a", 4 if d == 0 else 2 * NC))
                for j in range(2 * CC):
                    if d:
                        pe.wait_ge(S["l2_qk"], 4 * (d - 1) + j + 1)
                    for k in range(CC):
                        last = product(bank(4 + j), qkv_w("l2", j // 2, k, j % 2), h_chunk("l2_attn", k, d),
                                       k == 0, k == CC - 1)
                    last.then_inc(S["l2_qkp"], 1)
                if c in (1, CPB):
                    norm_transpose(pe, "l2_attn", c)
                for p in range(2):
                    if d:
                        pe.wait_ge(S["l2_v"], 2 * (d - 1) + p + 1)
                    for q in range(2):
                        for k in range(CC):
                            last = product(PS[:, 2 + p, q * D:(q + 1) * D],
                                           h_tile("l2_attn", k, CT * d + 2 * p + q), qkv_w("l2", 2, k),
                                           k == 0, k == CC - 1)
                    last.then_inc(S["l2_vp"], 1)
            pe.wait_ge(S["l2_qk"], 4 * NC)
            pe.wait_ge(S["l2_v"], 2 * NC)

            def scores(n):
                if n >= 2:
                    pe.wait_ge(S["l2_exp"], n - 1)
                b = n // TT
                for half in range(2):
                    for k in range(CC):
                        last = nc.tensor.matmul(bank(2 * (n % 2) + half), QT2[:, k, n * P:(n + 1) * P],
                                                KT2[:, k, b * T + half * CW:b * T + (half + 1) * CW],
                                                start=(k == 0), stop=(k == CC - 1))
                last.then_inc(S["l2_scores"], 1)

            def turn(n):
                pe.wait_ge(S["l2_exp"], n + 1)
                if n:
                    for half in range(2):
                        pe.wait_ge(S[f"l2_turn_used_{half}"], n)
                for k in range(TT):
                    last = nc.tensor.transpose(PS[:, 4 + k // 4, (k % 4) * P:(k % 4 + 1) * P],
                                               P2[:, n % 2, k * P:(k + 1) * P], ident[:, :])
                    if k % 4 == 3:
                        last.then_inc(S["l2_turned"], 1)

            def values(c):
                b = c // CPB
                for half in range(2):
                    pe.wait_ge(S[f"l2_turn_low_{half}"], CT * (c + 1))
                pe.wait_ge(S["l2_v_low"], CPB * (b + 1))
                if c:
                    pe.wait_ge(*at("x", "l2a", 2 * c))
                for m in range(CC):
                    if c or m:
                        pe.wait_ge(S["l2_oT"], 2 * c + m)
                    for k in range(TT):
                        high, low = (x[:, b * TT + k, m * P:(m + 1) * P] for x in (V2_high, V2_r))
                        last = product(bank(6), [high, low], [PT4_high[k // 4][:, k % 4, :], PT4_r[:, k, :]],
                                       k == 0, k == TT - 1)
                    last.then_inc(S["l2_op"], 1)

            def project(c):
                pe.wait_ge(S["l2_oT"], 2 * c + 2)
                for p in range(2):
                    if c:
                        pe.wait_ge(*at("x", "l2a", 2 * (c - 1) + p + 1))
                    for q in range(2):
                        for k in range(CC):
                            last = nc.tensor.matmul(PS[:, 7 - p, q * D:(q + 1) * D],
                                                    OTn[:, c % 2, k, (2 * p + q) * P:(2 * p + q + 1) * P],
                                                    wA[:, 3, k, :], start=(k == 0), stop=(k == CC - 1))
                    last.then_inc(S["out"], 1)

            scores(0)
            for n in range(NT):
                if n + 1 < NT:
                    scores(n + 1)
                turn(n)
                if n and n % CT == 0:
                    values(n // CT - 1)
                    project(n // CT - 1)
            values(NC - 1)
            project(NC - 1)

        def act_l2(act):
            def values_copy(c):
                for m in range(CC):
                    act.wait_ge(S["l2_op"], 2 * c + m + 1)
                    if c >= 2:
                        act.wait_ge(*at("out", "l2a", 2 * (c - 1)))
                    nc.scalar.copy(OTn[:, c % 2, m, :], bank(6)).then_inc(S["l2_oT"], 1)

            for c in range(NC + 1):
                if c < NC and c not in (1, CPB):
                    norm_modulate(act, "l2_attn", c)
                if c:
                    for j in range(2 * CC):
                        d = c - 1
                        act.wait_ge(S["l2_qkp"], 4 * d + j + 1)
                        dst = (QT2 if j < 2 else KT2)[:, j % 2, d * CW:(d + 1) * CW]
                        nc.scalar.activation(dst, bank(4 + j), ACT.Identity,
                                             bias=cols[:, COL_L2 + j:COL_L2 + j + 1]).then_inc(S["l2_qk"], 1)
                if c in (1, CPB):
                    norm_modulate(act, "l2_attn", c)
            for n in range(NT + 1):
                if n < NT:
                    act.wait_ge(S["l2_max"], n + 1)
                    if n >= 2:
                        act.wait_ge(S["l2_turned"], 2 * (n - 1))
                    nc.scalar.activation(P2[:, n % 2, :], bank2(2 * (n % 2)), ACT.Exp, scale=D ** -0.5,
                                         bias=nm2[:, n:n + 1], accum_out=sum2[:, n:n + 1]).then_inc(S["l2_exp"], 1)
                if n > 1 and (n - 1) % CT == 0:
                    values_copy((n - 1) // CT - 1)
                if n:
                    l2_turn_copy(act, n - 1, 1)
            values_copy(NC - 1)

        def l2_turn_copy(eng, n, half):
            q = n % CT
            eng.wait_ge(S["l2_turned"], 2 * n + half + 1)
            if n >= CT and q == 0:
                eng.wait_ge(S["l2_op"], 2 * (n // CT))
            src = PS[:, 4 + half, :].rearrange("p (k q) -> p k q", k=4)
            dst = PT4[:, 4 * half:4 * half + 4, q * P:(q + 1) * P]
            high = PT4_high[half][:, :, q * P:(q + 1) * P]
            if half:
                nc.scalar.copy(dst, src)
                nc.scalar.copy(high, src).then_inc(S["l2_turn_used_1"], 1)
            else:
                nc.vector.tensor_copy(dst, src)
                nc.vector.tensor_copy(high, src).then_inc(S["l2_turn_used_0"], 1)
                eng.wait_ge(S["l2_turn_used_0"], n + 1)
                nc.vector.tensor_tensor(PT4_r[:, 0:4, q * P:(q + 1) * P], dst, high.bitcast(F32),
                                        ALU.subtract).then_inc(S["l2_turn_low_0"], 1)

        def pool_l2(pool):
            for n in range(NT):
                q = n % CT
                pool.wait_ge(S["l2_turn_used_1"], n + 1)
                sl = (slice(None), slice(4, 8), slice(q * P, (q + 1) * P))
                nc.gpsimd.tensor_tensor(PT4_r[sl], PT4[sl], PT4_high[1][:, :, q * P:(q + 1) * P].bitcast(F32),
                                        ALU.subtract).then_inc(S["l2_turn_low_1"], 1)
                if n and q == 0:
                    norm_rstd(pool, "l2_mlp", n // CT - 1)

        def l2_values(dve, c):
            for p in range(2):
                g = 2 * c + p
                dve.wait_ge(S["l2_vp"], g + 1)
                nc.vector.tensor_tensor(V2[:, 2 * g:2 * g + 2, :], banks2t(2 + p),
                                        rows[:, ROW["bv2"], None, :].to_broadcast([P, 2, D]),
                                        ALU.add).then_inc(S["l2_v"], 1)

        def dve_l2(dve):
            for c in range(1, NC):
                l2_values(dve, c)

            def maximum(n):
                dve.wait_ge(S["l2_scores"], n + 1)
                nc.vector.tensor_reduce(nm2[:, n:n + 1], bank2(2 * (n % 2)), AX.X, ALU.max,
                                        negate=True).then_inc(S["l2_max_raw"], 1)
                dve.wait_ge(S["l2_max_raw"], n + 1)
                nc.vector.tensor_scalar(nm2[:, n:n + 1], nm2[:, n:n + 1], D ** -0.5, None,
                                        ALU.mult).then_inc(S["l2_max"], 1)

            def add(c):
                dve.wait_ge(S["l2_rinv"], CT * (c + 1))
                dve.wait_ge(*at("pre", "l2a", c + 1))
                for p in range(2):
                    dve.wait_ge(*at("out", "l2a", 2 * c + p + 1))
                    for q in range(2):
                        k = CT * c + 2 * p + q
                        last = nc.vector.scalar_tensor_tensor(X[:, k, :], PS[:, 7 - p, q * D:(q + 1) * D],
                                                              rinv2[:, k:k + 1], X[:, k, :], ALU.mult, ALU.add)
                    last.then_inc(S["x"], 1)
                norm_ahead(dve, "l2_mlp", X, c)

            maximum(0)
            for n in range(NT):
                if n + 1 < NT:
                    maximum(n + 1)
                dve.wait_ge(S["l2_exp"], n + 1)
                nc.vector.reciprocal(rinv2[:, n:n + 1], sum2[:, n:n + 1]).then_inc(S["l2_rinv"], 1)
                l2_turn_copy(dve, n, 0)
                if n < NC:
                    sl = slice(n * CT, (n + 1) * CT)
                    dve.wait_ge(S["l2_v"], 2 * NC)
                    dve.wait_ge(S["l2_vp"], 2 * NC)
                    nc.vector.tensor_copy(V2_high[:, sl], V2[:, sl]).then_inc(S["l2_v_high"], 1)
                    dve.wait_ge(S["l2_v_high"], n + 1)
                    nc.vector.tensor_tensor(V2_r[:, sl], V2[:, sl], V2_high[:, sl].bitcast(F32),
                                            ALU.subtract).then_inc(S["l2_v_low"], 1)
                if n and n % CT == 0:
                    add(n // CT - 1)
            add(NC - 1)

        def pe_mlp(pe, L, site):
            for c in range(NC + 2):
                late = L == "l3" and c == CPB
                if c < NC and not late:
                    norm_transpose(pe, site, c)
                if late:
                    pe.wait_ge(*at("gelu", L, FC))
                    pe_heads_out(pe, "l3", 1)
                if 1 <= c <= NC:
                    d = c - 1
                    h_ready(pe, site, d)
                    if d == 0:
                        pe.wait_ge(*at("mlp_w_high", L, 2 if L == "l2" else 4))
                    if L == "l2" and d == 0:
                        pe.wait_ge(*at("x", "l2a", 2 * NC))
                    if L == "l3":
                        if d == 0:
                            pe.wait_ge(*at("out_used", "l3", NH))
                        pe.wait_ge(*at("x", "l3a", 4 if d == 0 else 2 * NC))
                    for f in range(FC):
                        u = FC * d + f
                        if u >= 4:
                            pe.wait_ge(*at("gelu", L, u - 3))
                        for k in range(CC):
                            last = product(bank(4 + u % 4), [w[:, k, f * P:(f + 1) * P] for w in (wM1_high, wM1_r)],
                                           h_chunk(site, k, d), k == 0, k == CC - 1)
                        last.then_inc(S["hid"], 1)
                if late:
                    norm_transpose(pe, site, c)
                if c >= 2:
                    d = c - 2
                    pe.wait_ge(*at("gelu_low", L, FC * (d + 1)))
                    project_tiles(pe, MLP[L], d, 2,
                                  lambda k, q: [G_r[:, d % 2, l, k, q * P:(q + 1) * P] for l in range(2)],
                                  [[wM2_high[:, k, :], wM2_r[:, k, :]] for k in range(FC)])

        def act_mlp(act, L, site, col):
            for c in range(NC + 1):
                late = L == "l3" and c == CPB
                if c < NC and not late:
                    norm_modulate(act, site, c)
                if c:
                    d = c - 1
                    if d >= 2:
                        act.wait_ge(*at("out", MLP[L], 2 * (d - 1)))
                    for f in range(FC):
                        act.wait_ge(*at("hid", L, FC * d + f + 1))
                        for dst in (G[:, d % 2, 1, f, :], G_r[:, d % 2, 0, f, :]):
                            last = nc.scalar.activation(dst, bank(4 + (FC * d + f) % 4), ACT.Gelu,
                                                        bias=cols[:, col + f:col + f + 1])
                        last.then_inc(S["gelu"], 1)
                if late:
                    norm_modulate(act, site, c)

        def gelu_low(dve, L, c):
            for f in range(FC):
                dve.wait_ge(*at("gelu", L, FC * c + f + 1))
                nc.vector.tensor_tensor(G_r[:, c % 2, 1, f, :], G[:, c % 2, 1, f, :],
                                        G_r[:, c % 2, 0, f, :].bitcast(F32),
                                        ALU.subtract).then_inc(S["gelu_low"], 1)

        def dve_l2_mlp(dve):
            dve.wait_ge(S["l2_op"], 2 * NC)
            dve.wait_ge(S["w_m2"], 32)
            nc.vector.tensor_copy(wM2_high, wM2).then_inc(S["w_m2_high"], 1)
            dve.wait_ge(S["w_m2_high"], 1)
            nc.vector.tensor_tensor(wM2_r, wM2, wM2_high.bitcast(F32), ALU.subtract
                                    ).then_inc(at("mlp_w_high", "l2", 0)[0], 1)
            for c in range(NC + 2):
                norm_rest(dve, "l2_mlp", X, c + 1)
                if 1 <= c <= NC:
                    gelu_low(dve, "l2", c - 1)
                if c >= 2:
                    add_to_x(dve, "l2m", c - 2, 2)
                    norm_ahead(dve, "l3_attn", X, c - 2)

        def dve_l3_mlp(dve):
            for b in range(B):
                if b:
                    dve_invert(dve, "l3", b)
                dve_heads_out(dve, "l3", b)
                if b:
                    gelu_low(dve, "l3", 0)
                chunks = range(b * CPB, (b + 1) * CPB)
                for c in chunks:
                    add_to_x(dve, "l3a", c, 4)
                    norm_stats(dve, "l3_mlp", X, c)
                for c in chunks:
                    norm_apply(dve, "l3_mlp", X, c)
            for c in range(NC):
                if c + 1 < NC:
                    gelu_low(dve, "l3", c + 1)
                add_to_x(dve, "l3m", c, 2)

        block = ctx.enter_context(nc.Block())

        @block.sync
        def _(sp):
            sp_loads(sp)
            sp_heads(sp, "l1")
            sp.wait_ge(*at("x", "l1a", 2 * NC))
            sp.dma_start(wB[:, 0:6], ins["w_l3"].rearrange("w (k p) n -> p w k n", p=P)).then_inc(S["w_l3"], 16)
            sp.wait_ge(*at("x", "l2a", 2 * NC))
            sp.dma_start(rope, ins["rope"].rearrange("a p t -> p a t")).then_inc(S["rope"], 16)
            sp.wait_ge(*at("x", "l2m", 2 * NC))
            sp.dma_start(wM1, ins["w_m3a"].rearrange("(k p) n -> p k n", p=P)).then_inc(S["w_m3"], 16)
            sp.dma_start(wM2, ins["w_m3b"].rearrange("(k p) n -> p k n", p=P)).then_inc(S["w_m3"], 16)
            sp_heads(sp, "l3")
            for c in range(NC):
                sp.wait_ge(*at("x", "l3m", 2 * c + 2))
                sp.dma_start(out.rearrange("b (n p) d -> p (b n) d", p=P)[:, CT * c:CT * c + CT, :],
                             X[:, CT * c:CT * c + CT, :]).then_inc(S["stored"], 16)
            sp.wait_ge(S["stored"], 16 * NC)

        @block.scalar
        def _(act):
            act_loads(act)
            act.wait_ge(S["small"], 32)
            nc.scalar.activation(scond[:, :, :], condT[:, :, :], ACT.Silu).then_inc(S["scond"], 1)
            act_l0(act)
            act_qkv(act, "l1")
            act_heads(act, "l1")
            act_l2(act)
            act_mlp(act, "l2", "l2_mlp", COL_M2)
            act_qkv(act, "l3")
            act_heads(act, "l3")
            act_mlp(act, "l3", "l3_mlp", COL_M3)

        @block.vector
        def _(dve):
            dve_l0(dve)
            dve_qkv(dve, "l1")
            dve_heads(dve, "l1")
            dve_heads_out(dve, "l1", 0)
            dve_l1_post(dve, 0)
            dve_heads_out(dve, "l1", 1)
            l2_values(dve, 0)
            dve_l1_post(dve, 1)
            dve_l2(dve)
            dve_l2_mlp(dve)
            dve_qkv(dve, "l3")
            dve_heads(dve, "l3")
            dve_l3_mlp(dve)

        @block.gpsimd
        def _(pool):
            def row(name):
                return lambda b: rows[:, ROW[name], :]

            pool_l0(pool)
            pool_qkv(pool, "l1", row("bp1"))
            pool_heads(pool, "l1", (S["w_l2"], 16),
                       [(wA[:, w], w_high["l2"][:, w], wA_r[:, w], S["w_l2_low"]) for w in range(3)])
            for b in range(B):
                pool_l1_post(pool, b)
            pool_l2(pool)
            pool.wait_ge(S["w_m2"], 32)
            done, _ = at("mlp_w_high", "l2", 0)
            split_weights(pool, wM1, wM1_high, wM1_r, done)
            norm_rstd(pool, "l2_mlp", NC - 1)
            for c in range(NC):
                norm_low(pool, "l2_mlp", c)
                add_row(pool, "l2_mlp", c, row("b22"))
            pool.wait_ge(*at("x", "l2a", 2 * NC))
            pool.wait_ge(S["w_l3"], 16)
            split_weights(pool, wB[:, 0:2], qk_high, wB_r[:, 0:2], S["w_l3_low"])
            split_weights(pool, wB[:, 4:6], qks_high, wB_r[:, 4:6], S["w_l3_low"])

            def split_values():
                pool.wait_ge(*at("hid", "l2", FC * NC))
                split_weights(pool, wB[:, 2:3], v_high[:, 0:1], wB_r[:, 2:3], S["w_l3_low"])

            pool_qkv(pool, "l3", row("bo3"), split_values)
            half = FC // 2
            pool_heads(pool, "l3", (S["w_m3"], 32),
                       [(wM1[:, k], wM1_high[:, k], wM1_r[:, k], done) for k in range(CC)] +
                       [(wM2[:, k:k + half], wM2_high[:, k:k + half], wM2_r[:, k:k + half], done)
                        for k in (0, half)])
            for b in range(B):
                norms_of(pool, "l3_mlp", b, row("b23"))

        @block.tensor
        def _(pe):
            pe_l0(pe)
            pe_qkv(pe, "l1")
            pe_heads(pe, "l1")
            pe_l2(pe)
            pe_mlp(pe, "l2", "l2_mlp")
            pe_qkv(pe, "l3")
            pe_heads(pe, "l3")
            pe_mlp(pe, "l3", "l3_mlp")


def kernel(**inputs):
    import concourse.bacc as bacc
    from concourse.bass_utils import run_bass_kernel_spmd

    a = {k: np.asarray(x) for k, x in inputs.items()}

    def l(n, name):
        return a[f"L{n}_cond_{name}"]

    def pairs(w):
        return w.reshape(w.shape[:-1] + (D // 2, 2))[..., ::-1].reshape(w.shape)

    def halves(w):
        return np.concatenate([w[..., D:], w[..., :D]], axis=-1)

    def columns(x):
        return x.reshape(-1, P).T

    wqkv = l(1, "Wqkv").reshape(H, HD, 3, D).transpose(2, 3, 0, 1).reshape(3, D, D)
    bqkv = l(1, "bqkv").reshape(H, HD, 3).transpose(2, 0, 1).reshape(3, D)
    zero = np.zeros(D, np.float32)
    mod_b = [l(0, "emb_b"), l(1, "bg"), l(1, "bb"), halves(l(3, "ada1_b")), halves(l(3, "ada2_b")),
             l(2, "film1_b"), l(2, "film2_b")]
    gains = [l(0, "sn_g"), l(1, "ln_g"), l(3, "ln1_g"), l(3, "ln2_g"), l(2, "norm1_w"), l(2, "norm2_w")]
    offsets = [l(0, "sn_b"), l(1, "ln_b"), l(3, "ln1_b"), l(3, "ln2_b"), zero, zero]
    cols = columns(np.concatenate(
        mod_b + gains + offsets + [l(0, "norm_g"), l(0, "norm_b"), l(0, "bk"), bqkv[0], bqkv[1],
                                   l(2, "q_b"), l(2, "k_b"), l(3, "bq"), l(3, "bk"),
                                   pairs(l(3, "bq")), pairs(l(3, "bk")), l(2, "mlp_b1"), l(3, "ff_b1")]))
    rows = np.stack([l(0, "bq"), l(0, "bv"), l(0, "out_b"), a["cond_1024"][0], a["cond_1024"][1],
                     bqkv[2], l(1, "bp"), l(1, "bg"), l(1, "bb"), l(1, "ln_g"), l(1, "ln_b"),
                     l(2, "v_b"), l(2, "proj_b"), l(2, "mlp_b2"), l(3, "bv"), l(3, "bo"), l(3, "ff_b2")])
    cond_w = np.concatenate([l(0, "emb_W"), l(1, "Wg").T, l(1, "Wb").T, halves(l(3, "ada1_w")),
                             halves(l(3, "ada2_w")), l(2, "film1_w"), l(2, "film2_w")], axis=1)
    rot = HD // 2
    inv = (1.0 / np.float32(10000.0) ** (np.arange(rot, dtype=np.float32) / np.float32(rot))).astype(np.float32)
    freq = np.arange(T, dtype=np.float32)[None, :] * inv[:, None]
    chan = np.arange(P) % HD
    sign = np.where(chan % 2 == 0, -1.0, 1.0).astype(np.float32)
    tables = np.stack([np.cos(freq)[chan // 2], np.sin(freq)[chan // 2] * sign[:, None]])
    block = np.arange(P) // HD

    arrays = {
        "x": a["x"],
        "mask": a["mask_BxS_bf1"].view(np.uint8),
        "cols": cols,
        "rows": rows,
        "condT": a["cond_1024"].T.reshape(CC, P, B).transpose(1, 0, 2),
        "cond_w": cond_w,
        "w_l0": np.stack([l(0, "Wq"), l(0, "Wk"), l(0, "Wv"), l(0, "out_W")]),
        "w_l1": np.concatenate([wqkv, l(1, "Wp").T[None]]),
        "w_l2": np.stack([l(2, "q_w"), l(2, "k_w"), l(2, "v_w"), l(2, "proj_w")]),
        "w_l3": np.stack([l(3, "wq"), l(3, "wk"), l(3, "wv"), l(3, "wo"), pairs(l(3, "wq")), pairs(l(3, "wk"))]),
        "w_m2a": l(2, "mlp_w1"), "w_m2b": l(2, "mlp_w2"), "w_m3a": l(3, "ff_w1"), "w_m3b": l(3, "ff_w2"),
        "rope": tables.astype(np.float32),
        "ident": np.eye(P, dtype=np.float32),
        "zeros": np.zeros((1, T // 2), np.float32),
        "bdmask": (block[:, None] == block[None, :]).astype(np.float32),
    }
    arrays = {f"in_{k}": np.ascontiguousarray(x) for k, x in arrays.items()}
    nc = bacc.Bacc("TRN2", target_bir_lowering=False, num_devices=1)
    ins = {k[3:]: nc.dram_tensor(k, x.shape, mybir.dt.from_np(x.dtype), kind="ExternalInput").ap()
           for k, x in arrays.items()}
    out = nc.dram_tensor("out_0", (B, T, D), F32, kind="ExternalOutput").ap()
    build(nc, ins, out)
    r = run_bass_kernel_spmd(nc, [arrays], core_ids=[0])
    return r.results[0]["out_0"]
```
